# Optimizing a Trainium2 kernel written in Bass

```python
import numpy as np
import jax
import jax.numpy as jnp

def _softmax(x, axis=-1):
    return jax.nn.softmax(x, axis=axis)

def _gelu(x):
    return jax.nn.gelu(x, approximate=True)

def _silu(x):
    return jax.nn.silu(x)

def _sigmoid(x):
    return jax.nn.sigmoid(x)

def _layernorm(x, axis=-1, eps=1e-05):
    m = jnp.mean(x, axis=axis, keepdims=True)
    v = jnp.var(x, axis=axis, keepdims=True)
    return (x - m) / jnp.sqrt(v + eps)

def _scatter_add(tgt, idx, src, axis=0):
    return tgt.at[idx].add(src)

def _segment_sum(src, seg, n):
    return jax.ops.segment_sum(src, seg, n)
kernel_name = 'mk_seq_preln_d2_jaxref_r8_c6674a'

def setup_inputs(seed: int=0):
    np.random.seed(seed)
    _w = jnp.asarray

    def _L0_attn_setup():
        import jax, jax.numpy as jnp
        import numpy as np
        D = 128
        H = 16
        DH = D // H
        B, N = (4, 128)
        key = jax.random.key(seed)
        k0, k1, k2 = jax.random.split(key, 3)
        x = jax.random.normal(k0, (B, N, D), jnp.float32)
        Wkqv = jax.random.normal(k1, (H, D, 2 * D + DH), jnp.float32) * 0.02
        bkqv = jnp.zeros((H, 2 * D + DH), jnp.float32)
        Wp = jax.random.normal(k2, (D, D), jnp.float32) * 0.02
        bp = jnp.zeros((D,), jnp.float32)
        return {'x': x, 'Wkqv': Wkqv, 'bkqv': bkqv, 'Wp': Wp, 'bp': bp}
    _L0_attn_in = _L0_attn_setup()

    def _L0_ffn_setup():
        import jax, jax.numpy as jnp
        import numpy as np
        HIDDEN = 128
        INTER = 64
        N_EXPERTS = 16
        N_GROUP = 4
        TOPK_GROUP = 2
        TOP_K = 4
        SCALING = 2.5

        def _gate(x_flat, gate_w, e_bias):
            logits = x_flat @ gate_w.T
            scores = jax.nn.sigmoid(logits)
            scores_for_choice = scores + e_bias[None, :]
            T = x_flat.shape[0]
            per_group = N_EXPERTS // N_GROUP
            grouped = scores_for_choice.reshape(T, N_GROUP, per_group)
            top2, _ = jax.lax.top_k(grouped, 2)
            group_scores = top2.sum(-1)
            _, group_idx = jax.lax.top_k(group_scores, TOPK_GROUP)
            group_mask = jax.nn.one_hot(group_idx, N_GROUP, dtype=jnp.float32).sum(1) > 0
            score_mask = jnp.repeat(group_mask, per_group, axis=-1)
            tmp_scores = jnp.where(score_mask, scores_for_choice, 0.0)
            _, topk_idx = jax.lax.top_k(tmp_scores, TOP_K)
            topk_weight = jnp.take_along_axis(scores, topk_idx, axis=1)
            topk_weight = topk_weight / (topk_weight.sum(-1, keepdims=True) + 1e-20)
            topk_weight = topk_weight * SCALING
            return (topk_idx, topk_weight)
        key = jax.random.key(seed)
        ks = jax.random.split(key, 8)
        B, S = (2, 256)
        hidden_states = jax.random.normal(ks[0], (B, S, HIDDEN), dtype=jnp.float32)
        gate_w = jax.random.normal(ks[1], (N_EXPERTS, HIDDEN), dtype=jnp.float32) * 0.02
        e_bias = jnp.zeros((N_EXPERTS,), dtype=jnp.float32)
        gate_proj = jax.random.normal(ks[2], (N_EXPERTS, INTER, HIDDEN), dtype=jnp.float32) * 0.02
        up_proj = jax.random.normal(ks[3], (N_EXPERTS, INTER, HIDDEN), dtype=jnp.float32) * 0.02
        down_proj = jax.random.normal(ks[4], (N_EXPERTS, HIDDEN, INTER), dtype=jnp.float32) * 0.02
        shared_gate_w = jax.random.normal(ks[5], (INTER, HIDDEN), dtype=jnp.float32) * 0.02
        shared_up_w = jax.random.normal(ks[6], (INTER, HIDDEN), dtype=jnp.float32) * 0.02
        shared_down_w = jax.random.normal(ks[7], (HIDDEN, INTER), dtype=jnp.float32) * 0.02
        return {'hidden_states': hidden_states, 'gate_w': gate_w, 'e_bias': e_bias, 'gate_proj': gate_proj, 'up_proj': up_proj, 'down_proj': down_proj, 'shared_gate_w': shared_gate_w, 'shared_up_w': shared_up_w, 'shared_down_w': shared_down_w}
    _L0_ffn_in = _L0_ffn_setup()

    def _L1_attn_setup():
        import jax, jax.numpy as jnp
        import numpy as np
        D_MODEL = 128
        NUM_HEADS = 16
        HEAD_DIM = D_MODEL // NUM_HEADS
        CURVATURE = 1.0

        def _hyperbolic_distance(q, k, c):
            q_norm_sq = jnp.sum(q * q, axis=-1, keepdims=True)
            k_norm_sq = jnp.sum(k * k, axis=-1)[..., None, :]
            qk = jnp.einsum('bhnd,bhmd->bhnm', q, k)
            diff_sq = q_norm_sq + k_norm_sq - 2.0 * qk
            denom = (1.0 - c * q_norm_sq) * (1.0 - c * k_norm_sq)
            denom = jnp.maximum(denom, 1e-06)
            cosh_arg = 1.0 + 2.0 * c * diff_sq / denom
            cosh_arg = jnp.maximum(cosh_arg, 1.0)
            return jnp.arccosh(cosh_arg)
        key = jax.random.key(seed)
        kx, kq, kk, kv, ko = jax.random.split(key, 5)
        B, N = (2, 256)
        s = 1.0 / np.sqrt(D_MODEL)
        return {'x': jax.random.normal(kx, (B, N, D_MODEL), dtype=jnp.float32), 'wq': jax.random.normal(kq, (D_MODEL, D_MODEL), dtype=jnp.float32) * s, 'wk': jax.random.normal(kk, (D_MODEL, D_MODEL), dtype=jnp.float32) * s, 'wv': jax.random.normal(kv, (D_MODEL, D_MODEL), dtype=jnp.float32) * s, 'wo': jax.random.normal(ko, (D_MODEL, D_MODEL), dtype=jnp.float32) * s}
    _L1_attn_in = _L1_attn_setup()

    def _L1_ffn_setup():
        import jax, jax.numpy as jnp
        import numpy as np
        B, S, D = (4, 256, 128)
        N_EXPERTS, EXPERT_SIZE = (16, 32)
        WIDTH = N_EXPERTS * EXPERT_SIZE
        key = jax.random.key(seed)
        k_x, k_w1, k_w2, k_g = jax.random.split(key, 4)
        x = jax.random.normal(k_x, (B, S, D), dtype=jnp.float32)
        w1 = jax.random.normal(k_w1, (D, WIDTH), dtype=jnp.float32) / np.sqrt(D).astype(np.float32)
        b1 = jnp.zeros((WIDTH,), dtype=jnp.float32)
        w2 = jax.random.normal(k_w2, (WIDTH, D), dtype=jnp.float32) / np.sqrt(WIDTH).astype(np.float32)
        b2 = jnp.zeros((D,), dtype=jnp.float32)
        return {'x': x, 'w1': w1, 'b1': b1, 'w2': w2, 'b2': b2}
    _L1_ffn_in = _L1_ffn_setup()
    _d = {'L0_attn_x': _L0_attn_in['x'], 'L0_attn_Wkqv': _L0_attn_in['Wkqv'], 'L0_attn_bkqv': _L0_attn_in['bkqv'], 'L0_attn_Wp': _L0_attn_in['Wp'], 'L0_attn_bp': _L0_attn_in['bp'], 'L0_ffn_gate_w': _L0_ffn_in['gate_w'], 'L0_ffn_e_bias': _L0_ffn_in['e_bias'], 'L0_ffn_gate_proj': _L0_ffn_in['gate_proj'], 'L0_ffn_up_proj': _L0_ffn_in['up_proj'], 'L0_ffn_down_proj': _L0_ffn_in['down_proj'], 'L0_ffn_shared_gate_w': _L0_ffn_in['shared_gate_w'], 'L0_ffn_shared_up_w': _L0_ffn_in['shared_up_w'], 'L0_ffn_shared_down_w': _L0_ffn_in['shared_down_w'], 'L1_attn_wq': _L1_attn_in['wq'], 'L1_attn_wk': _L1_attn_in['wk'], 'L1_attn_wv': _L1_attn_in['wv'], 'L1_attn_wo': _L1_attn_in['wo'], 'L1_ffn_w1': _L1_ffn_in['w1'], 'L1_ffn_b1': _L1_ffn_in['b1'], 'L1_ffn_w2': _L1_ffn_in['w2'], 'L1_ffn_b2': _L1_ffn_in['b2']}
    _x0 = _d['L0_attn_x']
    _d['L0_attn_x'] = jax.random.normal(jax.random.fold_in(jax.random.key(seed), 1), (32, 256, 128), dtype=_x0.dtype)
    del _x0
    return _d

def reference(L0_attn_x, L0_attn_Wkqv, L0_attn_bkqv, L0_attn_Wp, L0_attn_bp, L0_ffn_gate_w, L0_ffn_e_bias, L0_ffn_gate_proj, L0_ffn_up_proj, L0_ffn_down_proj, L0_ffn_shared_gate_w, L0_ffn_shared_up_w, L0_ffn_shared_down_w, L1_attn_wq, L1_attn_wk, L1_attn_wv, L1_attn_wo, L1_ffn_w1, L1_ffn_b1, L1_ffn_w2, L1_ffn_b2):

    def _L0_attn_ref(x, Wkqv, bkqv, Wp, bp):
        import jax, jax.numpy as jnp
        import numpy as np
        D = 128
        H = 16
        DH = D // H
        B, N = (4, 128)
        Bm, Nm, Dm = x.shape
        y = jnp.einsum('bnd,hde->bhne', x, Wkqv) + bkqv[None, :, None, :]
        k = y[..., :Dm]
        q = y[..., Dm:2 * Dm]
        v = y[..., 2 * Dm:]
        A = jnp.einsum('bhnd,bhmd->bhnm', q, k) / jnp.sqrt(jnp.float32(Dm))
        mask = jnp.tril(jnp.ones((Nm, Nm), dtype=bool))
        A = jnp.where(mask[None, None], A, -jnp.inf)
        A = jax.nn.softmax(A, axis=-1)
        sa = jnp.einsum('bhnm,bhmd->bnhd', A, v).reshape(Bm, Nm, Dm)
        return sa @ Wp + bp

    def _L0_ffn_ref(hidden_states, gate_w, e_bias, gate_proj, up_proj, down_proj, shared_gate_w, shared_up_w, shared_down_w):
        import jax, jax.numpy as jnp
        import numpy as np
        HIDDEN = 128
        INTER = 64
        N_EXPERTS = 16
        N_GROUP = 4
        TOPK_GROUP = 2
        TOP_K = 4
        SCALING = 2.5

        def _gate(x_flat, gate_w, e_bias):
            logits = x_flat @ gate_w.T
            scores = jax.nn.sigmoid(logits)
            scores_for_choice = scores + e_bias[None, :]
            T = x_flat.shape[0]
            per_group = N_EXPERTS // N_GROUP
            grouped = scores_for_choice.reshape(T, N_GROUP, per_group)
            top2, _ = jax.lax.top_k(grouped, 2)
            group_scores = top2.sum(-1)
            _, group_idx = jax.lax.top_k(group_scores, TOPK_GROUP)
            group_mask = jax.nn.one_hot(group_idx, N_GROUP, dtype=jnp.float32).sum(1) > 0
            score_mask = jnp.repeat(group_mask, per_group, axis=-1)
            tmp_scores = jnp.where(score_mask, scores_for_choice, 0.0)
            _, topk_idx = jax.lax.top_k(tmp_scores, TOP_K)
            topk_weight = jnp.take_along_axis(scores, topk_idx, axis=1)
            topk_weight = topk_weight / (topk_weight.sum(-1, keepdims=True) + 1e-20)
            topk_weight = topk_weight * SCALING
            return (topk_idx, topk_weight)
        B, S, H = hidden_states.shape
        x = hidden_states.reshape(-1, H)
        T = x.shape[0]
        topk_idx, topk_weight = _gate(x, gate_w, e_bias)
        g = jnp.einsum('th,eih->eti', x, gate_proj)
        u = jnp.einsum('th,eih->eti', x, up_proj)
        inter = jax.nn.silu(g) * u
        expert_out = jnp.einsum('eti,ehi->eth', inter, down_proj)
        sel = expert_out[topk_idx, jnp.arange(T)[:, None]]
        y = jnp.einsum('tkh,tk->th', sel, topk_weight)
        y = y.reshape(B, S, H)
        sg = hidden_states @ shared_gate_w.T
        su = hidden_states @ shared_up_w.T
        shared_out = jax.nn.silu(sg) * su @ shared_down_w.T
        return y + shared_out

    def _L1_attn_ref(x, wq, wk, wv, wo):
        import jax, jax.numpy as jnp
        import numpy as np
        D_MODEL = 128
        NUM_HEADS = 16
        HEAD_DIM = D_MODEL // NUM_HEADS
        CURVATURE = 1.0

        def _hyperbolic_distance(q, k, c):
            q_norm_sq = jnp.sum(q * q, axis=-1, keepdims=True)
            k_norm_sq = jnp.sum(k * k, axis=-1)[..., None, :]
            qk = jnp.einsum('bhnd,bhmd->bhnm', q, k)
            diff_sq = q_norm_sq + k_norm_sq - 2.0 * qk
            denom = (1.0 - c * q_norm_sq) * (1.0 - c * k_norm_sq)
            denom = jnp.maximum(denom, 1e-06)
            cosh_arg = 1.0 + 2.0 * c * diff_sq / denom
            cosh_arg = jnp.maximum(cosh_arg, 1.0)
            return jnp.arccosh(cosh_arg)
        B, N, D = x.shape
        H, Dh = (NUM_HEADS, HEAD_DIM)
        q = (x @ wq.T).reshape(B, N, H, Dh).transpose(0, 2, 1, 3)
        k = (x @ wk.T).reshape(B, N, H, Dh).transpose(0, 2, 1, 3)
        v = (x @ wv.T).reshape(B, N, H, Dh).transpose(0, 2, 1, 3)
        dist = _hyperbolic_distance(q, k, CURVATURE)
        attn = jax.nn.softmax(-dist, axis=-1)
        out = jnp.einsum('bhnm,bhmd->bhnd', attn, v)
        out = out.transpose(0, 2, 1, 3).reshape(B, N, D)
        return out @ wo.T

    def _L1_ffn_ref(x, w1, b1, w2, b2):
        import jax, jax.numpy as jnp
        import numpy as np
        B, S, D = (4, 256, 128)
        N_EXPERTS, EXPERT_SIZE = (16, 32)
        WIDTH = N_EXPERTS * EXPERT_SIZE
        h = jax.nn.relu(jnp.einsum('bsd,dw->bsw', x, w1) + b1)
        return jnp.einsum('bsw,wd->bsd', h, w2) + b2
    x = L0_attn_x
    x = x + _L0_attn_ref(_layernorm(x, axis=-1), L0_attn_Wkqv, L0_attn_bkqv, L0_attn_Wp, L0_attn_bp)
    x = x + _L0_ffn_ref(_layernorm(x, axis=-1), L0_ffn_gate_w, L0_ffn_e_bias, L0_ffn_gate_proj, L0_ffn_up_proj, L0_ffn_down_proj, L0_ffn_shared_gate_w, L0_ffn_shared_up_w, L0_ffn_shared_down_w)
    x = x + _L1_attn_ref(_layernorm(x, axis=-1), L1_attn_wq, L1_attn_wk, L1_attn_wv, L1_attn_wo)
    x = x + _L1_ffn_ref(_layernorm(x, axis=-1), L1_ffn_w1, L1_ffn_b1, L1_ffn_w2, L1_ffn_b2)
    return x

_drawn_inputs = setup_inputs


def setup_inputs(seed=0):
    import zlib

    import numpy as np

    out = dict(_drawn_inputs(seed))
    spreads = {'L0_attn_bkqv': (0.0, 0.1),
     'L0_attn_bp': (0.0, 0.1),
     'L0_ffn_e_bias': (0.0, 0.8),
     'L1_ffn_b1': (0.0, 0.512),
     'L1_ffn_b2': (0.0, 0.324)}
    factors = {'L0_attn_Wkqv': 4.913,
     'L0_ffn_gate_w': 8.0,
     'L0_ffn_gate_proj': 7.172,
     'L0_ffn_up_proj': 7.45,
     'L0_ffn_down_proj': 7.668,
     'L0_ffn_shared_gate_w': 8.0,
     'L0_ffn_shared_up_w': 8.0,
     'L0_ffn_shared_down_w': 8.0,
     'L1_attn_wq': 6.956,
     'L1_attn_wk': 6.889}
    for name, (base, spread) in spreads.items():
        noise = np.random.default_rng([zlib.crc32(name.encode()), seed]).standard_normal(out[name].shape)
        drawn = base * np.exp(spread * noise) if base else spread * noise
        out[name] = jnp.asarray(drawn.astype(out[name].dtype))
    for name, factor in factors.items():
        out[name] = (out[name] * factor).astype(out[name].dtype)
    return out
```

```python
from contextlib import ExitStack

import concourse.bass as bass
from concourse import mybir

ALU = mybir.AluOpType
ACT = mybir.ActivationFunctionType
F32 = mybir.dt.float32
BF16 = mybir.dt.bfloat16
AX_X = mybir.AxisListType.X

P = 128
H = 16
DH = P // H
N = 256
TB = N // P
VW = DH + 1
LN_EPS = 1e-5

E = 16
INTER = 64
NG = 4
EG = E // NG
TOP_K = 4
TOPK_GROUP = 2
SCALING = 2.5
PAIRS = E // 2
BLOCKS = PAIRS + 1
CHUNK = 512
TC = CHUNK // P
WIDTH = 512
WB = WIDTH // P

PARTS = 3
PAIRINGS = ((0, 0), (0, 1), (0, 2), (1, 0), (1, 1), (2, 0))
QD = DH + 2
BIG = 1e15
TINY = 1e-15
DEN_MIN = 1e-6

C_IDENT, C_MASK, C_SEL, C_WIDTH = 0, P, 2 * P, 2 * P + PAIRS * P
R_BV, R_BP, R_EB, R_B2, R_WIDTH = 0, P, 2 * P, 2 * P + E, 3 * P + E


def after(engine, semaphore, count):
    if isinstance(count, int) and count <= 0:
        return
    engine.wait_ge(semaphore, count)


class Names:

    def __init__(self, nc, stack):
        self.nc, self.stack = nc, stack

    def sb(self, name, shape, dt=F32):
        return self.stack.enter_context(self.nc.sbuf_tensor(name, shape, dt))

    def ps(self, name, shape, dt=F32):
        return self.stack.enter_context(self.nc.psum_tensor(name, shape, dt))

    def sem(self, name):
        return self.stack.enter_context(self.nc.semaphore(name))


def load_and_fold(nc, io, keep, tiles):
    with ExitStack() as stack:
        m = Names(nc, stack)
        consts = m.sb("consts_sb", [P, C_WIDTH])
        wkqv = m.sb("wkqv", [P, H, 2 * P + DH])
        bq_rows = m.sb("bq_rows", [H, P])
        b1_rows = m.sb("b1_rows", [WB, P])
        bias_row = m.sb("bias_row", [1, R_WIDTH])
        ones_row = m.sb("ones_row", [1, P])
        gate_rows = m.sb("gate_rows", [P, BLOCKS, P])
        up_rows = m.sb("up_rows", [P, BLOCKS, P])
        down_cols = m.sb("down_cols", [P, E + 1, INTER])
        router_rows = m.sb("router_rows", [E, P])
        qkvo_rows = m.sb("qkvo_rows", [P, 4, P])
        wqT = m.sb("wqT", [P, H, P])
        wkT = m.sb("wkT", [P, H, P])
        bqT = m.sb("bqT", [P, H])
        bank = [m.ps(f"prep{i}", [P, 512]) for i in range(4)]

        consts_in, weights_in = m.sem("consts_in"), m.sem("weights_in")
        x_in = [m.sem(f"x_in{t}") for t in range(0, tiles, 4 * TB)]
        ones_set = m.sem("ones_set")
        bank_full = [m.sem(f"bank_full{i}") for i in range(4)]
        bank_read = [m.sem(f"bank_read{i}") for i in range(4)]

        jobs = []

        def transposes(sources, dst, parts=P):
            items = [(slice(P * i, P * i + s.shape[0]), s, None) for i, s in enumerate(sources)]
            jobs.append((parts, P * len(sources) if sources[0].shape[0] == P else sources[0].shape[0], items, dst))

        for h0 in range(0, H, 4):
            transposes([wkqv[:, h, P:2 * P] for h in range(h0, h0 + 4)], wqT[:, h0:h0 + 4, :])
            transposes([wkqv[:, h, 0:P] for h in range(h0, h0 + 4)], wkT[:, h0:h0 + 4, :])
        transposes([bq_rows[:, :]], bqT[:, :])
        transposes([b1_rows[:, :]], keep.b1T[:, :])
        for rows, dst in ((gate_rows, keep.gateT), (up_rows, keep.upT)):
            for j0 in (0, 4):
                transposes([rows[:, j, :] for j in range(j0, j0 + 4)], dst[:, j0:j0 + 4, :])
            transposes([rows[0:INTER, PAIRS, :]], dst[:, PAIRS, 0:INTER])
        down = down_cols[:, 0:E, :].rearrange("p (j e) i -> p j (e i)", e=2)
        for j0 in (0, 4):
            transposes([down[:, j, :] for j in range(j0, j0 + 4)], keep.downT[:, j0:j0 + 4, :])
        transposes([down_cols[:, E, :]], keep.downT[0:INTER, PAIRS, :], parts=INTER)
        transposes([router_rows[:, :]], keep.routerT[:, :])
        transposes([qkvo_rows[:, i, :] for i in range(4)], keep.qkvoT[:, :, :])
        for h0 in range(0, H, 4):
            jobs.append((P, 512, [(slice(P * i, P * i + P), wqT[:, h0 + i, :], wkT[:, h0 + i, :])
                                  for i in range(4)], keep.fold[:, h0:h0 + 4, :]))
        jobs.append((P, H, [(slice(h, h + 1), wkT[:, h, :], bqT[:, h:h + 1]) for h in range(H)],
                     keep.fold_bias[:, :]))
        jobs.append((P, R_WIDTH, [(slice(0, R_WIDTH), ones_row[:, :], bias_row[:, :])], keep.biases[:, :]))
        scaled = {id(jobs[i]) for i in range(len(jobs) - 2 - H // 4, len(jobs) - 1)}
        count_at = [[sum(1 for q in range(n + 1) if q % 4 == i) for n in range(len(jobs))] for i in range(4)]
        folds_from = len(jobs) - 2 - H // 4

        with nc.Block() as block:
            @block.sync
            def _(sp):
                sp.dma_start(keep.ident, io["consts"][:, C_IDENT:C_IDENT + P]).then_inc(consts_in, 16)
                sp.dma_start(consts[:, :], io["consts"]).then_inc(consts_in, 16)
                w = io["L0_attn_Wkqv"].rearrange("h d e -> d h e")
                for h0 in range(0, H, 4):
                    sp.dma_start(wkqv[:, h0:h0 + 4, :], w[:, h0:h0 + 4, :]).then_inc(weights_in, 16)
                row = lambda name: io[name].rearrange("(a n) -> a n", a=1)
                loads = [
                    (bq_rows[:, :], io["L0_attn_bkqv"][:, P:2 * P]),
                    (bias_row[:, R_BV:R_BV + P].rearrange("a (h e) -> a h e", h=H),
                     io["L0_attn_bkqv"][:, 2 * P:2 * P + DH].rearrange("(a h) e -> a h e", a=1)),
                    (bias_row[:, R_BP:R_BP + P], row("L0_attn_bp")),
                    (bias_row[:, R_EB:R_EB + E], row("L0_ffn_e_bias")),
                    (bias_row[:, R_B2:R_B2 + P], row("L1_ffn_b2")),
                    (b1_rows[:, :], io["L1_ffn_b1"].rearrange("(w p) -> w p", p=P)),
                    (gate_rows[:, 0:PAIRS, :], 
                     io["L0_ffn_gate_proj"].rearrange("e i d -> (e i) d").rearrange("(j p) d -> p j d", p=P)),
                    (up_rows[:, 0:PAIRS, :],
                     io["L0_ffn_up_proj"].rearrange("e i d -> (e i) d").rearrange("(j p) d -> p j d", p=P)),
                    (gate_rows[0:INTER, PAIRS, :], io["L0_ffn_shared_gate_w"]),
                    (up_rows[0:INTER, PAIRS, :], io["L0_ffn_shared_up_w"]),
                    (down_cols[:, 0:E, :], io["L0_ffn_down_proj"].rearrange("e d i -> d e i")),
                    (down_cols[:, E, :], io["L0_ffn_shared_down_w"]),
                    (router_rows[:, :], io["L0_ffn_gate_w"]),
                    (qkvo_rows[:, 0, :], io["L1_attn_wq"]),
                    (qkvo_rows[:, 1, :], io["L1_attn_wk"]),
                    (qkvo_rows[:, 2, :], io["L1_attn_wv"]),
                    (qkvo_rows[:, 3, :], io["L1_attn_wo"]),
                    (keep.wv0[:, :, :], w[:, :, 2 * P:2 * P + DH]),
                    (keep.wp[:, :], io["L0_attn_Wp"]),
                ]
                for dst, src in loads:
                    sp.dma_start(dst, src).then_inc(weights_in, 16)
                sp.wait_ge(weights_in, 16 * (len(loads) + H // 4))

            @block.gpsimd
            def _(pool):
                nc.gpsimd.memset(ones_row[:, :], 1.0).then_inc(ones_set, 1)
                nc.gpsimd.memset(keep.v0[:, :, :, :, DH:VW], 1.0).then_inc(ones_set, 1)
                nc.gpsimd.memset(keep.gateT[:, PAIRS, INTER:P], 0.0).then_inc(ones_set, 1)
                nc.gpsimd.memset(keep.upT[:, PAIRS, INTER:P], 0.0).then_inc(ones_set, 1)
                nc.gpsimd.memset(keep.downT[:, PAIRS, :], 0.0).then_inc(ones_set, 1)

            @block.tensor
            def _(pe):
                pe.wait_ge(consts_in, 32)
                pe.wait_ge(weights_in, 16 * (H // 4 + 19))
                pe.wait_ge(ones_set, 5)
                for n, (parts, cols, items, dst) in enumerate(jobs):
                    i = n % 4
                    if n == folds_from:
                        for q in range(4):
                            pe.wait_ge(bank_read[q], count_at[q][n - 1])
                    after(pe, bank_read[i], count_at[i][n] - 1)
                    for c, lhsT, rhs in items:
                        if rhs is None:
                            rows = lhsT.shape[0]
                            last = nc.tensor.transpose(bank[i][0:parts, c], lhsT, keep.ident[0:rows, 0:rows])
                        else:
                            last = nc.tensor.matmul(bank[i][0:parts, c], lhsT, rhs, start=True, stop=True)
                    last.then_inc(bank_full[i], 1)

            @block.vector
            def _(dve):
                dve.wait_ge(consts_in, 32)
                nc.vector.tensor_copy(keep.ident_bf[:, :], keep.ident)
                nc.vector.tensor_copy(keep.mask_bf[:, :], consts[:, C_MASK:C_MASK + P])
                nc.vector.tensor_copy(keep.sel_bf[:, :], consts[0:PARTS * E, C_SEL:C_WIDTH])
                for n, (parts, cols, items, dst) in enumerate(jobs):
                    i = n % 4
                    dve.wait_ge(bank_full[i], count_at[i][n])
                    src = bank[i][0:parts, 0:cols]
                    if len(dst.shape) == 3:
                        src = src.rearrange("p (a b) -> p a b", a=dst.shape[1])
                    if folds_from <= n < len(jobs) - 1:
                        ins = nc.vector.tensor_scalar(dst, src, float(P) ** -0.5, None, ALU.mult)
                    else:
                        ins = nc.vector.tensor_copy(dst, src)
                    ins.then_inc(bank_read[i], 1)
                for t in range(tiles):
                    if t % (4 * TB) == 0:
                        dve.wait_ge(x_in[t // (4 * TB)], 16)
                    nc.vector.bn_stats(keep.stats[:, t, :], keep.x[:, t, :])

            @block.scalar
            def _(act):
                x = io["L0_attn_x"].rearrange("b (j p) d -> p (b j) d", p=P)
                for t in range(0, tiles, 4 * TB):
                    act.dma_start(keep.x[:, t:t + 4 * TB, :], x[:, t:t + 4 * TB, :]).then_inc(x_in[t // (4 * TB)], 16)


def rstd_of_all(nc, keep, tiles, name):
    with ExitStack() as stack:
        m = Names(nc, stack)
        std, eps = m.sb(f"std_{name}", [P, tiles]), m.sb(f"eps_{name}", [P, 1])
        eps_set, var_done, std_done = m.sem(f"eps_set_{name}"), m.sem(f"var_done_{name}"), m.sem(f"std_done_{name}")
        with nc.Block() as block:
            @block.scalar
            def _(act):
                act.wait_ge(eps_set, 1)
                act.wait_ge(var_done, tiles)
                nc.scalar.activation(std[:, :], keep.mv[:, :, 1], ACT.Sqrt, bias=eps[:, 0:1]).then_inc(std_done, 1)

            @block.vector
            def _(dve):
                nc.vector.memset(eps[:, :], LN_EPS).then_inc(eps_set, 1)
                for t in range(tiles):
                    nc.vector.bn_aggr(keep.mv[:, t, :], keep.stats[:, t, :]).then_inc(var_done, 1)
                dve.wait_ge(std_done, 1)
                nc.vector.reciprocal(keep.rstd[:, :], std[:, :])


def causal_attention(nc, keep, batches):
    with ExitStack() as stack:
        m = Names(nc, stack)
        xh = m.sb("xh0", [P, TB, P])
        xT = m.sb("xT0", [P, 2, N])
        xTs = m.sb("xTs0", [P, N])
        gT = m.sb("gT", [P, 2, N])
        prob = m.sb("prob", [P, 2, 3 * P])
        probT = m.sb("probT", [P, 2, 3 * P])
        nmax = m.sb("nmax", [P, 2, TB])
        rec = m.sb("rec0", [P, TB, H])
        attn = m.sb("attn0", [P, TB, P])
        attnT = m.sb("attnT0", [P, N])
        g_ps = [m.ps(f"g_ps{i}", [P, 512]) for i in range(2)]
        s_ps = [m.ps(f"s_ps{i}", [P, 512]) for i in range(2)]
        t_ps = [m.ps(f"t_ps{i}", [P, 512]) for i in range(2)]
        o_ps = m.ps("o_ps0", [P, 512])
        misc = m.ps("misc0", [P, 512])
        o_view = o_ps[:, 0:TB * H * VW].rearrange("p (j h e) -> p j h e", j=TB, h=H)

        g_ready, g_copied = m.sem("g_ready"), m.sem("g_copied")
        s_ready, max_done, exp_done = m.sem("s_ready"), m.sem("max_done"), m.sem("exp_done")
        pT_ready, pT_copied, pv_done = m.sem("pT_ready"), m.sem("pT_copied"), m.sem("pv_done")
        xh_done, xh_turned, xTs_done, xT_done = m.sem("xh_done"), m.sem("xh_turned"), m.sem("xTs_done"), m.sem("xT_done")
        v_ready, v_done = m.sem("v_ready"), m.sem("v_done")
        bp_added, rec_done, attn_done = m.sem("bp_added"), m.sem("rec_done"), m.sem("attn_done")
        attn_turned, attnT_done, proj_ready = m.sem("attn_turned"), m.sem("attnT_done"), m.sem("proj_ready")
        res_done = m.sem("res_done")


        def pe_prep_turn(pe, b):
            after(pe, xh_done, (b + 1) * TB)
            after(pe, res_done, (b - 1) * TB)
            after(pe, v_done, b)
            for j in range(TB):
                last = nc.tensor.transpose(misc[:, j * P:(j + 1) * P], xh[:, j, :], keep.ident)
            last.then_inc(xh_turned, 1)

        def pe_prep_values(pe, b):
            pe.wait_ge(xTs_done, b + 1)
            for j in range(TB):
                last = nc.tensor.matmul(misc[:, N + j * P:N + (j + 1) * P], xTs[:, j * P:(j + 1) * P],
                                        keep.wv0[:, :, :], start=True, stop=True)
            last.then_inc(v_ready, 1)

        def act_prep(act, b):
            act.wait_ge(xh_turned, b + 1)
            after(act, v_ready, b)
            after(act, xT_done, b)
            nc.scalar.copy(xTs[:, :], misc[:, 0:N]).then_inc(xTs_done, 1)

        def dve_prep_norm(dve, b):
            after(dve, xh_turned, b)
            for j in range(TB):
                t = b * TB + j
                nc.vector.tensor_scalar(xh[:, j, :], keep.x[:, t, :], keep.mv[:, t, 0:1], keep.rstd_col(t),
                                        ALU.subtract, ALU.mult).then_inc(xh_done, 1)

        def dve_prep_bias(dve, b):
            dve.wait_ge(xh_done, (b + 1) * TB)
            for j in range(TB):
                t = b * TB + j
                nc.vector.tensor_tensor(keep.x[:, t, :], keep.x[:, t, :], keep.biases[:, R_BP:R_BP + P],
                                        ALU.add).then_inc(bp_added, 1)

        def dve_prep_copy(dve, b, half):
            dve.wait_ge(xTs_done, b + 1)
            after(dve, s_ready, (b - 1) * H)
            nc.vector.tensor_copy(xT[:, half, :], xTs[:, :]).then_inc(xT_done, 1)

        def dve_prep_values(dve, b, half):
            dve.wait_ge(v_ready, b + 1)
            after(dve, pv_done, (b - 1) * H)
            for j in range(TB):
                ins = nc.vector.tensor_tensor(
                    keep.v0[:, half, j, :, 0:DH],
                    misc[:, N + j * P:N + (j + 1) * P].rearrange("p (h e) -> p h e", h=H),
                    keep.biases[:, R_BV:R_BV + P].rearrange("p (h e) -> p h e", h=H), ALU.add)
            ins.then_inc(v_done, 1)

        def pe_folded(pe, k, h, i, half):
            after(pe, g_copied, k - 1)
            nc.tensor.matmul(g_ps[i][:, 0:N], keep.fold[:, h, :], xT[:, half, :], start=True,
                             stop=True).then_inc(g_ready, 1)

        def pe_scores(pe, k, i, half):
            pe.wait_ge(g_copied, k + 1)
            after(pe, exp_done, k - 1)
            s = s_ps[i]
            for out, j, keys in ((0, 0, P), (P, 1, 2 * P)):
                nc.tensor.matmul(s[:, out:out + keys], gT[:, i, j * P:(j + 1) * P], xT[:, half, 0:keys],
                                 start=True, stop=False)
                last = nc.tensor.matmul(s[:, out + keys - P:out + keys], keep.ident_bf[:, :], keep.mask_bf[:, :],
                                        start=False, stop=True)
            last.then_inc(s_ready, 1)

        def pe_turn(pe, k, i):
            pe.wait_ge(exp_done, k + 1)
            after(pe, pT_copied, k - 1)
            for c in range(3):
                last = nc.tensor.transpose(t_ps[i][:, c * P:(c + 1) * P], prob[:, i, c * P:(c + 1) * P], keep.ident)
            last.then_inc(pT_ready, 1)

        def pe_values(pe, k, h, i, half):
            pe.wait_ge(pT_copied, k + 1)
            for j, blocks in ((0, ((0, 0),)), (1, ((1, 0), (2, 1)))):
                for n, (c, kj) in enumerate(blocks):
                    last = nc.tensor.matmul(o_view[:, j, h, :], probT[:, i, c * P:(c + 1) * P],
                                            keep.v0[:, half, kj, h, :], start=(n == 0), stop=(n == len(blocks) - 1))
            last.then_inc(pv_done, 1)

        def pe_finish_turn(pe, b, values):
            pe.wait_ge(attn_done, (b + 1) * TB)
            pe.wait_ge(v_done, values)
            for j in range(TB):
                last = nc.tensor.transpose(misc[:, j * P:(j + 1) * P], attn[:, j, :], keep.ident)
            last.then_inc(attn_turned, 1)

        def pe_finish_project(pe, b):
            pe.wait_ge(attnT_done, b + 1)
            for j in range(TB):
                last = nc.tensor.matmul(misc[:, N + j * P:N + (j + 1) * P], attnT[:, j * P:(j + 1) * P],
                                        keep.wp[:, :], start=True, stop=True)
            last.then_inc(proj_ready, 1)

        def act_finish(act, b):
            act.wait_ge(attn_turned, b + 1)
            after(act, proj_ready, b)
            nc.scalar.copy(attnT[:, :], misc[:, 0:N]).then_inc(attnT_done, 1)

        def dve_finish_normalise(dve, b):
            dve.wait_ge(pv_done, (b + 1) * H)
            nc.vector.reciprocal(rec[:, :, :], o_view[:, :, :, DH]).then_inc(rec_done, 1)
            dve.wait_ge(rec_done, b + 1)
            after(dve, attn_turned, b)
            for j in range(TB):
                nc.vector.tensor_tensor(attn[:, j, :].rearrange("p (h e) -> p h e", h=H), o_view[:, j, :, 0:DH],
                                        rec[:, j, :].unsqueeze(2).to_broadcast([P, H, DH]),
                                        ALU.mult).then_inc(attn_done, 1)

        def dve_finish_residual(dve, b):
            dve.wait_ge(proj_ready, b + 1)
            dve.wait_ge(bp_added, (b + 1) * TB)
            for j in range(TB):
                t = b * TB + j
                nc.vector.tensor_tensor(keep.x[:, t, :], misc[:, N + j * P:N + (j + 1) * P], keep.x[:, t, :],
                                        ALU.add).then_inc(res_done, 1)

        def dve_stats(dve, b):
            for j in range(TB):
                nc.vector.bn_stats(keep.stats[:, b * TB + j, :], keep.x[:, b * TB + j, :])

        def act_head(act, k, i):
            act.wait_ge(max_done, k + 1)
            after(act, pT_ready, k - 1)
            nc.scalar.activation(prob[:, i, 0:P], s_ps[i][:, 0:P], ACT.Exp, bias=nmax[:, i, 0:1])
            nc.scalar.activation(prob[:, i, P:3 * P], s_ps[i][:, P:3 * P], ACT.Exp,
                                 bias=nmax[:, i, 1:2]).then_inc(exp_done, 1)

        def act_folded(act, k, h, i):
            act.wait_ge(g_ready, k + 1)
            after(act, s_ready, k - 1)
            nc.scalar.activation(gT[:, i, :], g_ps[i][:, 0:N], ACT.Identity,
                                 bias=keep.fold_bias[:, h:h + 1]).then_inc(g_copied, 1)

        def dve_head_max(dve, k, i):
            dve.wait_ge(s_ready, k + 1)
            after(dve, exp_done, k - 1)
            nc.vector.tensor_reduce(nmax[:, i, 0:1], s_ps[i][:, 0:P], AX_X, ALU.max, negate=True)
            nc.vector.tensor_reduce(nmax[:, i, 1:2], s_ps[i][:, P:3 * P], AX_X, ALU.max,
                                    negate=True).then_inc(max_done, 1)

        def dve_head_turned(dve, k, i):
            dve.wait_ge(pT_ready, k + 1)
            after(dve, pv_done, k - 1)
            nc.vector.tensor_copy(probT[:, i, :], t_ps[i][:, 0:3 * P]).then_inc(pT_copied, 1)

        def over_batches(engine, body):
            body(0, True, False)
            body(1, False, False)
            with engine.Fori(2, batches - 1) as b:
                body(b, False, False)
            body(batches - 1, False, True)

        with nc.Block() as block:
            @block.tensor
            def _(pe):
                pe_prep_turn(pe, 0)
                pe_prep_values(pe, 0)
                pe.wait_ge(xT_done, 1)
                pe_folded(pe, 0, 0, 0, 0)

                def body(b, first, last):
                    half = b % 2
                    for h in range(H):
                        k, i = b * H + h, h % 2
                        if h < H - 1:
                            pe_folded(pe, k + 1, h + 1, 1 - i, half)
                        elif not last:
                            pe.wait_ge(xT_done, b + 2)
                            pe_folded(pe, k + 1, 0, 1 - i, (b + 1) % 2)
                        pe_scores(pe, k, i, half)
                        if h >= 1 or not first:
                            pe_turn(pe, k - 1, 1 - i)
                        if h >= 2:
                            if h == 2:
                                pe.wait_ge(v_done, b + 1)
                                after(pe, attn_done, b * TB)
                            pe_values(pe, k - 2, h - 2, i, half)
                        elif not first:
                            pe_values(pe, k - 2, H + h - 2, i, (b + 1) % 2)
                        if h == 4 and not first:
                            pe_finish_turn(pe, b - 1, b + 1)
                        if h == 6 and not first:
                            pe_finish_project(pe, b - 1)
                        if h == 9 and not last:
                            pe_prep_turn(pe, b + 1)
                        if h == 11 and not last:
                            pe_prep_values(pe, b + 1)

                over_batches(pe, body)
                k = batches * H
                pe_turn(pe, k - 1, 1)
                pe_values(pe, k - 2, H - 2, 0, (batches - 1) % 2)
                pe_values(pe, k - 1, H - 1, 1, (batches - 1) % 2)
                pe_finish_turn(pe, batches - 1, batches)
                pe_finish_project(pe, batches - 1)

            @block.scalar
            def _(act):
                act_prep(act, 0)
                act_folded(act, 0, 0, 0)

                def body(b, first, last):
                    for h in range(H):
                        k, i = b * H + h, h % 2
                        if h < H - 1 or not last:
                            act_folded(act, k + 1, (h + 1) % H, 1 - i)
                        act_head(act, k, i)
                        if h == 4 and not first:
                            act_finish(act, b - 1)
                        if h == 9 and not last:
                            act_prep(act, b + 1)

                over_batches(act, body)
                act_finish(act, batches - 1)

            @block.vector
            def _(dve):
                dve_prep_norm(dve, 0)
                dve_prep_bias(dve, 0)
                dve_prep_copy(dve, 0, 0)
                dve_prep_values(dve, 0, 0)

                def body(b, first, last):
                    for h in range(H):
                        k, i = b * H + h, h % 2
                        if h == 2 and not first:
                            dve_finish_normalise(dve, b - 1)
                        if h == 7 and not first:
                            dve_finish_residual(dve, b - 1)
                        if h == 8 and not last:
                            dve_prep_norm(dve, b + 1)
                        if h == 9 and not last:
                            dve_prep_bias(dve, b + 1)
                        if h == 10 and not last:
                            dve_prep_copy(dve, b + 1, (b + 1) % 2)
                        if h == 12 and not last:
                            dve_prep_values(dve, b + 1, (b + 1) % 2)
                        dve_head_max(dve, k, i)
                        if h == 8 and not first:
                            dve.wait_ge(res_done, b * TB)
                        if h >= 1 or not first:
                            dve_head_turned(dve, k - 1, 1 - i)
                        if h == 8 and not first:
                            dve_stats(dve, b - 1)

                over_batches(dve, body)
                dve_head_turned(dve, batches * H - 1, 1)
                dve_finish_normalise(dve, batches - 1)
                dve_finish_residual(dve, batches - 1)
                dve.wait_ge(res_done, batches * TB)
                dve_stats(dve, batches - 1)


def over_pairs(engine, pairs, body):
    body(0, True)
    if pairs > 1:
        body(1, False)
    if pairs > 2:
        with engine.Fori(2, pairs) as p:
            body(p, False)


def route(nc, keep, wide, tiles):
    pairs = tiles // (2 * TC)
    with ExitStack() as stack:
        m = Names(nc, stack)
        xh = m.sb("xh1", [P, 2, TC, P])
        xTs = m.sb("xTs1", [P, 2, CHUNK])
        logits = m.sb("logits", [P, tiles, E])
        score = m.sb("score", [P, tiles, E])
        choice = m.sb("choice", [P, tiles, E])
        rank = m.sb("rank", [P, tiles, E])
        test = m.sb("test", [P, tiles, E])
        hi2 = m.sb("hi2", [P, tiles, NG, 2])
        sum2 = m.sb("sum2", [P, tiles, NG, 2])
        gscore = m.sb("gscore", [P, tiles, NG])
        grank = m.sb("grank", [P, tiles, NG])
        gtest = m.sb("gtest", [P, tiles, NG])
        total = m.sb("total", [P, tiles])
        inv = m.sb("inv", [P, tiles])
        x_ps = [m.ps(f"x_ps{i}", [P, 512]) for i in range(2)]
        l_ps = [m.ps(f"l_ps{i}", [P, 512]) for i in range(2)]

        xh_done, xh_turned = m.sem("xh_done1"), m.sem("xh_turned1")
        xTs_done, xT_done = m.sem("xTs_done1"), m.sem("xT_done1")
        l_ready, l_copied = m.sem("l_ready"), m.sem("l_copied")
        scored, step = m.sem("scored"), m.sem("route_step")

        with nc.Block() as block:
            @block.tensor
            def _(pe):
                def body(p, first):
                    for i in range(2):
                        c = 2 * p + i
                        pe.wait_ge(xh_done, (c + 1) * TC)
                        if not first:
                            pe.wait_ge(xTs_done, c - 1)
                            pe.wait_ge(xT_done, c - 1)
                        for t in range(TC):
                            last = nc.tensor.transpose(x_ps[i][:, t * P:(t + 1) * P], xh[:, i, t, :], keep.ident)
                        last.then_inc(xh_turned, 1)
                        pe.wait_ge(xTs_done, c + 1)
                        if not first:
                            pe.wait_ge(l_copied, c - 1)
                        for t in range(TC):
                            last = nc.tensor.matmul(l_ps[i][:, t * E:(t + 1) * E], xTs[:, i, t * P:(t + 1) * P],
                                                    keep.routerT[:, :], start=True, stop=True)
                        last.then_inc(l_ready, 1)
                over_pairs(pe, pairs, body)

            @block.scalar
            def _(act):
                def body(p, first):
                    for i in range(2):
                        c = 2 * p + i
                        act.wait_ge(xh_turned, c + 1)
                        if not first:
                            act.wait_ge(l_ready, c - 1)
                        nc.scalar.copy(xTs[:, i, :], x_ps[i][:, :]).then_inc(xTs_done, 1)
                        act.wait_ge(xTs_done, c + 1)
                        nc.scalar.copy(wide.xT[:, c, :], xTs[:, i, :]).then_inc(xT_done, 1)
                over_pairs(act, pairs, body)
                act.wait_ge(l_copied, 2 * pairs)
                nc.scalar.activation(score[:, :, :], logits[:, :, :], ACT.Sigmoid).then_inc(scored, 1)

            @block.vector
            def _(dve):
                def norm(c, i):
                    for t in range(TC):
                        n = c * TC + t
                        nc.vector.tensor_scalar(xh[:, i, t, :], keep.x[:, n, :], keep.mv[:, n, 0:1],
                                                keep.rstd_col(n), ALU.subtract, ALU.mult).then_inc(xh_done, 1)

                def body(p, first):
                    for i in range(2):
                        c = 2 * p + i
                        if not first:
                            dve.wait_ge(xh_turned, c - 1)
                        norm(c, i)
                    for i in range(2):
                        c = 2 * p + i
                        dve.wait_ge(l_ready, c + 1)
                        nc.vector.tensor_copy(logits[:, bass.ds(c * TC, TC), :],
                                              l_ps[i][:, 0:TC * E].rearrange("p (t e) -> p t e", t=TC)
                                              ).then_inc(l_copied, 1)
                over_pairs(dve, pairs, body)

                steps = [0]

                def then(ins):
                    steps[0] += 1
                    ins.then_inc(step, 1)
                    dve.wait_ge(step, steps[0])

                v = nc.vector
                dve.wait_ge(scored, 1)
                bias = keep.biases[:, R_EB:R_EB + E].unsqueeze(1).to_broadcast([P, tiles, E])
                then(v.tensor_tensor(choice[:, :, :], score[:, :, :], bias, ALU.add))
                quad = choice[:, :, :].rearrange("p t (g h a) -> p t g h a", g=NG, h=2)
                flat = lambda ap: ap.rearrange("p t g h -> p (t g h)")
                half = choice[:, :, :].rearrange("p t (q a) -> p (t q) a", a=2)
                hi2f, sum2f = flat(hi2[:, :, :, :]), flat(sum2[:, :, :, :])
                v.tensor_tensor(hi2f, half[:, :, 0], half[:, :, 1], ALU.max)
                then(v.tensor_tensor(sum2f, half[:, :, 0], half[:, :, 1], ALU.add))
                hi2p = hi2[:, :, :, :].rearrange("p t g h -> p (t g) h")
                sum2p = sum2[:, :, :, :].rearrange("p t g h -> p (t g) h")
                gs = gscore[:, :, :].rearrange("p t g -> p (t g)")
                gt = gtest[:, :, :].rearrange("p t g -> p (t g)")
                v.tensor_tensor(gs, hi2p[:, :, 0], hi2p[:, :, 1], ALU.add)
                then(v.tensor_tensor(gt, sum2p[:, :, 0], sum2p[:, :, 1], ALU.max))
                then(v.tensor_tensor(gs, gs, gt, ALU.max))

                def ranks(values, rank, test, width):
                    for e in range(width):
                        ins = v.memset(rank[:, :, e:e + 1], float(width - 1 - e))
                    then(ins)
                    for d in range(1, width):
                        lo, hi = slice(0, width - d), slice(d, width)
                        then(v.tensor_tensor(test[:, :, lo], values[:, :, lo], values[:, :, hi], ALU.is_ge))
                        then(v.tensor_tensor(rank[:, :, lo], rank[:, :, lo], test[:, :, lo], ALU.subtract))
                        then(v.tensor_tensor(rank[:, :, hi], rank[:, :, hi], test[:, :, lo], ALU.add))

                ranks(gscore, grank, gtest, NG)
                then(v.tensor_scalar(gtest[:, :, :], grank[:, :, :], float(TOPK_GROUP), None, ALU.is_lt))
                grouped = choice[:, :, :].rearrange("p t (g a) -> p (t g) a", g=NG)
                then(v.tensor_tensor(grouped, grouped,
                                     gtest[:, :, :].rearrange("p t g -> p (t g)").unsqueeze(2)
                                     .to_broadcast([P, tiles * NG, EG]), ALU.mult))
                ranks(choice, rank, test, E)
                then(v.scalar_tensor_tensor(out=test[:, :, :], in0=rank[:, :, :], scalar=float(TOP_K),
                                            in1=score[:, :, :], op0=ALU.is_lt, op1=ALU.mult))
                then(v.tensor_reduce(total[:, :], test[:, :, :], AX_X, ALU.add))
                then(v.tensor_scalar(total[:, :], total[:, :], 1e-20, None, ALU.add))
                then(v.reciprocal(inv[:, :], total[:, :]))
                then(v.scalar_tensor_tensor(out=rank[:, :, :], in0=test[:, :, :], scalar=SCALING,
                                            in1=inv[:, :].unsqueeze(2).to_broadcast([P, tiles, E]),
                                            op0=ALU.mult, op1=ALU.mult))
                v.memset(wide.weight[:, tiles:tiles + TC, :], 0.0)
                for part in range(PARTS):
                    w = wide.weight[:, 0:tiles, part * E:(part + 1) * E]
                    then(v.tensor_copy(w, rank[:, :, :]))
                    if part < PARTS - 1:
                        then(v.tensor_tensor(rank[:, :, :], rank[:, :, :], w, ALU.subtract))


def experts(nc, keep, wide, tiles):
    pairs = tiles // (2 * TC)
    chunks = 2 * pairs
    with ExitStack() as stack:
        m = Names(nc, stack)
        wst = m.sb("wst", [P, 2, TC, PARTS * E], BF16)
        wT = m.sb("wT", [PARTS * E, 2, CHUNK], BF16)
        act_g = m.sb("act_g", [P, 2, CHUNK])
        gated = m.sb("gated", [P, 2, CHUNK])
        inter = m.sb("inter", [P, 2, CHUNK])
        g_ps = [m.ps(f"eg_ps{i}", [P, 512]) for i in range(2)]
        u_ps = [m.ps(f"eu_ps{i}", [P, 512]) for i in range(2)]
        w_ps = [m.ps(f"ew_ps{i}", [P, 512]) for i in range(2)]
        wT_ps = m.ps("wT_ps", [P, 1024], BF16)
        y_ps = m.ps("y_ps", [P, 512])

        wst_done, w_turned, wT_done = m.sem("wst_done"), m.sem("w_turned"), m.sem("wT_done")
        g_ready, u_ready, w_ready = m.sem("eg_ready"), m.sem("eu_ready"), m.sem("ew_ready")
        silu_done, gated_done, inter_done = m.sem("silu_done"), m.sem("gated_done"), m.sem("inter_done")
        down_done, res_done = m.sem("down_done"), m.sem("res_done2")


        with nc.Block() as block:
            @block.tensor
            def _(pe):
                def weights_staged(c):
                    pe.wait_ge(wst_done, c + 1)
                    after(pe, wT_done, c)

                def turn_weights(i):
                    for t in range(TC):
                        last = nc.tensor.transpose(wT_ps[0:PARTS * E, t * P:(t + 1) * P], wst[:, i, t, :],
                                                   keep.ident_bf[:, :])
                    last.then_inc(w_turned, 1)

                def down(n, j, q, c, first):
                    pe.wait_ge(inter_done, n + 1)
                    if j == 0 and not first:
                        pe.wait_ge(res_done, c)
                    for t in range(TC):
                        last = nc.tensor.matmul(y_ps[:, t * P:(t + 1) * P], inter[:, q, t * P:(t + 1) * P],
                                                keep.downT[:, j, :], start=(j == 0 and t == 0),
                                                stop=(j == BLOCKS - 1), skip_group_check=True)
                    last.then_inc(down_done, 1)

                def body(p, first):
                    for i in range(2):
                        c = 2 * p + i
                        for j in range(BLOCKS):
                            q = (i * BLOCKS + j) % 2
                            n = c * BLOCKS + j
                            x = wide.xT[:, c, :]
                            early = first and i == 0
                            if j == 6:
                                weights_staged(c + 1)
                            if not (early and j < 2):
                                pe.wait_ge(silu_done, n - 1)
                            nc.tensor.matmul(g_ps[q][:, :], keep.gateT[:, j, :], x, start=True,
                                             stop=True).then_inc(g_ready, 1)
                            if j == 6:
                                turn_weights(1 - i)
                            if not (early and j < 2):
                                pe.wait_ge(inter_done, n - 1)
                            nc.tensor.matmul(u_ps[q][:, :], keep.upT[:, j, :], x, start=True,
                                             stop=True).then_inc(u_ready, 1)
                            if j < PAIRS:
                                if j == 0:
                                    pe.wait_ge(wT_done, c + 1)
                                nc.tensor.matmul(w_ps[q][:, :], keep.sel_bf[:, j * P:(j + 1) * P], wT[:, i, :],
                                                 start=True, stop=True).then_inc(w_ready, 1)
                            if j > 0:
                                down(n - 1, j - 1, 1 - q, c, early)
                            elif not early:
                                down(n - 1, BLOCKS - 1, 1 - q, c - 1, False)
                weights_staged(0)
                turn_weights(0)
                over_pairs(pe, pairs, body)
                down(chunks * BLOCKS - 1, BLOCKS - 1, 1, chunks - 1, False)

            @block.scalar
            def _(act):
                def copy_weights(c, i):
                    act.wait_ge(w_turned, c + 1)
                    after(act, w_ready, (c - 1) * PAIRS)
                    nc.scalar.copy(wT[:, i, :], wT_ps[0:PARTS * E, 0:CHUNK]).then_inc(wT_done, 1)

                def body(p, first):
                    for i in range(2):
                        c = 2 * p + i
                        for j in range(BLOCKS):
                            if j == 7:
                                copy_weights(c + 1, 1 - i)
                            q = (i * BLOCKS + j) % 2
                            n = c * BLOCKS + j
                            act.wait_ge(g_ready, n + 1)
                            if not (first and i == 0 and j < 2):
                                act.wait_ge(inter_done, n - 1)
                            nc.scalar.activation(act_g[:, q, :], g_ps[q][:, :], ACT.Silu).then_inc(silu_done, 1)
                copy_weights(0, 0)
                over_pairs(act, pairs, body)

            @block.vector
            def _(dve):
                def stage_weights(c, i):
                    after(dve, w_turned, c - 1)
                    nc.vector.tensor_copy(wst[:, i, :, :], wide.weight[:, bass.ds(c * TC, TC), :]).then_inc(wst_done, 1)

                def residual(c):
                    dve.wait_ge(down_done, (c + 1) * BLOCKS)
                    nc.vector.tensor_tensor(keep.x[:, bass.ds(c * TC, TC), :],
                                            y_ps[:, :].rearrange("p (t d) -> p t d", t=TC),
                                            keep.x[:, bass.ds(c * TC, TC), :], ALU.add).then_inc(res_done, 1)

                def statistics(c):
                    for t in range(TC):
                        nc.vector.bn_stats(keep.stats[:, c * TC + t, :], keep.x[:, c * TC + t, :])

                def body(p, first):
                    for i in range(2):
                        c = 2 * p + i
                        for j in range(BLOCKS):
                            q = (i * BLOCKS + j) % 2
                            n = c * BLOCKS + j
                            if j == 1 and not (first and i == 0):
                                residual(c - 1)
                            if j == 4:
                                stage_weights(c + 1, 1 - i)
                            dve.wait_ge(silu_done, n + 1)
                            dve.wait_ge(u_ready, n + 1)
                            early = first and i == 0 and j < 2
                            if not early:
                                dve.wait_ge(down_done, n - 1)
                            if j == 2 and not (first and i == 0):
                                dve.wait_ge(res_done, c)
                            if j < PAIRS:
                                nc.vector.tensor_tensor(gated[:, q, :], u_ps[q][:, :], act_g[:, q, :],
                                                        ALU.mult).then_inc(gated_done, 1)
                                dve.wait_ge(gated_done, c * PAIRS + j + 1)
                                dve.wait_ge(w_ready, c * PAIRS + j + 1)
                                nc.vector.tensor_tensor(inter[:, q, :], w_ps[q][:, :], gated[:, q, :],
                                                        ALU.mult).then_inc(inter_done, 1)
                            else:
                                nc.vector.tensor_tensor(inter[:, q, :], u_ps[q][:, :], act_g[:, q, :],
                                                        ALU.mult).then_inc(inter_done, 1)
                            if j == 2 and not (first and i == 0):
                                statistics(c - 1)

                stage_weights(0, 0)
                over_pairs(dve, pairs, body)
                residual(chunks - 1)
                dve.wait_ge(res_done, chunks)
                statistics(chunks - 1)


def hyperbolic_attention(nc, keep, batches):
    pairs = batches // 2
    S = len(PAIRINGS)
    GROUP = 4
    GROUPS = H // GROUP
    ROWS = 32
    IROW = 64
    JH = TB * H
    FW = QD + 2
    with ExitStack() as stack:
        m = Names(nc, stack)
        xh = m.sb("xh3", [P, TB, P])
        xTs = m.sb("xTs3", [P, N])
        qkv = m.sb("qkv", [P, TB, 3, P])
        square = m.sb("square", [P, TB, 2, P])
        norm2 = m.sb("norm2", [P, TB, 2, H])
        gap = m.sb("gap", [P, TB, 2, H])
        sides = m.sb("sides", [P, 2, TB, 2, H])
        isides = m.sb("isides", [P, 2, TB, 2, H])
        signs = m.sb("signs", [P, 2, TB, 2, H])
        feat = m.sb("feat", [P, 2, JH, FW])
        rest = m.sb("rest", [P, 2, JH, FW])
        part = [m.sb(f"part{i}", [P, 2, JH, FW], BF16) for i in range(PARTS)]
        rows = m.sb("rows", [P, 2, JH, P], BF16)
        rowsT = m.sb("rowsT", [P, 2, GROUPS, GROUP * N], BF16)
        dist = m.sb("dist", [P, 2, 2 * N])
        u = m.sb("u", [P, H, 2 * N])
        w = m.sb("w", [P, 2, H, 2 * N])
        v = m.sb("v3", [P, 2, TB, H, ROWS])
        o = m.sb("o3", [P, GROUPS, N])
        rec = m.sb("rec3", [P, TB, H])
        attn = m.sb("attn3", [P, TB, P])
        attnT = m.sb("attnT3", [P, N])

        d_ps = [m.ps(f"d_ps{i}", [P, 512]) for i in range(2)]
        i_ps = [m.ps(f"i_ps{i}", [P, 512]) for i in range(2)]
        o_ps = [m.ps(f"o_ps3{i}", [P, 512]) for i in range(2)]
        r_ps = m.ps("r_ps", [P, 1024], BF16)
        misc = m.ps("misc3", [P, 512])

        S_ = m.sem
        zeroed, v_cleared = S_("zeroed"), S_("v_cleared")
        xh_done, xh_turned, xT_done = S_("xh_done3"), S_("xh_turned3"), S_("xT_done3")
        qkv_ready, qkv_copied = S_("qkv_ready"), S_("qkv_copied")
        square_done, norm2_done, gap_done = S_("square_done"), S_("norm2_done"), S_("gap_done")
        sides_done, isides_done, masked_done, feat_done = S_("sides_done"), S_("isides_done"), S_("masked_done"), S_("feat_done")
        part_done, rest_done, rows_done = S_("part_done"), S_("rest_done"), S_("rows_done")
        rows_turned, rowsT_done, v_done = S_("rows_turned"), S_("rowsT_done"), S_("v_done3")
        d_ready, dist_done, u_done, prod_done = S_("d_ready"), S_("dist_done"), S_("u_done"), S_("prod_done")
        root_done, sum_done, ln_done, w_done, pv_done = S_("root_done"), S_("sum_done3"), S_("ln_done"), S_("w_done"), S_("pv_done3")
        o_copied, o_turned, rec_done, attn_done = S_("o_copied"), S_("o_turned"), S_("rec_done3"), S_("attn_done3")
        attn_turned, attnT_done, proj_ready = S_("attn_turned3"), S_("attnT_done3"), S_("proj_ready3")
        res_done = S_("res_done3")

        def on_scalar(h):
            return h % 2 == 0

        def pe_turn_x(pe, b):
            pe.wait_ge(xh_done, (b + 1) * TB)
            after(pe, res_done, (b - 2) * TB)
            after(pe, qkv_copied, b * TB)
            for j in range(TB):
                last = nc.tensor.transpose(misc[:, j * P:(j + 1) * P], xh[:, j, :], keep.ident)
            last.then_inc(xh_turned, 1)

        def pe_qkv(pe, b, j):
            pe.wait_ge(xT_done, b + 1)
            after(pe, qkv_copied, b * TB + j)
            nc.tensor.matmul(misc[:, 0:3 * P], xTs[:, j * P:(j + 1) * P], keep.qkvoT[:, 0:3, :], start=True,
                             stop=True).then_inc(qkv_ready, 1)

        def pe_turn_rows(pe, b, g):
            pe.wait_ge(rows_done, b + 1)
            for side in range(2):
                after(pe, rowsT_done, b * 2 * GROUPS + 2 * g + side)
                for q in range(GROUP):
                    for j in range(TB):
                        last = nc.tensor.transpose(r_ps[:, (q * TB + j) * P:(q * TB + j + 1) * P],
                                                   rows[:, side, j * H + g * GROUP + q, :], keep.ident_bf[:, :])
                last.then_inc(rows_turned, 1)

        def pe_distances(pe, b, h):
            k, i = b * H + h, h % 2
            g, q = h // GROUP, h % GROUP
            pe.wait_ge(rowsT_done, b * 2 * GROUPS + 2 * g + 2)
            after(pe, u_done, k - 1)
            after(pe, dist_done, k - 1)
            for r0, n, ps in ((0, S * QD, d_ps[i]), (IROW, 2 * S, i_ps[i])):
                for j in range(TB):
                    last = nc.tensor.matmul(
                        ps[:, j * N:(j + 1) * N],
                        rowsT[r0:r0 + n, 1, g, q * N + j * P:q * N + (j + 1) * P],
                        rowsT[r0:r0 + n, 0, g, q * N:(q + 1) * N], start=True, stop=True)
            last.then_inc(d_ready, 1)

        def pe_values(pe, b, h, i):
            pe.wait_ge(w_done, b * H + h + 1)
            if h == 0:
                pe.wait_ge(v_done, b + 1)
                after(pe, o_copied, b * 2)
            g, q = h // GROUP, h % GROUP
            out = o_ps[g // 2][q * ROWS:(q + 1) * ROWS, (g % 2) * N:(g % 2 + 1) * N]
            for j in range(TB):
                last = nc.tensor.matmul(out, v[:, i, j, h, :], w[:, i, h, j * N:(j + 1) * N], start=(j == 0),
                                        stop=(j == TB - 1))
            last.then_inc(pv_done, 1)

        def pe_turn_o(pe, b, j, users):
            pe.wait_ge(o_copied, (b + 1) * 2)
            after(pe, qkv_copied, users * TB)
            after(pe, attn_done, b * TB + j)
            for g in range(GROUPS):
                last = nc.tensor.transpose(misc[:, g * P:(g + 1) * P], o[:, g, j * P:(j + 1) * P], keep.ident)
            last.then_inc(o_turned, 1)

        def pe_turn_attn(pe, b):
            pe.wait_ge(attn_done, (b + 1) * TB)
            for j in range(TB):
                last = nc.tensor.transpose(misc[:, j * P:(j + 1) * P], attn[:, j, :], keep.ident)
            last.then_inc(attn_turned, 1)

        def pe_project(pe, b):
            pe.wait_ge(attnT_done, b + 1)
            for j in range(TB):
                last = nc.tensor.matmul(misc[:, N + j * P:N + (j + 1) * P], attnT[:, j * P:(j + 1) * P],
                                        keep.qkvoT[:, 3, :], start=True, stop=True)
            last.then_inc(proj_ready, 1)

        def act_xT(act, b):
            act.wait_ge(xh_turned, b + 1)
            after(act, qkv_ready, b * TB)
            nc.scalar.copy(xTs[:, :], misc[:, 0:N]).then_inc(xT_done, 1)

        def act_qkv(act, b, j):
            act.wait_ge(qkv_ready, b * TB + j + 1)
            after(act, feat_done, b)
            after(act, v_done, b)
            after(act, square_done, b)
            nc.scalar.copy(qkv[:, j, :, :], misc[:, 0:3 * P].rearrange("p (s c) -> p s c", s=3)
                           ).then_inc(qkv_copied, 1)

        def act_rows(act, b, g):
            for side in range(2):
                act.wait_ge(rows_turned, b * 2 * GROUPS + 2 * g + side + 1)
                after(act, d_ready, (b - 1) * H + (g + 1) * GROUP)
                nc.scalar.copy(rowsT[:, side, g, :], r_ps[:, :]).then_inc(rowsT_done, 1)

        def take_distances(engine, b, h):
            k, i = b * H + h, h % 2
            engine.wait_ge(d_ready, k + 1)
            after(engine, dist_done, k)
            after(engine, u_done, k - 1)
            if on_scalar(h):
                ins = nc.scalar.activation(dist[:, i, :], d_ps[i][:, :], ACT.Relu)
            else:
                ins = nc.vector.tensor_scalar(dist[:, i, :], d_ps[i][:, :], 0.0, None, ALU.max)
            ins.then_inc(dist_done, 1)

        def act_root(act, b, h, i):
            act.wait_ge(prod_done, b * H + h + 1)
            nc.scalar.activation(w[:, i, h, :], w[:, i, h, :], ACT.Sqrt).then_inc(root_done, 1)

        def act_weight(act, b, h, i):
            k = b * H + h
            act.wait_ge(sum_done, k + 1)
            nc.scalar.activation(w[:, i, h, :], w[:, i, h, :], ACT.Ln, bias=1.0).then_inc(ln_done, 1)
            act.wait_ge(ln_done, k + 1)
            nc.scalar.activation(w[:, i, h, :], w[:, i, h, :], ACT.Exp, scale=-1.0).then_inc(w_done, 1)

        def act_attnT(act, b):
            act.wait_ge(attn_turned, b + 1)
            after(act, proj_ready, b)
            nc.scalar.copy(attnT[:, :], misc[:, 0:N]).then_inc(attnT_done, 1)

        def pool_sum(pool, b, h, i):
            k = b * H + h
            pool.wait_ge(root_done, k + 1)
            pool.wait_ge(u_done, k + 1)
            nc.gpsimd.tensor_tensor(w[:, i, h, :], u[:, h, :], w[:, i, h, :], ALU.add).then_inc(sum_done, 1)

        def pool_square(pool, b):
            pool.wait_ge(qkv_copied, (b + 1) * TB)
            after(pool, norm2_done, b)
            nc.gpsimd.tensor_tensor(square[:, :, :, :], qkv[:, :, 0:2, :], qkv[:, :, 0:2, :], ALU.mult
                                    ).then_inc(square_done, 1)

        def dve_norm(dve, b):
            after(dve, xh_turned, b)
            for j in range(TB):
                t = b * TB + j
                nc.vector.tensor_scalar(xh[:, j, :], keep.x[:, t, :], keep.mv[:, t, 0:1], keep.rstd_col(t),
                                        ALU.subtract, ALU.mult).then_inc(xh_done, 1)

        def dve_features(dve, b):
            vec = nc.vector
            by_head = lambda ap: ap.rearrange("p j (h e) -> p j h e", h=H)
            f = [feat[:, s, :, :].rearrange("p (j h) f -> p j h f", j=TB) for s in range(2)]
            dve.wait_ge(qkv_copied, (b + 1) * TB)
            after(dve, part_done, b * PARTS)
            vec.tensor_scalar(f[0][:, :, :, 0:DH], by_head(qkv[:, :, 0, :]), -4.0, None, ALU.mult)
            vec.tensor_copy(f[1][:, :, :, 0:DH], by_head(qkv[:, :, 1, :]))
            dve.wait_ge(square_done, b + 1)
            vec.tensor_reduce(norm2[:, :, :, :].rearrange("p j s h -> p (j s h)"),
                              square[:, :, :, :].rearrange("p j s (h e) -> p (j s h) e", h=H), AX_X,
                              ALU.add).then_inc(norm2_done, 1)
            dve.wait_ge(norm2_done, b + 1)
            vec.tensor_scalar(f[0][:, :, :, DH], norm2[:, :, 0, :], 2.0, None, ALU.mult)
            vec.tensor_copy(f[1][:, :, :, DH + 1], norm2[:, :, 1, :])
            vec.tensor_scalar(gap[:, :, :, :], norm2[:, :, :, :], -1.0, 1.0, ALU.mult, ALU.add).then_inc(gap_done, 1)
            dve.wait_ge(gap_done, b + 1)
            vec.tensor_scalar(sides[:, 0], gap[:, :, :, :], TINY, None, ALU.max)
            vec.tensor_scalar(sides[:, 1], gap[:, :, :, :], -1.0, TINY, ALU.mult, ALU.max)
            vec.tensor_scalar(signs[:, 0], gap[:, :, :, :], 0.0, None, ALU.is_ge)
            vec.tensor_scalar(signs[:, 1], gap[:, :, :, :], 0.0, None, ALU.is_lt).then_inc(sides_done, 1)
            dve.wait_ge(sides_done, b + 1)
            vec.reciprocal(isides[:, :, :, :, :], sides[:, :, :, :, :]).then_inc(isides_done, 1)
            dve.wait_ge(isides_done, b + 1)
            vec.tensor_tensor(isides[:, :, :, :, :], isides[:, :, :, :, :], signs[:, :, :, :, :],
                              ALU.mult).then_inc(masked_done, 1)
            dve.wait_ge(masked_done, b + 1)
            for a in range(2):
                vec.tensor_copy(f[0][:, :, :, QD + a], isides[:, a, :, 0, :])
                ins = vec.scalar_tensor_tensor(out=f[1][:, :, :, QD + a], in0=signs[:, 1 - a, :, 1, :], scalar=BIG,
                                               in1=isides[:, a, :, 1, :], op0=ALU.mult, op1=ALU.add)
            ins.then_inc(feat_done, 1)

        def dve_split(dve, b):
            dve.wait_ge(feat_done, b + 1)
            after(dve, rows_done, b)
            src = feat
            for n in range(PARTS):
                nc.vector.tensor_copy(part[n][:, :, :, :], src[:, :, :, :]).then_inc(part_done, 1)
                if n < PARTS - 1:
                    dve.wait_ge(part_done, b * PARTS + n + 1)
                    nc.vector.tensor_tensor(rest[:, :, :, :], src[:, :, :, :], part[n][:, :, :, :],
                                            ALU.subtract).then_inc(rest_done, 1)
                    dve.wait_ge(rest_done, b * (PARTS - 1) + n + 1)
                    src = rest

        def dve_rows(dve, b):
            dve.wait_ge(part_done, (b + 1) * PARTS)
            after(dve, rows_turned, b * 2 * GROUPS)
            for side in range(2):
                for s, pair in enumerate(PAIRINGS):
                    p = part[pair[side]]
                    nc.vector.tensor_copy(rows[:, side, :, s * QD:(s + 1) * QD], p[:, side, :, 0:QD])
                    ins = nc.vector.tensor_copy(rows[:, side, :, IROW + 2 * s:IROW + 2 * s + 2], p[:, side, :, QD:FW])
            ins.then_inc(rows_done, 1)

        def dve_values(dve, b, i):
            dve.wait_ge(qkv_copied, (b + 1) * TB)
            after(dve, pv_done, (b - 1) * H)
            for j in range(TB):
                ins = nc.vector.tensor_copy(v[:, i, j, :, 0:DH], qkv[:, j, 2, :].rearrange("p (h e) -> p h e", h=H))
            ins.then_inc(v_done, 1)

        def dve_ratio(dve, b, h, i):
            k, q = b * H + h, h % 2
            dve.wait_ge(dist_done, k + 1)
            after(dve, sum_done, k + 1 - H)
            nc.vector.scalar_tensor_tensor(out=u[:, h, :], in0=i_ps[q][:, :], scalar=1.0 / DEN_MIN,
                                           in1=dist[:, q, :], op0=ALU.min, op1=ALU.mult).then_inc(u_done, 1)
            dve.wait_ge(u_done, k + 1)
            after(dve, pv_done, k + 1 - 2 * H)
            nc.vector.scalar_tensor_tensor(out=w[:, i, h, :], in0=u[:, h, :], scalar=2.0, in1=u[:, h, :],
                                           op0=ALU.add, op1=ALU.mult).then_inc(prod_done, 1)

        def dve_copy_o(dve, b):
            dve.wait_ge(pv_done, (b + 1) * H)
            after(dve, o_turned, b * TB)
            for n in range(2):
                nc.vector.tensor_copy(o[:, 2 * n:2 * n + 2, :], o_ps[n][:, :].rearrange("p (g n) -> p g n", g=2)
                                      ).then_inc(o_copied, 1)

        def dve_normalise(dve, b, j):
            dve.wait_ge(o_turned, b * TB + j + 1)
            after(dve, attn_turned, b)
            ov = misc[:, :].rearrange("p (h r) -> p h r", h=H)
            nc.vector.reciprocal(rec[:, j, :], ov[:, :, DH]).then_inc(rec_done, 1)
            dve.wait_ge(rec_done, b * TB + j + 1)
            nc.vector.tensor_tensor(attn[:, j, :].rearrange("p (h e) -> p h e", h=H), ov[:, :, 0:DH],
                                    rec[:, j, :].unsqueeze(2).to_broadcast([P, H, DH]), ALU.mult
                                    ).then_inc(attn_done, 1)

        def dve_residual(dve, b):
            dve.wait_ge(proj_ready, b + 1)
            for j in range(TB):
                t = b * TB + j
                nc.vector.tensor_tensor(keep.x[:, t, :], misc[:, N + j * P:N + (j + 1) * P], keep.x[:, t, :],
                                        ALU.add).then_inc(res_done, 1)

        def dve_stats(dve, b):
            for j in range(TB):
                nc.vector.bn_stats(keep.stats[:, b * TB + j, :], keep.x[:, b * TB + j, :])

        def over_batches(engine, body):
            def turn(p, first, last):
                for i in range(2):
                    b = 2 * p + i
                    body(b, i, not (first and i == 0), not first, not (last and i == 1))
            turn(0, True, pairs == 1)
            if pairs > 2:
                turn(1, False, False)
            if pairs > 3:
                with engine.Fori(2, pairs - 1) as p:
                    turn(p, False, False)
            if pairs > 1:
                turn(pairs - 1, False, True)

        END = batches - 1

        with nc.Block() as block:
            @block.tensor
            def _(pe):
                pe.wait_ge(zeroed, 4)
                pe_turn_x(pe, 0)
                for j in range(TB):
                    pe_qkv(pe, 0, j)
                for g in range(2):
                    pe_turn_rows(pe, 0, g)

                def body(b, i, one_before, two_before, one_after):
                    for h in range(H):
                        pe_distances(pe, b, h)
                        if h == 1:
                            pe_turn_rows(pe, b, 2)
                        if h == 3:
                            pe_turn_rows(pe, b, 3)
                        if two_before:
                            if h in (1, 2):
                                pe_turn_o(pe, b - 2, h - 1, b + 1)
                            if h == 3:
                                pe_turn_attn(pe, b - 2)
                            if h == 4:
                                pe_project(pe, b - 2)
                        if one_after:
                            if h == 6:
                                pe_turn_x(pe, b + 1)
                            if h in (7, 8):
                                pe_qkv(pe, b + 1, h - 7)
                            if h in (14, 15):
                                pe_turn_rows(pe, b + 1, h - 14)
                        if one_before:
                            pe_values(pe, b - 1, h, 1 - i)
                over_batches(pe, body)
                pe_turn_o(pe, END - 1, 0, batches)
                pe_turn_o(pe, END - 1, 1, batches)
                pe_turn_attn(pe, END - 1)
                pe_project(pe, END - 1)
                for h in range(H):
                    pe_values(pe, END, h, 1)
                after(pe, res_done, END * TB)
                pe_turn_o(pe, END, 0, batches)
                pe_turn_o(pe, END, 1, batches)
                pe_turn_attn(pe, END)
                pe_project(pe, END)

            @block.scalar
            def _(act):
                act_xT(act, 0)
                for j in range(TB):
                    act_qkv(act, 0, j)
                for g in range(2):
                    act_rows(act, 0, g)

                def body(b, i, one_before, two_before, one_after):
                    nc.scalar.preload_act_table_set("natural_log_exp_and_others")
                    for h in range(H):
                        if on_scalar(h):
                            take_distances(act, b, h)
                        if h == 1:
                            act_rows(act, b, 2)
                        if h == 3:
                            act_rows(act, b, 3)
                        if two_before and h == 4:
                            act_attnT(act, b - 2)
                        if one_after:
                            if h == 6:
                                act_xT(act, b + 1)
                            if h in (7, 8):
                                act_qkv(act, b + 1, h - 7)
                            if h in (14, 15):
                                act_rows(act, b + 1, h - 14)
                        if one_before:
                            act_weight(act, b - 1, h, 1 - i)
                    for h in range(H):
                        act_root(act, b, h, i)
                over_batches(act, body)
                nc.scalar.preload_act_table_set("natural_log_exp_and_others")
                act_attnT(act, END - 1)
                for h in range(H):
                    act_weight(act, END, h, 1)
                act_attnT(act, END)

            @block.gpsimd
            def _(pool):
                nc.gpsimd.memset(rows[:, :, :, :], 0.0).then_inc(zeroed, 1)
                nc.gpsimd.memset(v[:, :, :, :, DH:ROWS], 0.0).then_inc(v_cleared, 1)
                pool.wait_ge(v_cleared, 1)
                nc.gpsimd.memset(v[:, :, :, :, DH:VW], 1.0).then_inc(zeroed, 1)
                nc.gpsimd.memset(feat[:, 0, :, DH + 1:QD], 2.0).then_inc(zeroed, 1)
                nc.gpsimd.memset(feat[:, 1, :, DH:DH + 1], 1.0).then_inc(zeroed, 1)
                pool_square(pool, 0)

                def body(b, i, one_before, two_before, one_after):
                    if one_before:
                        for h in range(H):
                            pool_sum(pool, b - 1, h, 1 - i)
                    if one_after:
                        pool_square(pool, b + 1)
                over_batches(pool, body)
                for h in range(H):
                    pool_sum(pool, END, h, 1)

            @block.vector
            def _(dve):
                dve.wait_ge(zeroed, 4)
                dve_norm(dve, 0)
                dve_features(dve, 0)
                dve_split(dve, 0)
                dve_rows(dve, 0)

                def body(b, i, one_before, two_before, one_after):
                    for h in range(H):
                        if not on_scalar(h):
                            take_distances(dve, b, h)
                        if h == 6 and two_before:
                            dve.wait_ge(res_done, (b - 1) * TB)
                        dve_ratio(dve, b, h, i)
                        if h == 6 and two_before:
                            dve_stats(dve, b - 2)
                        if h == 0:
                            dve_values(dve, b, i)
                            if two_before:
                                dve_copy_o(dve, b - 2)
                        if two_before:
                            if h in (1, 2):
                                dve_normalise(dve, b - 2, h - 1)
                            if h == 5:
                                dve_residual(dve, b - 2)
                        if one_after:
                            if h == 6:
                                dve_norm(dve, b + 1)
                            if h == 10:
                                dve_features(dve, b + 1)
                            if h == 11:
                                dve_split(dve, b + 1)
                            if h == 12:
                                dve_rows(dve, b + 1)
                over_batches(dve, body)
                dve_copy_o(dve, END - 1)
                dve_normalise(dve, END - 1, 0)
                dve_normalise(dve, END - 1, 1)
                dve_residual(dve, END - 1)
                dve_copy_o(dve, END)
                dve_normalise(dve, END, 0)
                dve_normalise(dve, END, 1)
                dve_residual(dve, END)
                dve.wait_ge(res_done, batches * TB)
                dve_stats(dve, END - 1)
                dve_stats(dve, END)


def mlp(nc, io, keep, y_dram, tiles):
    pairs = tiles // (2 * TC)
    chunks = 2 * pairs
    with ExitStack() as stack:
        m = Names(nc, stack)
        xh = m.sb("xh4", [P, 2, TC, P])
        xTs = m.sb("xTs4", [P, 2, CHUNK])
        hidden = m.sb("hidden", [P, 2, WB, CHUNK])
        y = m.sb("y_rows", [P, 2, TC, P])
        w1 = m.sb("w1", [P, WIDTH])
        w2 = m.sb("w2", [P, WB, P])
        x_ps = m.ps("x_ps4", [P, 512])
        h_ps = [m.ps(f"h_ps{i}", [P, 512]) for i in range(4)]
        y_ps = [m.ps(f"y_ps4{i}", [P, 512]) for i in range(2)]

        xh_done, xh_turned, xT_done = m.sem("xh_done4"), m.sem("xh_turned4"), m.sem("xT_done4")
        h_ready, relu_done = m.sem("h_ready"), m.sem("relu_done")
        y_ready, bias_added, y_done = m.sem("y_ready"), m.sem("bias_added"), m.sem("y_done")
        weights_in = m.sem("weights_in4")
        stored = [m.sem(f"y_stored{i}") for i in range(2)]

        with nc.Block() as block:
            @block.tensor
            def _(pe):
                def turn(c, i):
                    pe.wait_ge(xh_done, (c + 1) * TC)
                    after(pe, xT_done, c)
                    for t in range(TC):
                        last = nc.tensor.transpose(x_ps[:, t * P:(t + 1) * P], xh[:, i, t, :], keep.ident)
                    last.then_inc(xh_turned, 1)

                def up(c, i, first):
                    pe.wait_ge(xT_done, c + 1)
                    for w in range(WB):
                        if not (first and i == 0):
                            pe.wait_ge(relu_done, (c - 1) * WB + w + 1)
                        nc.tensor.matmul(h_ps[w][:, :], w1[:, w * P:(w + 1) * P], xTs[:, i, :], start=True,
                                         stop=True).then_inc(h_ready, 1)

                def down(c, i):
                    after(pe, y_done, c - 1)
                    for w in range(WB):
                        pe.wait_ge(relu_done, c * WB + w + 1)
                        for t in range(TC):
                            last = nc.tensor.matmul(y_ps[i][:, t * P:(t + 1) * P], hidden[:, i, w, t * P:(t + 1) * P],
                                                    w2[:, w, :], start=(w == 0 and t == 0),
                                                    stop=(w == WB - 1), skip_group_check=True)
                    last.then_inc(y_ready, 1)

                pe.wait_ge(weights_in, 32)

                def body(p, first):
                    for i in range(2):
                        c = 2 * p + i
                        turn(c, i)
                        if not (first and i == 0):
                            down(c - 1, 1 - i)
                        up(c, i, first)
                over_pairs(pe, pairs, body)
                down(chunks - 1, 1)

            @block.scalar
            def _(act):
                def body(p, first):
                    for i in range(2):
                        c = 2 * p + i
                        act.wait_ge(xh_turned, c + 1)
                        if not first:
                            act.wait_ge(h_ready, (c - 1) * WB)
                        nc.scalar.copy(xTs[:, i, :], x_ps[:, :]).then_inc(xT_done, 1)
                        for w in range(WB):
                            act.wait_ge(h_ready, c * WB + w + 1)
                            if not first:
                                act.wait_ge(y_ready, c - 1)
                            nc.scalar.activation(hidden[:, i, w, :], h_ps[w][:, :], ACT.Relu,
                                                 bias=keep.b1T[:, w:w + 1]).then_inc(relu_done, 1)
                over_pairs(act, pairs, body)

            @block.vector
            def _(dve):
                b2 = keep.biases[:, R_B2:R_B2 + P].unsqueeze(1).to_broadcast([P, TC, P])

                def norm(c, i):
                    after(dve, xh_turned, c - 1)
                    for t in range(TC):
                        n = c * TC + t
                        nc.vector.tensor_scalar(xh[:, i, t, :], keep.x[:, n, :], keep.mv[:, n, 0:1],
                                                keep.rstd_col(n), ALU.subtract, ALU.mult).then_inc(xh_done, 1)

                def finish(p, i, first):
                    c = 2 * p + i
                    if not first and not (isinstance(p, int) and p == 0):
                        dve.wait_ge(stored[i], 16 * p)
                    nc.vector.tensor_tensor(y[:, i, :, :], keep.x[:, bass.ds(c * TC, TC), :], b2,
                                            ALU.add).then_inc(bias_added, 1)
                    dve.wait_ge(bias_added, c + 1)
                    dve.wait_ge(y_ready, c + 1)
                    nc.vector.tensor_tensor(y[:, i, :, :], y_ps[i][:, :].rearrange("p (t d) -> p t d", t=TC),
                                            y[:, i, :, :], ALU.add).then_inc(y_done, 1)

                def body(p, first):
                    norm(2 * p, 0)
                    if not first:
                        finish(p - 1, 1, False)
                    norm(2 * p + 1, 1)
                    finish(p, 0, first)
                over_pairs(dve, pairs, body)
                finish(pairs - 1, 1, pairs == 1)

            @block.sync
            def _(sp):
                sp.dma_start(w1[:, :], io["L1_ffn_w1"]).then_inc(weights_in, 16)
                sp.dma_start(w2[:, :, :], io["L1_ffn_w2"].rearrange("(w p) d -> p w d", p=P)).then_inc(weights_in, 16)
                dram = y_dram.rearrange("b (j p) d -> p (b j) d", p=P)

                def body(p, first):
                    for i in range(2):
                        c = 2 * p + i
                        sp.wait_ge(y_done, c + 1)
                        sp.dma_start(dram[:, bass.ds(c * TC, TC), :], y[:, i, :, :]).then_inc(stored[i], 16)
                over_pairs(sp, pairs, body)
                for i in range(2):
                    sp.wait_ge(stored[i], 16 * pairs)


class Kept:

    def __init__(self, m, tiles):
        self.x = m.sb("x", [P, tiles, P])
        self.mv = m.sb("mv", [P, tiles, 2])
        self.rstd = m.sb("rstd", [P, tiles])
        self.stats = m.sb("stats", [P, tiles, 6])
        self.ident_f = m.sb("ident", [P, P])
        self.ident = self.ident_f[:, :]
        self.ident_bf = m.sb("ident_bf", [P, P], BF16)
        self.biases = m.sb("biases", [P, R_WIDTH])
        self.qkvoT = m.sb("qkvoT", [P, 4, P])
        self.b1T = m.sb("b1T", [P, WB])

    def first_block(self, m):
        self.mask_bf = m.sb("mask_bf", [P, P], BF16)
        self.sel_bf = m.sb("sel_bf", [PARTS * E, PAIRS * P], BF16)
        self.fold = m.sb("fold", [P, H, P])
        self.fold_bias = m.sb("fold_bias", [P, H])
        self.wv0 = m.sb("wv0", [P, H, DH])
        self.wp = m.sb("wp", [P, P])
        self.v0 = m.sb("v0", [P, 2, TB, H, VW])
        self.gateT = m.sb("gateT", [P, BLOCKS, P])
        self.upT = m.sb("upT", [P, BLOCKS, P])
        self.downT = m.sb("downT", [P, BLOCKS, P])
        self.routerT = m.sb("routerT", [P, E])

    def rstd_col(self, t):
        return self.rstd[:, bass.ds(t, 1)] if not isinstance(t, int) else self.rstd[:, t:t + 1]


class Wide:

    def __init__(self, m, tiles):
        self.xT = m.sb("xT_all", [P, tiles // TC, CHUNK])
        self.weight = m.sb("weight", [P, tiles + TC, PARTS * E], BF16)


def two_blocks(nc, io, out, batches, stop=9):
    tiles = batches * TB
    with ExitStack() as stack:
        keep = Kept(Names(nc, stack), tiles)
        with ExitStack() as first:
            keep.first_block(Names(nc, first))
            load_and_fold(nc, io, keep, tiles)
            rstd_of_all(nc, keep, tiles, "attn")
            if stop >= 1:
                causal_attention(nc, keep, batches)
            if stop >= 2:
                wide = Wide(Names(nc, first), tiles)
                rstd_of_all(nc, keep, tiles, "moe")
                route(nc, keep, wide, tiles)
                experts(nc, keep, wide, tiles)
        if stop >= 3:
            rstd_of_all(nc, keep, tiles, "hyp")
            hyperbolic_attention(nc, keep, batches)
        if stop >= 4:
            rstd_of_all(nc, keep, tiles, "mlp")
            mlp(nc, io, keep, out, tiles)
            return
        stored = stack.enter_context(nc.semaphore("stored"))
        with nc.Block() as block:
            @block.sync
            def _(sp):
                y = out.rearrange("b (j p) d -> p (b j) d", p=P)
                sp.dma_start(y, keep.x[:, :, :]).then_inc(stored, 16)
                sp.wait_ge(stored, 16)


def constants():
    import numpy as np

    c = np.zeros((P, C_WIDTH), np.float32)
    c[:, C_IDENT:C_IDENT + P] = np.eye(P)
    c[:, C_MASK:C_MASK + P] = np.triu(np.full((P, P), -3e38), 1)
    for part in range(PARTS):
        for e in range(E):
            c[part * E + e, C_SEL + e * INTER:C_SEL + (e + 1) * INTER] = 1
    return c


_INPUTS = (
    "L0_attn_x", "L0_attn_Wkqv", "L0_attn_bkqv", "L0_attn_Wp", "L0_attn_bp", "L0_ffn_gate_w", "L0_ffn_e_bias",
    "L0_ffn_gate_proj", "L0_ffn_up_proj", "L0_ffn_down_proj", "L0_ffn_shared_gate_w", "L0_ffn_shared_up_w",
    "L0_ffn_shared_down_w", "L1_attn_wq", "L1_attn_wk", "L1_attn_wv", "L1_attn_wo", "L1_ffn_w1", "L1_ffn_b1",
    "L1_ffn_w2", "L1_ffn_b2",
)


def kernel(**inputs):
    import numpy as np
    import concourse.bacc as bacc
    from concourse.bass_utils import run_bass_kernel_spmd

    nc = bacc.Bacc("TRN2", target_bir_lowering=False, num_devices=1)
    arrays = {name: np.ascontiguousarray(inputs[name]) for name in _INPUTS}
    arrays["consts"] = constants()
    io = {name: nc.dram_tensor(name, a.shape, mybir.dt.from_np(a.dtype), kind="ExternalInput").ap()
          for name, a in arrays.items()}
    shape = arrays["L0_attn_x"].shape
    y = nc.dram_tensor("y", shape, F32, kind="ExternalOutput").ap()
    two_blocks(nc, io, y, shape[0])
    r = run_bass_kernel_spmd(nc, [arrays], core_ids=[0])
    return r.results[0]["y"]
```

```python
from contextlib import ExitStack

import concourse.bass as bass
from concourse import mybir

ALU = mybir.AluOpType
ACT = mybir.ActivationFunctionType
F32 = mybir.dt.float32
BF16 = mybir.dt.bfloat16
AX_X = mybir.AxisListType.X

P = 128
H = 16
DH = P // H
N = 256
TB = N // P
VW = DH + 1
LN_EPS = 1e-5

E = 16
INTER = 64
NG = 4
EG = E // NG
TOP_K = 4
TOPK_GROUP = 2
SCALING = 2.5
PAIRS = E // 2
BLOCKS = PAIRS + 1
CHUNK = 512
TC = CHUNK // P
WIDTH = 512
WB = WIDTH // P

PARTS = 3
PAIRINGS = ((0, 1), (0, 2), (0, 0), (1, 0), (2, 0), (1, 1))
QD = DH + 2
BIG = 1e15
TINY = 1e-15
DEN_MIN = 1e-6

C_IDENT, C_MASK, C_SEL, C_WIDTH = 0, P, 2 * P, 2 * P + PAIRS * P
R_BV, R_BP, R_EB, R_B2, R_WIDTH = 0, P, 2 * P, 2 * P + E, 3 * P + E


def after(engine, semaphore, count):
    if isinstance(count, int) and count <= 0:
        return
    engine.wait_ge(semaphore, count)


class Names:

    def __init__(self, nc, stack):
        self.nc, self.stack = nc, stack

    def sb(self, name, shape, dt=F32):
        return self.stack.enter_context(self.nc.sbuf_tensor(name, shape, dt))

    def ps(self, name, shape, dt=F32):
        return self.stack.enter_context(self.nc.psum_tensor(name, shape, dt))

    def sem(self, name):
        return self.stack.enter_context(self.nc.semaphore(name))


def load_and_fold(nc, io, keep, tiles):
    with ExitStack() as stack:
        m = Names(nc, stack)
        consts = m.sb("consts_sb", [P, C_WIDTH])
        wkqv = m.sb("wkqv", [P, H, 2 * P + DH])
        bq_rows = m.sb("bq_rows", [H, P])
        b1_rows = m.sb("b1_rows", [WB, P])
        bias_row = m.sb("bias_row", [1, R_WIDTH])
        ones_row = m.sb("ones_row", [1, P])
        gate_rows = m.sb("gate_rows", [P, BLOCKS, P])
        up_rows = m.sb("up_rows", [P, BLOCKS, P])
        down_cols = m.sb("down_cols", [P, E + 1, INTER])
        router_rows = m.sb("router_rows", [E, P])
        qkvo_rows = m.sb("qkvo_rows", [P, 4, P])
        wqT = m.sb("wqT", [P, H, P])
        wkT = m.sb("wkT", [P, H, P])
        bqT = m.sb("bqT", [P, H])
        bank = [m.ps(f"prep{i}", [P, 512]) for i in range(4)]

        consts_in, weights_in = m.sem("consts_in"), m.sem("weights_in")
        x_in = [m.sem(f"x_in{t}") for t in range(0, tiles, 4 * TB)]
        ones_set = m.sem("ones_set")
        bank_full = [m.sem(f"bank_full{i}") for i in range(4)]
        bank_read = [m.sem(f"bank_read{i}") for i in range(4)]

        jobs = []

        def transposes(sources, dst, parts=P):
            items = [(slice(P * i, P * i + s.shape[0]), s, None) for i, s in enumerate(sources)]
            jobs.append((parts, P * len(sources) if sources[0].shape[0] == P else sources[0].shape[0], items, dst))

        for h0 in range(0, H, 4):
            transposes([wkqv[:, h, P:2 * P] for h in range(h0, h0 + 4)], wqT[:, h0:h0 + 4, :])
            transposes([wkqv[:, h, 0:P] for h in range(h0, h0 + 4)], wkT[:, h0:h0 + 4, :])
        transposes([bq_rows[:, :]], bqT[:, :])
        transposes([b1_rows[:, :]], keep.b1T[:, :])
        for rows, dst in ((gate_rows, keep.gateT), (up_rows, keep.upT)):
            for j0 in (0, 4):
                transposes([rows[:, j, :] for j in range(j0, j0 + 4)], dst[:, j0:j0 + 4, :])
            transposes([rows[0:INTER, PAIRS, :]], dst[:, PAIRS, 0:INTER])
        down = down_cols[:, 0:E, :].rearrange("p (j e) i -> p j (e i)", e=2)
        for j0 in (0, 4):
            transposes([down[:, j, :] for j in range(j0, j0 + 4)], keep.downT[:, j0:j0 + 4, :])
        transposes([down_cols[:, E, :]], keep.downT[0:INTER, PAIRS, :], parts=INTER)
        transposes([router_rows[:, :]], keep.routerT[:, :])
        transposes([qkvo_rows[:, i, :] for i in range(4)], keep.qkvoT[:, :, :])
        for h0 in range(0, H, 4):
            jobs.append((P, 512, [(slice(P * i, P * i + P), wqT[:, h0 + i, :], wkT[:, h0 + i, :])
                                  for i in range(4)], keep.fold[:, h0:h0 + 4, :]))
        jobs.append((P, H, [(slice(h, h + 1), wkT[:, h, :], bqT[:, h:h + 1]) for h in range(H)],
                     keep.fold_bias[:, :]))
        jobs.append((P, R_WIDTH, [(slice(0, R_WIDTH), ones_row[:, :], bias_row[:, :])], keep.biases[:, :]))
        scaled = {id(jobs[i]) for i in range(len(jobs) - 2 - H // 4, len(jobs) - 1)}
        count_at = [[sum(1 for q in range(n + 1) if q % 4 == i) for n in range(len(jobs))] for i in range(4)]
        folds_from = len(jobs) - 2 - H // 4

        with nc.Block() as block:
            @block.sync
            def _(sp):
                sp.dma_start(keep.ident, io["consts"][:, C_IDENT:C_IDENT + P]).then_inc(consts_in, 16)
                sp.dma_start(consts[:, :], io["consts"]).then_inc(consts_in, 16)
                w = io["L0_attn_Wkqv"].rearrange("h d e -> d h e")
                for h0 in range(0, H, 4):
                    sp.dma_start(wkqv[:, h0:h0 + 4, :], w[:, h0:h0 + 4, :]).then_inc(weights_in, 16)
                row = lambda name: io[name].rearrange("(a n) -> a n", a=1)
                loads = [
                    (bq_rows[:, :], io["L0_attn_bkqv"][:, P:2 * P]),
                    (bias_row[:, R_BV:R_BV + P].rearrange("a (h e) -> a h e", h=H),
                     io["L0_attn_bkqv"][:, 2 * P:2 * P + DH].rearrange("(a h) e -> a h e", a=1)),
                    (bias_row[:, R_BP:R_BP + P], row("L0_attn_bp")),
                    (bias_row[:, R_EB:R_EB + E], row("L0_ffn_e_bias")),
                    (bias_row[:, R_B2:R_B2 + P], row("L1_ffn_b2")),
                    (b1_rows[:, :], io["L1_ffn_b1"].rearrange("(w p) -> w p", p=P)),
                    (gate_rows[:, 0:PAIRS, :], 
                     io["L0_ffn_gate_proj"].rearrange("e i d -> (e i) d").rearrange("(j p) d -> p j d", p=P)),
                    (up_rows[:, 0:PAIRS, :],
                     io["L0_ffn_up_proj"].rearrange("e i d -> (e i) d").rearrange("(j p) d -> p j d", p=P)),
                    (gate_rows[0:INTER, PAIRS, :], io["L0_ffn_shared_gate_w"]),
                    (up_rows[0:INTER, PAIRS, :], io["L0_ffn_shared_up_w"]),
                    (down_cols[:, 0:E, :], io["L0_ffn_down_proj"].rearrange("e d i -> d e i")),
                    (down_cols[:, E, :], io["L0_ffn_shared_down_w"]),
                    (router_rows[:, :], io["L0_ffn_gate_w"]),
                    (qkvo_rows[:, 0, :], io["L1_attn_wq"]),
                    (qkvo_rows[:, 1, :], io["L1_attn_wk"]),
                    (qkvo_rows[:, 2, :], io["L1_attn_wv"]),
                    (qkvo_rows[:, 3, :], io["L1_attn_wo"]),
                    (keep.wv0[:, :, :], w[:, :, 2 * P:2 * P + DH]),
                    (keep.wp[:, :], io["L0_attn_Wp"]),
                ]
                for dst, src in loads:
                    sp.dma_start(dst, src).then_inc(weights_in, 16)
                sp.wait_ge(weights_in, 16 * (len(loads) + H // 4))

            @block.gpsimd
            def _(pool):
                nc.gpsimd.memset(ones_row[:, :], 1.0).then_inc(ones_set, 1)
                nc.gpsimd.memset(keep.v0[:, :, :, :, DH:VW], 1.0).then_inc(ones_set, 1)
                nc.gpsimd.memset(keep.gateT[:, PAIRS, INTER:P], 0.0).then_inc(ones_set, 1)
                nc.gpsimd.memset(keep.upT[:, PAIRS, INTER:P], 0.0).then_inc(ones_set, 1)
                nc.gpsimd.memset(keep.downT[:, PAIRS, :], 0.0).then_inc(ones_set, 1)

            @block.tensor
            def _(pe):
                pe.wait_ge(consts_in, 32)
                pe.wait_ge(weights_in, 16 * (H // 4 + 19))
                pe.wait_ge(ones_set, 5)
                for n, (parts, cols, items, dst) in enumerate(jobs):
                    i = n % 4
                    if n == folds_from:
                        for q in range(4):
                            pe.wait_ge(bank_read[q], count_at[q][n - 1])
                    after(pe, bank_read[i], count_at[i][n] - 1)
                    for c, lhsT, rhs in items:
                        if rhs is None:
                            rows = lhsT.shape[0]
                            last = nc.tensor.transpose(bank[i][0:parts, c], lhsT, keep.ident[0:rows, 0:rows])
                        else:
                            last = nc.tensor.matmul(bank[i][0:parts, c], lhsT, rhs, start=True, stop=True)
                    last.then_inc(bank_full[i], 1)

            @block.vector
            def _(dve):
                dve.wait_ge(consts_in, 32)
                nc.vector.tensor_copy(keep.ident_bf[:, :], keep.ident)
                nc.vector.tensor_copy(keep.mask_bf[:, :], consts[:, C_MASK:C_MASK + P])
                nc.vector.tensor_copy(keep.sel_bf[:, :], consts[0:PARTS * E, C_SEL:C_WIDTH])
                for n, (parts, cols, items, dst) in enumerate(jobs):
                    i = n % 4
                    dve.wait_ge(bank_full[i], count_at[i][n])
                    src = bank[i][0:parts, 0:cols]
                    if len(dst.shape) == 3:
                        src = src.rearrange("p (a b) -> p a b", a=dst.shape[1])
                    if folds_from <= n < len(jobs) - 1:
                        ins = nc.vector.tensor_scalar(dst, src, float(P) ** -0.5, None, ALU.mult)
                    else:
                        ins = nc.vector.tensor_copy(dst, src)
                    ins.then_inc(bank_read[i], 1)
                for t in range(tiles):
                    if t % (4 * TB) == 0:
                        dve.wait_ge(x_in[t // (4 * TB)], 16)
                    nc.vector.bn_stats(keep.stats[:, t, :], keep.x[:, t, :])

            @block.scalar
            def _(act):
                x = io["L0_attn_x"].rearrange("b (j p) d -> p (b j) d", p=P)
                for t in range(0, tiles, 4 * TB):
                    act.dma_start(keep.x[:, t:t + 4 * TB, :], x[:, t:t + 4 * TB, :]).then_inc(x_in[t // (4 * TB)], 16)


def rstd_of_all(nc, keep, tiles, name):
    with ExitStack() as stack:
        m = Names(nc, stack)
        std, eps = m.sb(f"std_{name}", [P, tiles]), m.sb(f"eps_{name}", [P, 1])
        eps_set, var_done, std_done = m.sem(f"eps_set_{name}"), m.sem(f"var_done_{name}"), m.sem(f"std_done_{name}")
        with nc.Block() as block:
            @block.scalar
            def _(act):
                act.wait_ge(eps_set, 1)
                act.wait_ge(var_done, tiles)
                nc.scalar.activation(std[:, :], keep.mv[:, :, 1], ACT.Sqrt, bias=eps[:, 0:1]).then_inc(std_done, 1)

            @block.vector
            def _(dve):
                nc.vector.memset(eps[:, :], LN_EPS).then_inc(eps_set, 1)
                for t in range(tiles):
                    nc.vector.bn_aggr(keep.mv[:, t, :], keep.stats[:, t, :]).then_inc(var_done, 1)
                dve.wait_ge(std_done, 1)
                nc.vector.reciprocal(keep.rstd[:, :], std[:, :])


def causal_attention(nc, keep, batches):
    with ExitStack() as stack:
        m = Names(nc, stack)
        xh = m.sb("xh0", [P, TB, P])
        xT = m.sb("xT0", [P, 2, N])
        xTs = m.sb("xTs0", [P, N])
        gT = m.sb("gT", [P, 2, N])
        prob = m.sb("prob", [P, 2, 3 * P])
        probT = m.sb("probT", [P, 2, 3 * P])
        nmax = m.sb("nmax", [P, 2, TB])
        rec = m.sb("rec0", [P, TB, H])
        attn = m.sb("attn0", [P, TB, P])
        attnT = m.sb("attnT0", [P, N])
        g_ps = [m.ps(f"g_ps{i}", [P, 512]) for i in range(2)]
        s_ps = [m.ps(f"s_ps{i}", [P, 512]) for i in range(2)]
        t_ps = [m.ps(f"t_ps{i}", [P, 512]) for i in range(2)]
        o_ps = m.ps("o_ps0", [P, 512])
        misc = m.ps("misc0", [P, 512])
        o_view = o_ps[:, 0:TB * H * VW].rearrange("p (j h e) -> p j h e", j=TB, h=H)

        g_ready, g_copied = m.sem("g_ready"), m.sem("g_copied")
        s_ready, max_done, exp_done = m.sem("s_ready"), m.sem("max_done"), m.sem("exp_done")
        pT_ready, pT_copied, pv_done = m.sem("pT_ready"), m.sem("pT_copied"), m.sem("pv_done")
        xh_done, xh_turned, xTs_done, xT_done = m.sem("xh_done"), m.sem("xh_turned"), m.sem("xTs_done"), m.sem("xT_done")
        v_ready, v_done = m.sem("v_ready"), m.sem("v_done")
        bp_added, rec_done, attn_done = m.sem("bp_added"), m.sem("rec_done"), m.sem("attn_done")
        attn_turned, attnT_done, proj_ready = m.sem("attn_turned"), m.sem("attnT_done"), m.sem("proj_ready")
        res_done = m.sem("res_done")


        def pe_prep_turn(pe, b):
            after(pe, xh_done, (b + 1) * TB)
            after(pe, res_done, (b - 1) * TB)
            after(pe, v_done, b)
            for j in range(TB):
                last = nc.tensor.transpose(misc[:, j * P:(j + 1) * P], xh[:, j, :], keep.ident)
            last.then_inc(xh_turned, 1)

        def pe_prep_values(pe, b):
            pe.wait_ge(xTs_done, b + 1)
            for j in range(TB):
                last = nc.tensor.matmul(misc[:, N + j * P:N + (j + 1) * P], xTs[:, j * P:(j + 1) * P],
                                        keep.wv0[:, :, :], start=True, stop=True)
            last.then_inc(v_ready, 1)

        def act_prep(act, b):
            act.wait_ge(xh_turned, b + 1)
            after(act, v_ready, b)
            after(act, xT_done, b)
            nc.scalar.copy(xTs[:, :], misc[:, 0:N]).then_inc(xTs_done, 1)

        def dve_prep_norm(dve, b):
            after(dve, xh_turned, b)
            for j in range(TB):
                t = b * TB + j
                nc.vector.tensor_scalar(xh[:, j, :], keep.x[:, t, :], keep.mv[:, t, 0:1], keep.rstd_col(t),
                                        ALU.subtract, ALU.mult).then_inc(xh_done, 1)

        def dve_prep_bias(dve, b):
            dve.wait_ge(xh_done, (b + 1) * TB)
            for j in range(TB):
                t = b * TB + j
                nc.vector.tensor_tensor(keep.x[:, t, :], keep.x[:, t, :], keep.biases[:, R_BP:R_BP + P],
                                        ALU.add).then_inc(bp_added, 1)

        def dve_prep_copy(dve, b, half):
            dve.wait_ge(xTs_done, b + 1)
            after(dve, s_ready, (b - 1) * H)
            nc.vector.tensor_copy(xT[:, half, :], xTs[:, :]).then_inc(xT_done, 1)

        def dve_prep_values(dve, b, half):
            dve.wait_ge(v_ready, b + 1)
            after(dve, pv_done, (b - 1) * H)
            for j in range(TB):
                ins = nc.vector.tensor_tensor(
                    keep.v0[:, half, j, :, 0:DH],
                    misc[:, N + j * P:N + (j + 1) * P].rearrange("p (h e) -> p h e", h=H),
                    keep.biases[:, R_BV:R_BV + P].rearrange("p (h e) -> p h e", h=H), ALU.add)
            ins.then_inc(v_done, 1)

        def pe_folded(pe, k, h, i, half):
            after(pe, g_copied, k - 1)
            nc.tensor.matmul(g_ps[i][:, 0:N], keep.fold[:, h, :], xT[:, half, :], start=True,
                             stop=True).then_inc(g_ready, 1)

        def pe_scores(pe, k, i, half):
            pe.wait_ge(g_copied, k + 1)
            after(pe, exp_done, k - 1)
            s = s_ps[i]
            for out, j, keys in ((0, 0, P), (P, 1, 2 * P)):
                nc.tensor.matmul(s[:, out:out + keys], gT[:, i, j * P:(j + 1) * P], xT[:, half, 0:keys],
                                 start=True, stop=False)
                last = nc.tensor.matmul(s[:, out + keys - P:out + keys], keep.ident_bf[:, :], keep.mask_bf[:, :],
                                        start=False, stop=True)
            last.then_inc(s_ready, 1)

        def pe_turn(pe, k, i):
            pe.wait_ge(exp_done, k + 1)
            after(pe, pT_copied, k - 1)
            for c in range(3):
                last = nc.tensor.transpose(t_ps[i][:, c * P:(c + 1) * P], prob[:, i, c * P:(c + 1) * P], keep.ident)
            last.then_inc(pT_ready, 1)

        def pe_values(pe, k, h, i, half):
            pe.wait_ge(pT_copied, k + 1)
            for j, blocks in ((0, ((0, 0),)), (1, ((1, 0), (2, 1)))):
                for n, (c, kj) in enumerate(blocks):
                    last = nc.tensor.matmul(o_view[:, j, h, :], probT[:, i, c * P:(c + 1) * P],
                                            keep.v0[:, half, kj, h, :], start=(n == 0), stop=(n == len(blocks) - 1))
            last.then_inc(pv_done, 1)

        def pe_finish_turn(pe, b, values):
            pe.wait_ge(attn_done, (b + 1) * TB)
            pe.wait_ge(v_done, values)
            for j in range(TB):
                last = nc.tensor.transpose(misc[:, j * P:(j + 1) * P], attn[:, j, :], keep.ident)
            last.then_inc(attn_turned, 1)

        def pe_finish_project(pe, b):
            pe.wait_ge(attnT_done, b + 1)
            for j in range(TB):
                last = nc.tensor.matmul(misc[:, N + j * P:N + (j + 1) * P], attnT[:, j * P:(j + 1) * P],
                                        keep.wp[:, :], start=True, stop=True)
            last.then_inc(proj_ready, 1)

        def act_finish(act, b):
            act.wait_ge(attn_turned, b + 1)
            after(act, proj_ready, b)
            nc.scalar.copy(attnT[:, :], misc[:, 0:N]).then_inc(attnT_done, 1)

        def dve_finish_normalise(dve, b):
            dve.wait_ge(pv_done, (b + 1) * H)
            nc.vector.reciprocal(rec[:, :, :], o_view[:, :, :, DH]).then_inc(rec_done, 1)
            dve.wait_ge(rec_done, b + 1)
            after(dve, attn_turned, b)
            for j in range(TB):
                nc.vector.tensor_tensor(attn[:, j, :].rearrange("p (h e) -> p h e", h=H), o_view[:, j, :, 0:DH],
                                        rec[:, j, :].unsqueeze(2).to_broadcast([P, H, DH]),
                                        ALU.mult).then_inc(attn_done, 1)

        def dve_finish_residual(dve, b):
            dve.wait_ge(proj_ready, b + 1)
            dve.wait_ge(bp_added, (b + 1) * TB)
            for j in range(TB):
                t = b * TB + j
                nc.vector.tensor_tensor(keep.x[:, t, :], misc[:, N + j * P:N + (j + 1) * P], keep.x[:, t, :],
                                        ALU.add).then_inc(res_done, 1)

        def dve_stats(dve, b):
            for j in range(TB):
                nc.vector.bn_stats(keep.stats[:, b * TB + j, :], keep.x[:, b * TB + j, :])

        def act_head(act, k, i):
            act.wait_ge(max_done, k + 1)
            after(act, pT_ready, k - 1)
            nc.scalar.activation(prob[:, i, 0:P], s_ps[i][:, 0:P], ACT.Exp, bias=nmax[:, i, 0:1])
            nc.scalar.activation(prob[:, i, P:3 * P], s_ps[i][:, P:3 * P], ACT.Exp,
                                 bias=nmax[:, i, 1:2]).then_inc(exp_done, 1)

        def act_folded(act, k, h, i):
            act.wait_ge(g_ready, k + 1)
            after(act, s_ready, k - 1)
            nc.scalar.activation(gT[:, i, :], g_ps[i][:, 0:N], ACT.Identity,
                                 bias=keep.fold_bias[:, h:h + 1]).then_inc(g_copied, 1)

        def dve_head_max(dve, k, i):
            dve.wait_ge(s_ready, k + 1)
            after(dve, exp_done, k - 1)
            nc.vector.tensor_reduce(nmax[:, i, 0:1], s_ps[i][:, 0:P], AX_X, ALU.max, negate=True)
            nc.vector.tensor_reduce(nmax[:, i, 1:2], s_ps[i][:, P:3 * P], AX_X, ALU.max,
                                    negate=True).then_inc(max_done, 1)

        def dve_head_turned(dve, k, i):
            dve.wait_ge(pT_ready, k + 1)
            after(dve, pv_done, k - 1)
            nc.vector.tensor_copy(probT[:, i, :], t_ps[i][:, 0:3 * P]).then_inc(pT_copied, 1)

        def over_batches(engine, body):
            body(0, True, False)
            body(1, False, False)
            with engine.Fori(2, batches - 1) as b:
                body(b, False, False)
            body(batches - 1, False, True)

        with nc.Block() as block:
            @block.tensor
            def _(pe):
                pe_prep_turn(pe, 0)
                pe_prep_values(pe, 0)
                pe.wait_ge(xT_done, 1)
                pe_folded(pe, 0, 0, 0, 0)

                def body(b, first, last):
                    half = b % 2
                    for h in range(H):
                        k, i = b * H + h, h % 2
                        if h < H - 1:
                            pe_folded(pe, k + 1, h + 1, 1 - i, half)
                        elif not last:
                            pe.wait_ge(xT_done, b + 2)
                            pe_folded(pe, k + 1, 0, 1 - i, (b + 1) % 2)
                        pe_scores(pe, k, i, half)
                        if h >= 1 or not first:
                            pe_turn(pe, k - 1, 1 - i)
                        if h >= 2:
                            if h == 2:
                                pe.wait_ge(v_done, b + 1)
                                after(pe, attn_done, b * TB)
                            pe_values(pe, k - 2, h - 2, i, half)
                        elif not first:
                            pe_values(pe, k - 2, H + h - 2, i, (b + 1) % 2)
                        if h == 4 and not first:
                            pe_finish_turn(pe, b - 1, b + 1)
                        if h == 6 and not first:
                            pe_finish_project(pe, b - 1)
                        if h == 9 and not last:
                            pe_prep_turn(pe, b + 1)
                        if h == 11 and not last:
                            pe_prep_values(pe, b + 1)

                over_batches(pe, body)
                k = batches * H
                pe_turn(pe, k - 1, 1)
                pe_values(pe, k - 2, H - 2, 0, (batches - 1) % 2)
                pe_values(pe, k - 1, H - 1, 1, (batches - 1) % 2)
                pe_finish_turn(pe, batches - 1, batches)
                pe_finish_project(pe, batches - 1)

            @block.scalar
            def _(act):
                act_prep(act, 0)
                act_folded(act, 0, 0, 0)

                def body(b, first, last):
                    for h in range(H):
                        k, i = b * H + h, h % 2
                        if h < H - 1 or not last:
                            act_folded(act, k + 1, (h + 1) % H, 1 - i)
                        act_head(act, k, i)
                        if h == 4 and not first:
                            act_finish(act, b - 1)
                        if h == 9 and not last:
                            act_prep(act, b + 1)

                over_batches(act, body)
                act_finish(act, batches - 1)

            @block.vector
            def _(dve):
                dve_prep_norm(dve, 0)
                dve_prep_bias(dve, 0)
                dve_prep_copy(dve, 0, 0)
                dve_prep_values(dve, 0, 0)

                def body(b, first, last):
                    for h in range(H):
                        k, i = b * H + h, h % 2
                        if h == 2 and not first:
                            dve_finish_normalise(dve, b - 1)
                        if h == 7 and not first:
                            dve_finish_residual(dve, b - 1)
                        if h == 8 and not last:
                            dve_prep_norm(dve, b + 1)
                        if h == 9 and not last:
                            dve_prep_bias(dve, b + 1)
                        if h == 10 and not last:
                            dve_prep_copy(dve, b + 1, (b + 1) % 2)
                        if h == 12 and not last:
                            dve_prep_values(dve, b + 1, (b + 1) % 2)
                        dve_head_max(dve, k, i)
                        if h == 8 and not first:
                            dve.wait_ge(res_done, b * TB)
                        if h >= 1 or not first:
                            dve_head_turned(dve, k - 1, 1 - i)
                        if h == 8 and not first:
                            dve_stats(dve, b - 1)

                over_batches(dve, body)
                dve_head_turned(dve, batches * H - 1, 1)
                dve_finish_normalise(dve, batches - 1)
                dve_finish_residual(dve, batches - 1)
                dve.wait_ge(res_done, batches * TB)
                dve_stats(dve, batches - 1)


def over_pairs(engine, pairs, body):
    body(0, True)
    if pairs > 1:
        body(1, False)
    if pairs > 2:
        with engine.Fori(2, pairs) as p:
            body(p, False)


def route(nc, keep, wide, tiles):
    pairs = tiles // (2 * TC)
    with ExitStack() as stack:
        m = Names(nc, stack)
        xh = m.sb("xh1", [P, 2, TC, P])
        xTs = m.sb("xTs1", [P, 2, CHUNK])
        logits = m.sb("logits", [P, tiles, E])
        score = m.sb("score", [P, tiles, E])
        choice = m.sb("choice", [P, tiles, E])
        rank = m.sb("rank", [P, tiles, E])
        test = m.sb("test", [P, tiles, E])
        hi2 = m.sb("hi2", [P, tiles, NG, 2])
        sum2 = m.sb("sum2", [P, tiles, NG, 2])
        gscore = m.sb("gscore", [P, tiles, NG])
        grank = m.sb("grank", [P, tiles, NG])
        gtest = m.sb("gtest", [P, tiles, NG])
        total = m.sb("total", [P, tiles])
        inv = m.sb("inv", [P, tiles])
        x_ps = [m.ps(f"x_ps{i}", [P, 512]) for i in range(2)]
        l_ps = [m.ps(f"l_ps{i}", [P, 512]) for i in range(2)]

        xh_done, xh_turned = m.sem("xh_done1"), m.sem("xh_turned1")
        xTs_done, xT_done = m.sem("xTs_done1"), m.sem("xT_done1")
        l_ready, l_copied = m.sem("l_ready"), m.sem("l_copied")
        scored, step = m.sem("scored"), m.sem("route_step")

        with nc.Block() as block:
            @block.tensor
            def _(pe):
                def body(p, first):
                    for i in range(2):
                        c = 2 * p + i
                        pe.wait_ge(xh_done, (c + 1) * TC)
                        if not first:
                            pe.wait_ge(xTs_done, c - 1)
                            pe.wait_ge(xT_done, c - 1)
                        for t in range(TC):
                            last = nc.tensor.transpose(x_ps[i][:, t * P:(t + 1) * P], xh[:, i, t, :], keep.ident)
                        last.then_inc(xh_turned, 1)
                        pe.wait_ge(xTs_done, c + 1)
                        if not first:
                            pe.wait_ge(l_copied, c - 1)
                        for t in range(TC):
                            last = nc.tensor.matmul(l_ps[i][:, t * E:(t + 1) * E], xTs[:, i, t * P:(t + 1) * P],
                                                    keep.routerT[:, :], start=True, stop=True)
                        last.then_inc(l_ready, 1)
                over_pairs(pe, pairs, body)

            @block.scalar
            def _(act):
                def body(p, first):
                    for i in range(2):
                        c = 2 * p + i
                        act.wait_ge(xh_turned, c + 1)
                        if not first:
                            act.wait_ge(l_ready, c - 1)
                        nc.scalar.copy(xTs[:, i, :], x_ps[i][:, :]).then_inc(xTs_done, 1)
                        act.wait_ge(xTs_done, c + 1)
                        nc.scalar.copy(wide.xT[:, c, :], xTs[:, i, :]).then_inc(xT_done, 1)
                over_pairs(act, pairs, body)
                act.wait_ge(l_copied, 2 * pairs)
                nc.scalar.activation(score[:, :, :], logits[:, :, :], ACT.Sigmoid).then_inc(scored, 1)

            @block.vector
            def _(dve):
                def norm(c, i):
                    for t in range(TC):
                        n = c * TC + t
                        nc.vector.tensor_scalar(xh[:, i, t, :], keep.x[:, n, :], keep.mv[:, n, 0:1],
                                                keep.rstd_col(n), ALU.subtract, ALU.mult).then_inc(xh_done, 1)

                def body(p, first):
                    for i in range(2):
                        c = 2 * p + i
                        if not first:
                            dve.wait_ge(xh_turned, c - 1)
                        norm(c, i)
                    for i in range(2):
                        c = 2 * p + i
                        dve.wait_ge(l_ready, c + 1)
                        nc.vector.tensor_copy(logits[:, bass.ds(c * TC, TC), :],
                                              l_ps[i][:, 0:TC * E].rearrange("p (t e) -> p t e", t=TC)
                                              ).then_inc(l_copied, 1)
                over_pairs(dve, pairs, body)

                steps = [0]

                def then(ins):
                    steps[0] += 1
                    ins.then_inc(step, 1)
                    dve.wait_ge(step, steps[0])

                v = nc.vector
                dve.wait_ge(scored, 1)
                bias = keep.biases[:, R_EB:R_EB + E].unsqueeze(1).to_broadcast([P, tiles, E])
                then(v.tensor_tensor(choice[:, :, :], score[:, :, :], bias, ALU.add))
                quad = choice[:, :, :].rearrange("p t (g h a) -> p t g h a", g=NG, h=2)
                flat = lambda ap: ap.rearrange("p t g h -> p (t g h)")
                half = choice[:, :, :].rearrange("p t (q a) -> p (t q) a", a=2)
                hi2f, sum2f = flat(hi2[:, :, :, :]), flat(sum2[:, :, :, :])
                v.tensor_tensor(hi2f, half[:, :, 0], half[:, :, 1], ALU.max)
                then(v.tensor_tensor(sum2f, half[:, :, 0], half[:, :, 1], ALU.add))
                hi2p = hi2[:, :, :, :].rearrange("p t g h -> p (t g) h")
                sum2p = sum2[:, :, :, :].rearrange("p t g h -> p (t g) h")
                gs = gscore[:, :, :].rearrange("p t g -> p (t g)")
                gt = gtest[:, :, :].rearrange("p t g -> p (t g)")
                v.tensor_tensor(gs, hi2p[:, :, 0], hi2p[:, :, 1], ALU.add)
                then(v.tensor_tensor(gt, sum2p[:, :, 0], sum2p[:, :, 1], ALU.max))
                then(v.tensor_tensor(gs, gs, gt, ALU.max))

                def ranks(values, rank, test, width):
                    for e in range(width):
                        ins = v.memset(rank[:, :, e:e + 1], float(width - 1 - e))
                    then(ins)
                    for d in range(1, width):
                        lo, hi = slice(0, width - d), slice(d, width)
                        then(v.tensor_tensor(test[:, :, lo], values[:, :, lo], values[:, :, hi], ALU.is_ge))
                        then(v.tensor_tensor(rank[:, :, lo], rank[:, :, lo], test[:, :, lo], ALU.subtract))
                        then(v.tensor_tensor(rank[:, :, hi], rank[:, :, hi], test[:, :, lo], ALU.add))

                ranks(gscore, grank, gtest, NG)
                then(v.tensor_scalar(gtest[:, :, :], grank[:, :, :], float(TOPK_GROUP), None, ALU.is_lt))
                grouped = choice[:, :, :].rearrange("p t (g a) -> p (t g) a", g=NG)
                then(v.tensor_tensor(grouped, grouped,
                                     gtest[:, :, :].rearrange("p t g -> p (t g)").unsqueeze(2)
                                     .to_broadcast([P, tiles * NG, EG]), ALU.mult))
                ranks(choice, rank, test, E)
                then(v.scalar_tensor_tensor(out=test[:, :, :], in0=rank[:, :, :], scalar=float(TOP_K),
                                            in1=score[:, :, :], op0=ALU.is_lt, op1=ALU.mult))
                then(v.tensor_reduce(total[:, :], test[:, :, :], AX_X, ALU.add))
                then(v.tensor_scalar(total[:, :], total[:, :], 1e-20, None, ALU.add))
                then(v.reciprocal(inv[:, :], total[:, :]))
                then(v.scalar_tensor_tensor(out=rank[:, :, :], in0=test[:, :, :], scalar=SCALING,
                                            in1=inv[:, :].unsqueeze(2).to_broadcast([P, tiles, E]),
                                            op0=ALU.mult, op1=ALU.mult))
                v.memset(wide.weight[:, tiles:tiles + TC, :], 0.0)
                for part in range(PARTS):
                    w = wide.weight[:, 0:tiles, part * E:(part + 1) * E]
                    then(v.tensor_copy(w, rank[:, :, :]))
                    if part < PARTS - 1:
                        then(v.tensor_tensor(rank[:, :, :], rank[:, :, :], w, ALU.subtract))


def experts(nc, keep, wide, tiles):
    pairs = tiles // (2 * TC)
    chunks = 2 * pairs
    with ExitStack() as stack:
        m = Names(nc, stack)
        wst = m.sb("wst", [P, 2, TC, PARTS * E], BF16)
        wT = m.sb("wT", [PARTS * E, 2, CHUNK], BF16)
        act_g = m.sb("act_g", [P, 2, CHUNK])
        gated = m.sb("gated", [P, 2, CHUNK])
        inter = m.sb("inter", [P, 2, CHUNK])
        g_ps = [m.ps(f"eg_ps{i}", [P, 512]) for i in range(2)]
        u_ps = [m.ps(f"eu_ps{i}", [P, 512]) for i in range(2)]
        w_ps = [m.ps(f"ew_ps{i}", [P, 512]) for i in range(2)]
        wT_ps = m.ps("wT_ps", [P, 1024], BF16)
        y_ps = m.ps("y_ps", [P, 512])

        wst_done, w_turned, wT_done = m.sem("wst_done"), m.sem("w_turned"), m.sem("wT_done")
        g_ready, u_ready, w_ready = m.sem("eg_ready"), m.sem("eu_ready"), m.sem("ew_ready")
        silu_done, gated_done, inter_done = m.sem("silu_done"), m.sem("gated_done"), m.sem("inter_done")
        down_done, res_done = m.sem("down_done"), m.sem("res_done2")


        with nc.Block() as block:
            @block.tensor
            def _(pe):
                def weights_staged(c):
                    pe.wait_ge(wst_done, c + 1)
                    after(pe, wT_done, c)

                def turn_weights(i):
                    for t in range(TC):
                        last = nc.tensor.transpose(wT_ps[0:PARTS * E, t * P:(t + 1) * P], wst[:, i, t, :],
                                                   keep.ident_bf[:, :])
                    last.then_inc(w_turned, 1)

                def down(n, j, q, c, first):
                    pe.wait_ge(inter_done, n + 1)
                    if j == 0 and not first:
                        pe.wait_ge(res_done, c)
                    for t in range(TC):
                        last = nc.tensor.matmul(y_ps[:, t * P:(t + 1) * P], inter[:, q, t * P:(t + 1) * P],
                                                keep.downT[:, j, :], start=(j == 0 and t == 0),
                                                stop=(j == BLOCKS - 1), skip_group_check=True)
                    last.then_inc(down_done, 1)

                def body(p, first):
                    for i in range(2):
                        c = 2 * p + i
                        for j in range(BLOCKS):
                            q = (i * BLOCKS + j) % 2
                            n = c * BLOCKS + j
                            x = wide.xT[:, c, :]
                            early = first and i == 0
                            if j == 6:
                                weights_staged(c + 1)
                            if not (early and j < 2):
                                pe.wait_ge(silu_done, n - 1)
                            nc.tensor.matmul(g_ps[q][:, :], keep.gateT[:, j, :], x, start=True,
                                             stop=True).then_inc(g_ready, 1)
                            if j == 6:
                                turn_weights(1 - i)
                            if not (early and j < 2):
                                pe.wait_ge(inter_done, n - 1)
                            nc.tensor.matmul(u_ps[q][:, :], keep.upT[:, j, :], x, start=True,
                                             stop=True).then_inc(u_ready, 1)
                            if j < PAIRS:
                                if j == 0:
                                    pe.wait_ge(wT_done, c + 1)
                                nc.tensor.matmul(w_ps[q][:, :], keep.sel_bf[:, j * P:(j + 1) * P], wT[:, i, :],
                                                 start=True, stop=True).then_inc(w_ready, 1)
                            if j > 0:
                                down(n - 1, j - 1, 1 - q, c, early)
                            elif not early:
                                down(n - 1, BLOCKS - 1, 1 - q, c - 1, False)
                weights_staged(0)
                turn_weights(0)
                over_pairs(pe, pairs, body)
                down(chunks * BLOCKS - 1, BLOCKS - 1, 1, chunks - 1, False)

            @block.scalar
            def _(act):
                def copy_weights(c, i):
                    act.wait_ge(w_turned, c + 1)
                    after(act, w_ready, (c - 1) * PAIRS)
                    nc.scalar.copy(wT[:, i, :], wT_ps[0:PARTS * E, 0:CHUNK]).then_inc(wT_done, 1)

                def body(p, first):
                    for i in range(2):
                        c = 2 * p + i
                        for j in range(BLOCKS):
                            if j == 7:
                                copy_weights(c + 1, 1 - i)
                            q = (i * BLOCKS + j) % 2
                            n = c * BLOCKS + j
                            act.wait_ge(g_ready, n + 1)
                            if not (first and i == 0 and j < 2):
                                act.wait_ge(inter_done, n - 1)
                            nc.scalar.activation(act_g[:, q, :], g_ps[q][:, :], ACT.Silu).then_inc(silu_done, 1)
                copy_weights(0, 0)
                over_pairs(act, pairs, body)

            @block.vector
            def _(dve):
                def stage_weights(c, i):
                    after(dve, w_turned, c - 1)
                    nc.vector.tensor_copy(wst[:, i, :, :], wide.weight[:, bass.ds(c * TC, TC), :]).then_inc(wst_done, 1)

                def residual(c):
                    dve.wait_ge(down_done, (c + 1) * BLOCKS)
                    nc.vector.tensor_tensor(keep.x[:, bass.ds(c * TC, TC), :],
                                            y_ps[:, :].rearrange("p (t d) -> p t d", t=TC),
                                            keep.x[:, bass.ds(c * TC, TC), :], ALU.add).then_inc(res_done, 1)

                def statistics(c):
                    for t in range(TC):
                        nc.vector.bn_stats(keep.stats[:, c * TC + t, :], keep.x[:, c * TC + t, :])

                def body(p, first):
                    for i in range(2):
                        c = 2 * p + i
                        for j in range(BLOCKS):
                            q = (i * BLOCKS + j) % 2
                            n = c * BLOCKS + j
                            if j == 1 and not (first and i == 0):
                                residual(c - 1)
                            if j == 4:
                                stage_weights(c + 1, 1 - i)
                            dve.wait_ge(silu_done, n + 1)
                            dve.wait_ge(u_ready, n + 1)
                            early = first and i == 0 and j < 2
                            if not early:
                                dve.wait_ge(down_done, n - 1)
                            if j == 2 and not (first and i == 0):
                                dve.wait_ge(res_done, c)
                            if j < PAIRS:
                                nc.vector.tensor_tensor(gated[:, q, :], u_ps[q][:, :], act_g[:, q, :],
                                                        ALU.mult).then_inc(gated_done, 1)
                                dve.wait_ge(gated_done, c * PAIRS + j + 1)
                                dve.wait_ge(w_ready, c * PAIRS + j + 1)
                                nc.vector.tensor_tensor(inter[:, q, :], w_ps[q][:, :], gated[:, q, :],
                                                        ALU.mult).then_inc(inter_done, 1)
                            else:
                                nc.vector.tensor_tensor(inter[:, q, :], u_ps[q][:, :], act_g[:, q, :],
                                                        ALU.mult).then_inc(inter_done, 1)
                            if j == 2 and not (first and i == 0):
                                statistics(c - 1)

                stage_weights(0, 0)
                over_pairs(dve, pairs, body)
                residual(chunks - 1)
                dve.wait_ge(res_done, chunks)
                statistics(chunks - 1)


def hyperbolic_attention(nc, keep, batches):
    pairs = batches // 2
    S = len(PAIRINGS)
    GROUP = 4
    GROUPS = H // GROUP
    HP = H // 2
    ROWS = 32
    AHEAD = 2
    IROW = 64
    JH = TB * H
    RW = IROW + 2 * S
    LAG = 5
    MAKE_AT = 2
    FINISH_AT = MAKE_AT + 6
    FEATURES_AT = 9
    SQUARE_AT = 5
    FW = QD + 2
    with ExitStack() as stack:
        m = Names(nc, stack)
        xh = m.sb("xh3", [P, TB, P])
        xTs = m.sb("xTs3", [P, N])
        vst = m.sb("vst", [P, 2, TB, P])
        norm2 = m.sb("norm2", [P, 2, JH])
        gap = m.sb("gap", [P, 2, JH])
        sides = m.sb("sides", [P, 2, 2, JH])
        isides = m.sb("isides", [P, 2, 2, JH])
        signs = m.sb("signs", [P, 2, 2, JH])
        feat = m.sb("feat", [P, 2, JH, FW])
        rest = m.sb("rest", [P, 2, JH, FW])
        square = rest[:, :, :, 0:DH]
        part = [m.sb(f"part{i}", [P, 2, JH, FW], BF16) for i in range(PARTS)]
        rows = m.sb("rows", [P, 2, 2, JH, RW], BF16)
        one = m.sb("one", [P, 1], BF16)
        rowsT = m.sb("rowsT", [RW, 2, GROUPS, GROUP * N], BF16)
        dist = m.sb("dist", [P, AHEAD + 2, 2 * N])
        u = m.sb("u", [P, H, 2 * N])
        w = m.sb("w", [P, 2, H, 2 * N])
        v = m.sb("v3", [P, 2, TB, H, ROWS])
        o = m.sb("o3", [P, GROUPS, N])
        rec = m.sb("rec3", [P, TB, H])
        attn = xh
        attnT = m.sb("attnT3", [P, N])

        d_ps = [m.ps(f"d_ps{i}", [P, 512]) for i in range(2)]
        i_ps = [m.ps(f"i_ps{i}", [P, 512]) for i in range(2)]
        o_ps = [m.ps(f"o_ps3{i}", [P, 512]) for i in range(2)]
        r_ps = m.ps("r_ps", [P, 1024], BF16)
        misc = m.ps("misc3", [P, 512])

        S_ = m.sem
        zeroed, v_cleared = S_("zeroed"), S_("v_cleared")
        xh_done, xh_turned, xT_done = S_("xh_done3"), S_("xh_turned3"), S_("xT_done3")
        qkv_ready, qkv_copied = S_("qkv_ready"), S_("qkv_copied")
        square_done, norm2_done, gap_done = S_("square_done"), S_("norm2_done"), S_("gap_done")
        sides_done, isides_done, masked_done, feat_done = S_("sides_done"), S_("isides_done"), S_("masked_done"), S_("feat_done")
        part_done, rest_done, rows_done = S_("part_done"), S_("rest_done"), S_("rows_done")
        rows_turned, rowsT_done, v_done = S_("rows_turned"), S_("rowsT_done"), S_("v_done3")
        d_ready, i_ready, dist_done = S_("d_ready"), S_("i_ready"), S_("dist_done")
        u_done, prod_done = S_("u_done"), S_("prod_done")
        root_done, sum_done, ln_done, w_done, pv_done = S_("root_done"), S_("sum_done3"), S_("ln_done"), S_("w_done"), S_("pv_done3")
        o_copied, o_turned, rec_done, attn_done = S_("o_copied"), S_("o_turned"), S_("rec_done3"), S_("attn_done3")
        attn_turned, attnT_done, proj_ready = S_("attn_turned3"), S_("attnT_done3"), S_("proj_ready3")
        res_done = S_("res_done3")

        def on_scalar(h):
            return h == 0 or h in (6, 8) or 10 <= h < 15

        def two_heads(buffer, p):
            return buffer[:, 2 * p:2 * p + 2, :].rearrange("p h n -> p (h n)")

        def pe_turn_x(pe, b):
            pe.wait_ge(xh_done, (b + 1) * TB)
            after(pe, res_done, (b - 4) * TB)
            after(pe, qkv_copied, b * TB)
            for j in range(TB):
                last = nc.tensor.transpose(misc[:, j * P:(j + 1) * P], xh[:, j, :], keep.ident)
            last.then_inc(xh_turned, 1)

        def pe_qkv(pe, b, j):
            pe.wait_ge(xT_done, b + 1)
            after(pe, qkv_copied, b * TB + j)
            nc.tensor.matmul(misc[:, 0:3 * P], xTs[:, j * P:(j + 1) * P], keep.qkvoT[:, 0:3, :], start=True,
                             stop=True).then_inc(qkv_ready, 1)

        def pe_turn_rows(pe, b, i, g, side):
            pe.wait_ge(rows_done, b + 1)
            after(pe, rowsT_done, b * 2 * GROUPS + 2 * g + side)
            for q in range(GROUP):
                for j in range(TB):
                    last = nc.tensor.transpose(r_ps[0:RW, (q * TB + j) * P:(q * TB + j + 1) * P],
                                               rows[:, i, side, j * H + g * GROUP + q, :], keep.ident_bf[:, :])
            last.then_inc(rows_turned, 1)

        def pe_pairwise(pe, h, r0, n, ps):
            g, q = h // GROUP, h % GROUP
            for j in range(TB):
                last = nc.tensor.matmul(ps[:, j * N:(j + 1) * N],
                                        rowsT[r0:r0 + n, 1, g, q * N + j * P:q * N + (j + 1) * P],
                                        rowsT[r0:r0 + n, 0, g, q * N:(q + 1) * N], start=True, stop=True)
            return last

        def pe_distances(pe, b, h):
            pe.wait_ge(rowsT_done, b * 2 * GROUPS + 2 * (h // GROUP) + 2)
            after(pe, dist_done, b * H + h - 1)
            pe_pairwise(pe, h, 0, S * QD, d_ps[h % 2]).then_inc(d_ready, 1)

        def pe_inverses(pe, b, h):
            after(pe, u_done, b * H + h - 1)
            pe_pairwise(pe, h, IROW, 2 * S, i_ps[h % 2]).then_inc(i_ready, 1)

        def pe_values(pe, b, h, i):
            pe.wait_ge(w_done, b * HP + h // 2 + 1)
            if h == 0:
                pe.wait_ge(v_done, b + 1)
                after(pe, o_copied, b * 2)
            g, q = h // GROUP, h % GROUP
            out = o_ps[g // 2][q * ROWS:(q + 1) * ROWS, (g % 2) * N:(g % 2 + 1) * N]
            for j in range(TB):
                last = nc.tensor.matmul(out, v[:, i, j, h, :], w[:, i, h, j * N:(j + 1) * N],
                                        start=(j == 0), stop=(j == TB - 1))
            last.then_inc(pv_done, 1)

        def pe_turn_o(pe, b, j, users):
            pe.wait_ge(o_copied, (b + 1) * 2)
            after(pe, qkv_copied, users * TB)
            after(pe, attn_done, b * TB + j)
            for g in range(GROUPS):
                last = nc.tensor.transpose(misc[:, g * P:(g + 1) * P], o[:, g, j * P:(j + 1) * P], keep.ident)
            last.then_inc(o_turned, 1)

        def pe_turn_attn(pe, b):
            pe.wait_ge(attn_done, (b + 1) * TB)
            for j in range(TB):
                last = nc.tensor.transpose(misc[:, j * P:(j + 1) * P], attn[:, j, :], keep.ident)
            last.then_inc(attn_turned, 1)

        def pe_project(pe, b):
            pe.wait_ge(attnT_done, b + 1)
            for j in range(TB):
                last = nc.tensor.matmul(misc[:, N + j * P:N + (j + 1) * P], attnT[:, j * P:(j + 1) * P],
                                        keep.qkvoT[:, 3, :], start=True, stop=True)
            last.then_inc(proj_ready, 1)

        def act_xT(act, b):
            act.wait_ge(xh_turned, b + 1)
            after(act, qkv_ready, b * TB)
            nc.scalar.copy(xTs[:, :], misc[:, 0:N]).then_inc(xT_done, 1)

        def act_qkv(act, b, i, j):
            act.wait_ge(qkv_ready, b * TB + j + 1)
            after(act, part_done, b * PARTS)
            after(act, rest_done, b * (PARTS - 1))
            after(act, square_done, b)
            after(act, v_done, b - 1)
            by_head = lambda n: misc[:, n * P:(n + 1) * P].rearrange("p (h e) -> p h e", h=H)
            nc.scalar.activation(feat[:, 0, j * H:(j + 1) * H, 0:DH], by_head(0), ACT.Copy, scale=-2.0)
            nc.scalar.activation(feat[:, 1, j * H:(j + 1) * H, 0:DH], by_head(1), ACT.Copy, scale=2.0)
            nc.scalar.copy(vst[:, i, j, :], misc[:, 2 * P:3 * P]).then_inc(qkv_copied, 1)

        def rows_turn(b, h, one_after):
            if h % 2:
                return []
            if h < GROUP:
                return [(b, GROUPS - 1, h // 2)]
            return [(b + 1, h // GROUP - 1, h % GROUP // 2)] if one_after else []

        def rows_on_scalar(g, side):
            return g < GROUPS - 1

        def copy_rows(engine, b, g, side):
            engine.wait_ge(rows_turned, b * 2 * GROUPS + 2 * g + side + 1)
            after(engine, i_ready, (b - 1) * H + (g + 1) * GROUP)
            if engine is nc.scalar:
                ins = nc.scalar.copy(rowsT[:, side, g, :], r_ps[0:RW, :])
            else:
                ins = nc.vector.tensor_copy(rowsT[:, side, g, :], r_ps[0:RW, :])
            ins.then_inc(rowsT_done, 1)

        def take_distances(engine, b, h):
            k, i, slot = b * H + h, h % 2, h % (AHEAD + 2)
            engine.wait_ge(d_ready, k + 1)
            after(engine, dist_done, k)
            after(engine, u_done, k - 1 - AHEAD)
            if on_scalar(h):
                ins = nc.scalar.activation(dist[:, slot, :], d_ps[i][:, :], ACT.Relu)
            else:
                ins = nc.vector.tensor_scalar(dist[:, slot, :], d_ps[i][:, :], 0.0, None, ALU.max)
            ins.then_inc(dist_done, 1)

        def act_root(act, b, p, i):
            act.wait_ge(prod_done, b * HP + p + 1)
            nc.scalar.activation(two_heads(w[:, i], p), two_heads(w[:, i], p), ACT.Sqrt).then_inc(root_done, 1)

        def act_ln(act, b, p, i):
            act.wait_ge(sum_done, b * HP + p + 1)
            nc.scalar.activation(two_heads(w[:, i], p), two_heads(w[:, i], p), ACT.Ln, bias=1.0).then_inc(ln_done, 1)

        def act_exp(act, b, p, i):
            act.wait_ge(ln_done, b * HP + p + 1)
            nc.scalar.activation(two_heads(w[:, i], p), two_heads(w[:, i], p), ACT.Exp, scale=-1.0).then_inc(w_done, 1)

        def act_attnT(act, b):
            act.wait_ge(attn_turned, b + 1)
            after(act, proj_ready, b)
            nc.scalar.copy(attnT[:, :], misc[:, 0:N]).then_inc(attnT_done, 1)

        def pool_sum(pool, b, p, i):
            pool.wait_ge(root_done, b * HP + p + 1)
            nc.gpsimd.tensor_tensor(two_heads(w[:, i], p), two_heads(u, p), two_heads(w[:, i], p), ALU.add
                                    ).then_inc(sum_done, 1)

        def pool_square(pool, b):
            pool.wait_ge(qkv_copied, (b + 1) * TB)
            after(pool, part_done, b * PARTS)
            qk = feat[:, :, :, 0:DH].rearrange("p s j e -> p (s j) e")
            nc.gpsimd.tensor_tensor(square.rearrange("p s j e -> p (s j) e"), qk, qk, ALU.mult
                                    ).then_inc(square_done, 1)

        def pool_rows(pool, b, i):
            pool.wait_ge(part_done, (b + 1) * PARTS)
            after(pool, rows_turned, (b - 1) * 2 * GROUPS)
            first = True
            for side in range(2):
                for n in reversed(range(PARTS)):
                    at = [s for s, pair in enumerate(PAIRINGS) if pair[side] == n]
                    step = at[1] - at[0] if len(at) > 1 else 1
                    for r0, width, f0 in ((IROW, 2, QD), (0, QD, 0)):
                        dst = rows[:, i, side, :, r0:r0 + S * width].rearrange("p j (s f) -> p j s f", s=S)
                        dst = dst[:, :, at[0]:at[-1] + 1:step, :]
                        src = part[n][:, side, :, f0:f0 + width].unsqueeze(2).to_broadcast([P, JH, len(at), width])
                        if first:
                            ones = one[:, :].unsqueeze(2).unsqueeze(3).to_broadcast([P, JH, len(at), width])
                            ins = nc.gpsimd.tensor_tensor(dst, src, ones, ALU.mult)
                        else:
                            ins = nc.gpsimd.tensor_scalar(dst, src, 1.0, 0.0, ALU.mult, ALU.add)
                        first = False
            ins.then_inc(rows_done, 1)

        def dve_norm(dve, b):
            after(dve, xh_turned, b)
            after(dve, attn_turned, b - 4)
            for j in range(TB):
                t = b * TB + j
                nc.vector.tensor_scalar(xh[:, j, :], keep.x[:, t, :], keep.mv[:, t, 0:1], keep.rstd_col(t),
                                        ALU.subtract, ALU.mult).then_inc(xh_done, 1)

        def dve_features(dve, b):
            vec = nc.vector
            dve.wait_ge(square_done, b + 1)
            vec.tensor_reduce(norm2[:, :, :].rearrange("p s j -> p (s j)"),
                              square.rearrange("p s j e -> p (s j) e"), AX_X,
                              ALU.add).then_inc(norm2_done, 1)
            dve.wait_ge(norm2_done, b + 1)
            vec.tensor_scalar(gap[:, :, :], norm2[:, :, :], -0.25, 1.0, ALU.mult, ALU.add).then_inc(gap_done, 1)
            vec.tensor_copy(feat[:, 0, :, DH], norm2[:, 0, :])
            vec.tensor_copy(feat[:, 1, :, DH + 1], norm2[:, 1, :])
            dve.wait_ge(gap_done, b + 1)
            vec.tensor_scalar(sides[:, 0], gap[:, :, :], TINY, None, ALU.max)
            vec.tensor_scalar(sides[:, 1], gap[:, :, :], -1.0, TINY, ALU.mult, ALU.max).then_inc(sides_done, 1)
            vec.tensor_scalar(signs[:, 0], gap[:, :, :], 0.0, None, ALU.is_ge)
            vec.tensor_scalar(signs[:, 1], gap[:, :, :], 0.0, None, ALU.is_lt).then_inc(sides_done, 1)
            dve.wait_ge(sides_done, 2 * (b + 1))
            vec.reciprocal(isides[:, :, :, :], sides[:, :, :, :]).then_inc(isides_done, 1)

        def dve_features_end(dve, b):
            vec = nc.vector
            dve.wait_ge(isides_done, b + 1)
            vec.tensor_tensor(isides[:, :, :, :], isides[:, :, :, :], signs[:, :, :, :],
                              ALU.mult).then_inc(masked_done, 1)
            dve.wait_ge(masked_done, b + 1)
            for a in range(2):
                vec.tensor_copy(feat[:, 0, :, QD + a], isides[:, a, 0, :])
                ins = vec.scalar_tensor_tensor(out=feat[:, 1, :, QD + a], in0=signs[:, 1 - a, 1, :], scalar=BIG,
                                               in1=isides[:, a, 1, :], op0=ALU.mult, op1=ALU.add)
            ins.then_inc(feat_done, 1)

        def dve_split(dve, b, n):
            if n == 0:
                dve.wait_ge(feat_done, b + 1)
                after(dve, rows_done, b)
                left = feat
            else:
                left = rest
                dve.wait_ge(rest_done, b * (PARTS - 1) + n)
            nc.vector.tensor_copy(part[n][:, :, :, :], left[:, :, :, :]).then_inc(part_done, 1)
            if n < PARTS - 1:
                dve.wait_ge(part_done, b * PARTS + n + 1)
                nc.vector.tensor_tensor(rest[:, :, :, :], left[:, :, :, :], part[n][:, :, :, :],
                                        ALU.subtract).then_inc(rest_done, 1)

        def dve_values(dve, b, i):
            dve.wait_ge(qkv_copied, (b + 1) * TB)
            after(dve, pv_done, (b - 1) * H)
            for j in range(TB):
                ins = nc.vector.tensor_copy(v[:, i, j, :, 0:DH], vst[:, i, j, :].rearrange("p (h e) -> p h e", h=H))
            ins.then_inc(v_done, 1)

        def dve_ratio(dve, b, h):
            k, q = b * H + h, h % 2
            dve.wait_ge(dist_done, k + 1)
            dve.wait_ge(i_ready, k + 1)
            after(dve, sum_done, (b - 1) * HP + h // 2 + 1)
            nc.vector.scalar_tensor_tensor(out=u[:, h, :], in0=i_ps[q][:, :], scalar=1.0 / DEN_MIN,
                                           in1=dist[:, h % (AHEAD + 2), :], op0=ALU.min, op1=ALU.mult).then_inc(u_done, 1)

        def dve_product(dve, b, p, i):
            dve.wait_ge(u_done, b * H + 2 * p + 2)
            after(dve, pv_done, (b - 2) * H + 2 * p + 2)
            nc.vector.scalar_tensor_tensor(out=two_heads(w[:, i], p), in0=two_heads(u, p), scalar=2.0,
                                           in1=two_heads(u, p), op0=ALU.add, op1=ALU.mult).then_inc(prod_done, 1)

        def dve_copy_o(dve, b):
            dve.wait_ge(pv_done, (b + 1) * H)
            after(dve, o_turned, b * TB)
            for n in range(2):
                nc.vector.tensor_copy(o[:, 2 * n:2 * n + 2, :], o_ps[n][:, :].rearrange("p (g n) -> p g n", g=2)
                                      ).then_inc(o_copied, 1)

        def dve_reciprocals(dve, b, j):
            dve.wait_ge(o_turned, b * TB + j + 1)
            nc.vector.reciprocal(rec[:, j, :], misc[:, :].rearrange("p (h r) -> p h r", h=H)[:, :, DH]
                                 ).then_inc(rec_done, 1)

        def dve_normalise(dve, b, j, users):
            dve.wait_ge(rec_done, b * TB + j + 1)
            dve.wait_ge(xh_turned, users)
            after(dve, attn_turned, b)
            ov = misc[:, :].rearrange("p (h r) -> p h r", h=H)
            nc.vector.tensor_tensor(attn[:, j, :].rearrange("p (h e) -> p h e", h=H), ov[:, :, 0:DH],
                                    rec[:, j, :].unsqueeze(2).to_broadcast([P, H, DH]), ALU.mult
                                    ).then_inc(attn_done, 1)

        def dve_residual(dve, b):
            dve.wait_ge(proj_ready, b + 1)
            for j in range(TB):
                t = b * TB + j
                nc.vector.tensor_tensor(keep.x[:, t, :], misc[:, N + j * P:N + (j + 1) * P], keep.x[:, t, :],
                                        ALU.add).then_inc(res_done, 1)

        def dve_stats(dve, b):
            for j in range(TB):
                nc.vector.bn_stats(keep.stats[:, b * TB + j, :], keep.x[:, b * TB + j, :])

        def ahead(b, h, one_after):
            if h + AHEAD < H:
                return [(b, h + AHEAD)]
            return [(b + 1, h + AHEAD - H)] if one_after else []

        def over_batches(engine, body):
            def turn(p, first, last):
                for i in range(2):
                    b = 2 * p + i
                    body(b, i, not (first and i == 0), not first, not (last and i == 1), not last)
            turn(0, True, pairs == 1)
            if pairs > 2:
                turn(1, False, False)
            if pairs > 3:
                with engine.Fori(2, pairs - 1) as p:
                    turn(p, False, False)
            if pairs > 1:
                turn(pairs - 1, False, True)

        END = batches - 1

        with nc.Block() as block:
            @block.tensor
            def _(pe):
                pe.wait_ge(zeroed, 5)
                for b in range(2):
                    pe_turn_x(pe, b)
                    for j in range(TB):
                        pe_qkv(pe, b, j)
                for g in range(GROUPS - 1):
                    for side in range(2):
                        pe_turn_rows(pe, 0, 0, g, side)
                for h in range(AHEAD):
                    pe_distances(pe, 0, h)

                def body(b, i, one_before, two_before, one_after, two_after):
                    for h in range(H):
                        pe_inverses(pe, b, h)
                        for a in ahead(b, h, one_after):
                            pe_distances(pe, *a)
                        for r in rows_turn(b, h, one_after):
                            pe_turn_rows(pe, r[0], i if h < GROUP else 1 - i, r[1], r[2])
                        if two_after:
                            if h == MAKE_AT:
                                pe_turn_x(pe, b + 2)
                            if h in (MAKE_AT + 2, MAKE_AT + 4):
                                pe_qkv(pe, b + 2, (h - MAKE_AT) // 2 - 1)
                        if two_before:
                            if h in (FINISH_AT, FINISH_AT + 2):
                                pe_turn_o(pe, b - 2, (h - FINISH_AT) // 2, b + 3 if two_after else batches)
                            if h == FINISH_AT + 4:
                                pe_turn_attn(pe, b - 2)
                            if h == FINISH_AT + 6:
                                pe_project(pe, b - 2)
                        if one_before and h >= LAG:
                            pe_values(pe, b - 1, h - LAG, 1 - i)
                    if one_before:
                        for h in range(H - LAG, H):
                            pe_values(pe, b - 1, h, 1 - i)
                over_batches(pe, body)

                def finish(b):
                    after(pe, res_done, b * TB)
                    for j in range(TB):
                        pe_turn_o(pe, b, j, batches)
                    pe_turn_attn(pe, b)
                    pe_project(pe, b)
                finish(END - 1)
                for h in range(H):
                    pe_values(pe, END, h, 1)
                finish(END)

            @block.scalar
            def _(act):
                nc.scalar.preload_act_table_set("natural_log_exp_and_others")
                for b in range(2):
                    act_xT(act, b)
                    for j in range(TB):
                        act_qkv(act, b, b, j)
                for g in range(GROUPS - 1):
                    for side in range(2):
                        copy_rows(act, 0, g, side)
                for h in range(AHEAD):
                    if on_scalar(h):
                        take_distances(act, 0, h)

                def body(b, i, one_before, two_before, one_after, two_after):
                    nc.scalar.preload_act_table_set("natural_log_exp_and_others")
                    for h in range(H):
                        if h % 2 == 1:
                            for r in rows_turn(b, h - 1, one_after):
                                if rows_on_scalar(r[1], r[2]):
                                    copy_rows(act, *r)
                        for a in ahead(b, h, one_after):
                            if on_scalar(a[1]):
                                take_distances(act, *a)
                        if two_after:
                            if h == MAKE_AT + 1:
                                act_xT(act, b + 2)
                            if h in (MAKE_AT + 3, MAKE_AT + 5):
                                act_qkv(act, b + 2, i, (h - MAKE_AT - 3) // 2)
                        if two_before and h == FINISH_AT + 5:
                            act_attnT(act, b - 2)
                        if one_before:
                            if h % 2 == 1:
                                act_ln(act, b - 1, h // 2, 1 - i)
                            elif h > 0:
                                act_exp(act, b - 1, h // 2 - 1, 1 - i)
                    if one_before:
                        act_exp(act, b - 1, HP - 1, 1 - i)
                    for p in range(HP):
                        act_root(act, b, p, i)
                over_batches(act, body)
                nc.scalar.preload_act_table_set("natural_log_exp_and_others")
                act_attnT(act, END - 1)
                for p in range(HP):
                    act_ln(act, END, p, 1)
                    act_exp(act, END, p, 1)
                act_attnT(act, END)

            @block.gpsimd
            def _(pool):
                nc.gpsimd.memset(rows[:, :, :, :, :], 0.0).then_inc(zeroed, 1)
                nc.gpsimd.memset(one[:, :], 1.0).then_inc(zeroed, 1)
                nc.gpsimd.memset(v[:, :, :, :, DH:ROWS], 0.0).then_inc(v_cleared, 1)
                pool.wait_ge(v_cleared, 1)
                nc.gpsimd.memset(v[:, :, :, :, DH:VW], 1.0).then_inc(zeroed, 1)
                nc.gpsimd.memset(feat[:, 0, :, DH + 1:QD], 0.5).then_inc(zeroed, 1)
                nc.gpsimd.memset(feat[:, 1, :, DH:DH + 1], 0.5).then_inc(zeroed, 1)
                pool.wait_ge(zeroed, 5)
                for b in range(2):
                    pool_square(pool, b)
                    pool_rows(pool, b, b)

                def body(b, i, one_before, two_before, one_after, two_after):
                    for p in range(HP):
                        if two_after and p == SQUARE_AT:
                            pool_square(pool, b + 2)
                        if one_before:
                            pool_sum(pool, b - 1, p, 1 - i)
                    if two_after:
                        pool_rows(pool, b + 2, i)
                over_batches(pool, body)
                for p in range(HP):
                    pool_sum(pool, END, p, 1)

            @block.vector
            def _(dve):
                dve.wait_ge(zeroed, 5)

                dve_norm(dve, 0)
                for b in range(2):
                    dve_features(dve, b)
                    dve_features_end(dve, b)
                    for n in range(PARTS):
                        dve_split(dve, b, n)
                    if b == 0:
                        dve_norm(dve, 1)
                for h in range(AHEAD):
                    if not on_scalar(h):
                        take_distances(dve, 0, h)

                def body(b, i, one_before, two_before, one_after, two_after):
                    if two_after:
                        dve_norm(dve, b + 2)
                    dve_values(dve, b, i)
                    if two_before:
                        dve_copy_o(dve, b - 2)
                    for h in range(H):
                        for a in ahead(b, h, one_after):
                            if not on_scalar(a[1]):
                                take_distances(dve, *a)
                        dve_ratio(dve, b, h)
                        if h >= 2 and h % 2 == 0:
                            dve_product(dve, b, h // 2 - 1, i)
                        if h % 2 == 1:
                            for r in rows_turn(b, h - 1, one_after):
                                if not rows_on_scalar(r[1], r[2]):
                                    copy_rows(dve, *r)
                        if two_before:
                            if h in (FINISH_AT + 1, FINISH_AT + 3):
                                dve_reciprocals(dve, b - 2, (h - FINISH_AT) // 2)
                                dve_normalise(dve, b - 2, (h - FINISH_AT) // 2, b + 3 if two_after else batches)
                            if h == FINISH_AT + 7:
                                dve_residual(dve, b - 2)
                        if two_after:
                            if h == FEATURES_AT:
                                dve_features(dve, b + 2)
                            if h == FEATURES_AT + 1:
                                dve_features_end(dve, b + 2)
                            if FEATURES_AT + 2 <= h < FEATURES_AT + 2 + PARTS:
                                dve_split(dve, b + 2, h - FEATURES_AT - 2)
                    if two_before:
                        dve.wait_ge(res_done, (b - 1) * TB)
                    dve_product(dve, b, HP - 1, i)
                    if two_before:
                        dve_stats(dve, b - 2)
                over_batches(dve, body)
                for b in (END - 1, END):
                    dve_copy_o(dve, b)
                    for j in range(TB):
                        dve_reciprocals(dve, b, j)
                        dve_normalise(dve, b, j, batches)
                    dve_residual(dve, b)
                dve.wait_ge(res_done, batches * TB)
                dve_stats(dve, END - 1)
                dve_stats(dve, END)


def mlp(nc, io, keep, y_dram, tiles):
    pairs = tiles // (2 * TC)
    chunks = 2 * pairs
    with ExitStack() as stack:
        m = Names(nc, stack)
        xh = m.sb("xh4", [P, 2, TC, P])
        xTs = m.sb("xTs4", [P, 2, CHUNK])
        hidden = m.sb("hidden", [P, 2, WB, CHUNK])
        y = m.sb("y_rows", [P, 2, TC, P])
        w1 = m.sb("w1", [P, WIDTH])
        w2 = m.sb("w2", [P, WB, P])
        x_ps = m.ps("x_ps4", [P, 512])
        h_ps = [m.ps(f"h_ps{i}", [P, 512]) for i in range(4)]
        y_ps = [m.ps(f"y_ps4{i}", [P, 512]) for i in range(2)]

        xh_done, xh_turned, xT_done = m.sem("xh_done4"), m.sem("xh_turned4"), m.sem("xT_done4")
        h_ready, relu_done = m.sem("h_ready"), m.sem("relu_done")
        y_ready, bias_added, y_done = m.sem("y_ready"), m.sem("bias_added"), m.sem("y_done")
        weights_in = m.sem("weights_in4")
        stored = [m.sem(f"y_stored{i}") for i in range(2)]

        with nc.Block() as block:
            @block.tensor
            def _(pe):
                def turn(c, i):
                    pe.wait_ge(xh_done, (c + 1) * TC)
                    after(pe, xT_done, c)
                    for t in range(TC):
                        last = nc.tensor.transpose(x_ps[:, t * P:(t + 1) * P], xh[:, i, t, :], keep.ident)
                    last.then_inc(xh_turned, 1)

                def up(c, i, first):
                    pe.wait_ge(xT_done, c + 1)
                    for w in range(WB):
                        if not (first and i == 0):
                            pe.wait_ge(relu_done, (c - 1) * WB + w + 1)
                        nc.tensor.matmul(h_ps[w][:, :], w1[:, w * P:(w + 1) * P], xTs[:, i, :], start=True,
                                         stop=True).then_inc(h_ready, 1)

                def down(c, i):
                    after(pe, y_done, c - 1)
                    for w in range(WB):
                        pe.wait_ge(relu_done, c * WB + w + 1)
                        for t in range(TC):
                            last = nc.tensor.matmul(y_ps[i][:, t * P:(t + 1) * P], hidden[:, i, w, t * P:(t + 1) * P],
                                                    w2[:, w, :], start=(w == 0 and t == 0),
                                                    stop=(w == WB - 1), skip_group_check=True)
                    last.then_inc(y_ready, 1)

                pe.wait_ge(weights_in, 32)

                def body(p, first):
                    for i in range(2):
                        c = 2 * p + i
                        turn(c, i)
                        if not (first and i == 0):
                            down(c - 1, 1 - i)
                        up(c, i, first)
                over_pairs(pe, pairs, body)
                down(chunks - 1, 1)

            @block.scalar
            def _(act):
                def body(p, first):
                    for i in range(2):
                        c = 2 * p + i
                        act.wait_ge(xh_turned, c + 1)
                        if not first:
                            act.wait_ge(h_ready, (c - 1) * WB)
                        nc.scalar.copy(xTs[:, i, :], x_ps[:, :]).then_inc(xT_done, 1)
                        for w in range(WB):
                            act.wait_ge(h_ready, c * WB + w + 1)
                            if not first:
                                act.wait_ge(y_ready, c - 1)
                            nc.scalar.activation(hidden[:, i, w, :], h_ps[w][:, :], ACT.Relu,
                                                 bias=keep.b1T[:, w:w + 1]).then_inc(relu_done, 1)
                over_pairs(act, pairs, body)

            @block.vector
            def _(dve):
                b2 = keep.biases[:, R_B2:R_B2 + P].unsqueeze(1).to_broadcast([P, TC, P])

                def norm(c, i):
                    after(dve, xh_turned, c - 1)
                    for t in range(TC):
                        n = c * TC + t
                        nc.vector.tensor_scalar(xh[:, i, t, :], keep.x[:, n, :], keep.mv[:, n, 0:1],
                                                keep.rstd_col(n), ALU.subtract, ALU.mult).then_inc(xh_done, 1)

                def finish(p, i, first):
                    c = 2 * p + i
                    if not first and not (isinstance(p, int) and p == 0):
                        dve.wait_ge(stored[i], 16 * p)
                    nc.vector.tensor_tensor(y[:, i, :, :], keep.x[:, bass.ds(c * TC, TC), :], b2,
                                            ALU.add).then_inc(bias_added, 1)
                    dve.wait_ge(bias_added, c + 1)
                    dve.wait_ge(y_ready, c + 1)
                    nc.vector.tensor_tensor(y[:, i, :, :], y_ps[i][:, :].rearrange("p (t d) -> p t d", t=TC),
                                            y[:, i, :, :], ALU.add).then_inc(y_done, 1)

                def body(p, first):
                    norm(2 * p, 0)
                    if not first:
                        finish(p - 1, 1, False)
                    norm(2 * p + 1, 1)
                    finish(p, 0, first)
                over_pairs(dve, pairs, body)
                finish(pairs - 1, 1, pairs == 1)

            @block.sync
            def _(sp):
                sp.dma_start(w1[:, :], io["L1_ffn_w1"]).then_inc(weights_in, 16)
                sp.dma_start(w2[:, :, :], io["L1_ffn_w2"].rearrange("(w p) d -> p w d", p=P)).then_inc(weights_in, 16)
                dram = y_dram.rearrange("b (j p) d -> p (b j) d", p=P)

                def body(p, first):
                    for i in range(2):
                        c = 2 * p + i
                        sp.wait_ge(y_done, c + 1)
                        sp.dma_start(dram[:, bass.ds(c * TC, TC), :], y[:, i, :, :]).then_inc(stored[i], 16)
                over_pairs(sp, pairs, body)
                for i in range(2):
                    sp.wait_ge(stored[i], 16 * pairs)


class Kept:

    def __init__(self, m, tiles):
        self.x = m.sb("x", [P, tiles, P])
        self.mv = m.sb("mv", [P, tiles, 2])
        self.rstd = m.sb("rstd", [P, tiles])
        self.stats = m.sb("stats", [P, tiles, 6])
        self.ident_f = m.sb("ident", [P, P])
        self.ident = self.ident_f[:, :]
        self.ident_bf = m.sb("ident_bf", [P, P], BF16)
        self.biases = m.sb("biases", [P, R_WIDTH])
        self.qkvoT = m.sb("qkvoT", [P, 4, P])
        self.b1T = m.sb("b1T", [P, WB])

    def first_block(self, m):
        self.mask_bf = m.sb("mask_bf", [P, P], BF16)
        self.sel_bf = m.sb("sel_bf", [PARTS * E, PAIRS * P], BF16)
        self.fold = m.sb("fold", [P, H, P])
        self.fold_bias = m.sb("fold_bias", [P, H])
        self.wv0 = m.sb("wv0", [P, H, DH])
        self.wp = m.sb("wp", [P, P])
        self.v0 = m.sb("v0", [P, 2, TB, H, VW])
        self.gateT = m.sb("gateT", [P, BLOCKS, P])
        self.upT = m.sb("upT", [P, BLOCKS, P])
        self.downT = m.sb("downT", [P, BLOCKS, P])
        self.routerT = m.sb("routerT", [P, E])

    def rstd_col(self, t):
        return self.rstd[:, bass.ds(t, 1)] if not isinstance(t, int) else self.rstd[:, t:t + 1]


class Wide:

    def __init__(self, m, tiles):
        self.xT = m.sb("xT_all", [P, tiles // TC, CHUNK])
        self.weight = m.sb("weight", [P, tiles + TC, PARTS * E], BF16)


def two_blocks(nc, io, out, batches, stop=9):
    tiles = batches * TB
    with ExitStack() as stack:
        keep = Kept(Names(nc, stack), tiles)
        with ExitStack() as first:
            keep.first_block(Names(nc, first))
            load_and_fold(nc, io, keep, tiles)
            rstd_of_all(nc, keep, tiles, "attn")
            if stop >= 1:
                causal_attention(nc, keep, batches)
            if stop >= 2:
                wide = Wide(Names(nc, first), tiles)
                rstd_of_all(nc, keep, tiles, "moe")
                route(nc, keep, wide, tiles)
                experts(nc, keep, wide, tiles)
        if stop >= 3:
            rstd_of_all(nc, keep, tiles, "hyp")
            hyperbolic_attention(nc, keep, batches)
        if stop >= 4:
            rstd_of_all(nc, keep, tiles, "mlp")
            mlp(nc, io, keep, out, tiles)
            return
        stored = stack.enter_context(nc.semaphore("stored"))
        with nc.Block() as block:
            @block.sync
            def _(sp):
                y = out.rearrange("b (j p) d -> p (b j) d", p=P)
                sp.dma_start(y, keep.x[:, :, :]).then_inc(stored, 16)
                sp.wait_ge(stored, 16)


def constants():
    import numpy as np

    c = np.zeros((P, C_WIDTH), np.float32)
    c[:, C_IDENT:C_IDENT + P] = np.eye(P)
    c[:, C_MASK:C_MASK + P] = np.triu(np.full((P, P), -3e38), 1)
    for part in range(PARTS):
        for e in range(E):
            c[part * E + e, C_SEL + e * INTER:C_SEL + (e + 1) * INTER] = 1
    return c


_INPUTS = (
    "L0_attn_x", "L0_attn_Wkqv", "L0_attn_bkqv", "L0_attn_Wp", "L0_attn_bp", "L0_ffn_gate_w", "L0_ffn_e_bias",
    "L0_ffn_gate_proj", "L0_ffn_up_proj", "L0_ffn_down_proj", "L0_ffn_shared_gate_w", "L0_ffn_shared_up_w",
    "L0_ffn_shared_down_w", "L1_attn_wq", "L1_attn_wk", "L1_attn_wv", "L1_attn_wo", "L1_ffn_w1", "L1_ffn_b1",
    "L1_ffn_w2", "L1_ffn_b2",
)


def kernel(**inputs):
    import numpy as np
    import concourse.bacc as bacc
    from concourse.bass_utils import run_bass_kernel_spmd

    nc = bacc.Bacc("TRN2", target_bir_lowering=False, num_devices=1)
    arrays = {name: np.ascontiguousarray(inputs[name]) for name in _INPUTS}
    arrays["consts"] = constants()
    io = {name: nc.dram_tensor(name, a.shape, mybir.dt.from_np(a.dtype), kind="ExternalInput").ap()
          for name, a in arrays.items()}
    shape = arrays["L0_attn_x"].shape
    y = nc.dram_tensor("y", shape, F32, kind="ExternalOutput").ap()
    two_blocks(nc, io, y, shape[0])
    r = run_bass_kernel_spmd(nc, [arrays], core_ids=[0])
    return r.results[0]["y"]
```

```python
from contextlib import ExitStack

import concourse.bass as bass
from concourse import mybir

ALU = mybir.AluOpType
ACT = mybir.ActivationFunctionType
F32 = mybir.dt.float32
BF16 = mybir.dt.bfloat16
F32R = mybir.dt.float32r
AX_X = mybir.AxisListType.X

P = 128
H = 16
DH = P // H
N = 256
TB = N // P
VW = DH + 1
VS = 3 * VW + 1
LN_EPS = 1e-5

E = 16
INTER = 64
NG = 4
EG = E // NG
TOP_K = 4
TOPK_GROUP = 2
SCALING = 2.5
PAIRS = E // 2
BLOCKS = PAIRS + 1
CHUNK = 512
TC = CHUNK // P
WIDTH = 512
WB = WIDTH // P

PARTS = 3
PAIRINGS = ((0, 1), (0, 2), (0, 0), (1, 0), (2, 0), (1, 1))
QD = DH + 2
BIG = 1e15
TINY = 1e-15
DEN_MIN = 1e-6

C_IDENT, C_MASK, C_SEL, C_WIDTH = 0, P, 2 * P, 2 * P + PAIRS * P
R_BV, R_BP, R_EB, R_B2, R_WIDTH = 0, P, 2 * P, 2 * P + E, 3 * P + E


def after(engine, semaphore, count):
    if isinstance(count, int) and count <= 0:
        return
    engine.wait_ge(semaphore, count)


def pe_split_product(nc, out, hi, lo, other_hi, other_lo, stop):
    nc.tensor.matmul(out, hi, other_hi, start=True, stop=False)
    nc.tensor.matmul(out, hi, other_lo, start=False, stop=False)
    return nc.tensor.matmul(out, lo, other_hi, start=False, stop=stop)


class Names:

    def __init__(self, nc, stack):
        self.nc, self.stack = nc, stack

    def sb(self, name, shape, dt=F32):
        return self.stack.enter_context(self.nc.sbuf_tensor(name, shape, dt))

    def ps(self, name, shape, dt=F32):
        return self.stack.enter_context(self.nc.psum_tensor(name, shape, dt))

    def sem(self, name):
        return self.stack.enter_context(self.nc.semaphore(name))


def load_and_fold(nc, io, keep, tiles):
    with ExitStack() as stack:
        m = Names(nc, stack)
        consts = m.sb("consts_sb", [P, C_WIDTH])
        wkqv = m.sb("wkqv", [P, H, 2 * P + DH])
        bq_rows = m.sb("bq_rows", [H, P])
        b1_rows = m.sb("b1_rows", [WB, P])
        bias_row = m.sb("bias_row", [1, R_WIDTH])
        ones_row = m.sb("ones_row", [1, P])
        gate_rows = m.sb("gate_rows", [P, BLOCKS, P])
        up_rows = m.sb("up_rows", [P, BLOCKS, P])
        down_cols = m.sb("down_cols", [P, E + 1, INTER])
        router_rows = m.sb("router_rows", [E, P])
        qkvo_rows = m.sb("qkvo_rows", [P, 4, P])
        wqT = m.sb("wqT", [P, H, P])
        wkT = m.sb("wkT", [P, H, P])
        bqT = m.sb("bqT", [P, H])
        bank = [m.ps(f"prep{i}", [P, 512]) for i in range(4)]

        consts_in, weights_in = m.sem("consts_in"), m.sem("weights_in")
        x_in = [m.sem(f"x_in{t}") for t in range(0, tiles, 4 * TB)]
        ones_set, rounded = m.sem("ones_set"), m.sem("rounded")
        bank_full = [m.sem(f"bank_full{i}") for i in range(4)]
        bank_read = [m.sem(f"bank_read{i}") for i in range(4)]

        jobs = []

        def transposes(sources, dst, parts=P):
            items = [(slice(P * i, P * i + s.shape[0]), s, None) for i, s in enumerate(sources)]
            jobs.append((parts, P * len(sources) if sources[0].shape[0] == P else sources[0].shape[0], items, dst))

        for h0 in range(0, H, 4):
            transposes([wkqv[:, h, P:2 * P] for h in range(h0, h0 + 4)], wqT[:, h0:h0 + 4, :])
            transposes([wkqv[:, h, 0:P] for h in range(h0, h0 + 4)], wkT[:, h0:h0 + 4, :])
        transposes([bq_rows[:, :]], bqT[:, :])
        transposes([b1_rows[:, :]], keep.b1T[:, :])
        for rows, pair in ((gate_rows, keep.gateT), (up_rows, keep.upT)):
            for j0 in (0, 4):
                transposes([rows[:, j, :] for j in range(j0, j0 + 4)], tuple(t[:, j0:j0 + 4, :] for t in pair))
            transposes([rows[0:INTER, PAIRS, :]], tuple(t[:, PAIRS:PAIRS + 1, 0:INTER] for t in pair))
        down = down_cols[:, 0:E, :].rearrange("p (j e) i -> p j (e i)", e=2)
        for j0 in (0, 4):
            transposes([down[:, j, :] for j in range(j0, j0 + 4)], keep.downT[:, j0:j0 + 4, :])
        transposes([down_cols[:, E, :]], keep.downT[0:INTER, PAIRS, :], parts=INTER)
        transposes([router_rows[:, :]], keep.routerT[:, :])
        transposes([qkvo_rows[:, i, :] for i in range(4)], keep.qkvoT[:, :, :])
        for h0 in range(0, H, 4):
            jobs.append((P, 512, [(slice(P * i, P * i + P), wqT[:, h0 + i, :], wkT[:, h0 + i, :])
                                  for i in range(4)], (keep.fold_hi[:, h0:h0 + 4, :], keep.fold_lo[:, h0:h0 + 4, :])))
        jobs.append((P, H, [(slice(h, h + 1), wkT[:, h, :], bqT[:, h:h + 1]) for h in range(H)],
                     keep.fold_bias[:, :]))
        jobs.append((P, R_WIDTH, [(slice(0, R_WIDTH), ones_row[:, :], bias_row[:, :])], keep.biases[:, :]))
        count_at = [[sum(1 for q in range(n + 1) if q % 4 == i) for n in range(len(jobs))] for i in range(4)]
        folds_from = len(jobs) - 2 - H // 4

        with nc.Block() as block:
            @block.sync
            def _(sp):
                sp.dma_start(keep.ident, io["consts"][:, C_IDENT:C_IDENT + P]).then_inc(consts_in, 16)
                sp.dma_start(consts[:, :], io["consts"]).then_inc(consts_in, 16)
                w = io["L0_attn_Wkqv"].rearrange("h d e -> d h e")
                for h0 in range(0, H, 4):
                    sp.dma_start(wkqv[:, h0:h0 + 4, :], w[:, h0:h0 + 4, :]).then_inc(weights_in, 16)
                row = lambda name: io[name].rearrange("(a n) -> a n", a=1)
                loads = [
                    (bq_rows[:, :], io["L0_attn_bkqv"][:, P:2 * P]),
                    (bias_row[:, R_BV:R_BV + P].rearrange("a (h e) -> a h e", h=H),
                     io["L0_attn_bkqv"][:, 2 * P:2 * P + DH].rearrange("(a h) e -> a h e", a=1)),
                    (bias_row[:, R_BP:R_BP + P], row("L0_attn_bp")),
                    (bias_row[:, R_EB:R_EB + E], row("L0_ffn_e_bias")),
                    (bias_row[:, R_B2:R_B2 + P], row("L1_ffn_b2")),
                    (b1_rows[:, :], io["L1_ffn_b1"].rearrange("(w p) -> w p", p=P)),
                    (gate_rows[:, 0:PAIRS, :],
                     io["L0_ffn_gate_proj"].rearrange("e i d -> (e i) d").rearrange("(j p) d -> p j d", p=P)),
                    (up_rows[:, 0:PAIRS, :],
                     io["L0_ffn_up_proj"].rearrange("e i d -> (e i) d").rearrange("(j p) d -> p j d", p=P)),
                    (gate_rows[0:INTER, PAIRS, :], io["L0_ffn_shared_gate_w"]),
                    (up_rows[0:INTER, PAIRS, :], io["L0_ffn_shared_up_w"]),
                    (down_cols[:, 0:E, :], io["L0_ffn_down_proj"].rearrange("e d i -> d e i")),
                    (down_cols[:, E, :], io["L0_ffn_shared_down_w"]),
                    (router_rows[:, :], io["L0_ffn_gate_w"]),
                    (qkvo_rows[:, 0, :], io["L1_attn_wq"]),
                    (qkvo_rows[:, 1, :], io["L1_attn_wk"]),
                    (qkvo_rows[:, 2, :], io["L1_attn_wv"]),
                    (qkvo_rows[:, 3, :], io["L1_attn_wo"]),
                    (keep.wv0[:, :, :], w[:, :, 2 * P:2 * P + DH]),
                    (keep.wp[:, :], io["L0_attn_Wp"]),
                ]
                for dst, src in loads:
                    sp.dma_start(dst, src).then_inc(weights_in, 16)
                sp.wait_ge(weights_in, 16 * (len(loads) + H // 4))

            @block.gpsimd
            def _(pool):
                nc.gpsimd.memset(ones_row[:, :], 1.0).then_inc(ones_set, 1)
                nc.gpsimd.memset(keep.v0[:, :, :, :, VW:VS], 0.0).then_inc(ones_set, 1)
                nc.gpsimd.memset(keep.v0[:, :, :, :, DH:VW], 1.0).then_inc(ones_set, 1)
                for part in keep.gateT + keep.upT:
                    nc.gpsimd.memset(part[:, PAIRS, INTER:P].bitcast(F32), 0.0).then_inc(ones_set, 1)
                nc.gpsimd.memset(keep.downT[:, PAIRS, :], 0.0).then_inc(ones_set, 1)

            @block.tensor
            def _(pe):
                pe.wait_ge(consts_in, 32)
                pe.wait_ge(weights_in, 16 * (H // 4 + 19))
                pe.wait_ge(ones_set, 8)
                for n, (parts, cols, items, dst) in enumerate(jobs):
                    i = n % 4
                    if n == folds_from:
                        for q in range(4):
                            pe.wait_ge(bank_read[q], count_at[q][n - 1])
                    after(pe, bank_read[i], count_at[i][n] - 1)
                    for c, lhsT, rhs in items:
                        if rhs is None:
                            rows = lhsT.shape[0]
                            last = nc.tensor.transpose(bank[i][0:parts, c], lhsT, keep.ident[0:rows, 0:rows])
                        else:
                            last = nc.tensor.matmul(bank[i][0:parts, c], lhsT, rhs, start=True, stop=True)
                    last.then_inc(bank_full[i], 1)

            @block.vector
            def _(dve):
                dve.wait_ge(consts_in, 32)
                nc.vector.tensor_copy(keep.ident_bf[:, :], keep.ident)
                nc.vector.tensor_copy(keep.mask_bf[:, :], consts[:, C_MASK:C_MASK + P])
                nc.vector.tensor_copy(keep.sel_bf[:, :], consts[0:PARTS * E, C_SEL:C_WIDTH])
                split = 0
                for n, (parts, cols, items, dst) in enumerate(jobs):
                    i = n % 4
                    dve.wait_ge(bank_full[i], count_at[i][n])
                    src = bank[i][0:parts, 0:cols]
                    scale = float(P) ** -0.5
                    if isinstance(dst, tuple):
                        hi, lo = dst
                        src = src.rearrange("p (a b) -> p a b", a=hi.shape[1])
                        scale = scale if n >= folds_from else 1.0
                        split += 1
                        dve.wait_ge(rounded, split)
                        ins = nc.vector.scalar_tensor_tensor(out=lo, in0=src, scalar=scale, in1=hi, op0=ALU.mult,
                                                             op1=ALU.subtract)
                    elif n == len(jobs) - 2:
                        ins = nc.vector.tensor_scalar(dst, src, scale, None, ALU.mult)
                    else:
                        if len(dst.shape) == 3:
                            src = src.rearrange("p (a b) -> p a b", a=dst.shape[1])
                        ins = nc.vector.tensor_copy(dst, src)
                    ins.then_inc(bank_read[i], 1)
                for t in range(tiles):
                    if t % (4 * TB) == 0:
                        dve.wait_ge(x_in[t // (4 * TB)], 16)
                    nc.vector.bn_stats(keep.stats[:, t, :], keep.x[:, t, :])

            @block.scalar
            def _(act):
                x = io["L0_attn_x"].rearrange("b (j p) d -> p (b j) d", p=P)
                for t in range(0, tiles, 4 * TB):
                    act.dma_start(keep.x[:, t:t + 4 * TB, :], x[:, t:t + 4 * TB, :]).then_inc(x_in[t // (4 * TB)], 16)
                for n, (parts, cols, items, dst) in enumerate(jobs):
                    if isinstance(dst, tuple):
                        act.wait_ge(bank_full[n % 4], count_at[n % 4][n])
                        src = bank[n % 4][0:parts, 0:cols].rearrange("p (a b) -> p a b", a=dst[0].shape[1])
                        nc.scalar.activation(dst[0], src, ACT.Copy, scale=float(P) ** -0.5 if n >= folds_from else 1.0
                                             ).then_inc(rounded, 1)


def rstd_of_all(nc, keep, tiles, name):
    with ExitStack() as stack:
        m = Names(nc, stack)
        std, eps = m.sb(f"std_{name}", [P, tiles]), m.sb(f"eps_{name}", [P, 1])
        eps_set, var_done, std_done = m.sem(f"eps_set_{name}"), m.sem(f"var_done_{name}"), m.sem(f"std_done_{name}")
        with nc.Block() as block:
            @block.scalar
            def _(act):
                act.wait_ge(eps_set, 1)
                act.wait_ge(var_done, tiles)
                nc.scalar.activation(std[:, :], keep.mv[:, :, 1], ACT.Sqrt, bias=eps[:, 0:1]).then_inc(std_done, 1)

            @block.vector
            def _(dve):
                nc.vector.memset(eps[:, :], LN_EPS).then_inc(eps_set, 1)
                for t in range(tiles):
                    nc.vector.bn_aggr(keep.mv[:, t, :], keep.stats[:, t, :]).then_inc(var_done, 1)
                dve.wait_ge(std_done, 1)
                nc.vector.reciprocal(keep.rstd[:, :], std[:, :])


def causal_attention(nc, keep, batches):
    with ExitStack() as stack:
        m = Names(nc, stack)
        xh = m.sb("xh0", [P, TB, P])
        x_hi = m.sb("x_hi", [P, 2, N], F32R)
        x_lo = m.sb("x_lo", [P, 2, N], F32R)
        x_first = m.sb("x_first", [P, 2, P])
        xTs = m.sb("xTs0", [P, N])
        g_all = m.sb("g_all", [P, 4, N])
        g_hi = m.sb("g_hi", [P, 4, P], F32R)
        g_lo = m.sb("g_lo", [P, 4, P], F32R)
        prob = m.sb("prob", [P, 2, 3 * P])
        pT = [m.sb(f"pT{n}", [P, 4, 3 * P], BF16) for n in range(PARTS)]
        p_rest = m.sb("p_rest", [P, 2, 3 * P])
        vals = m.sb("vals0", [P, TB, H, DH])
        v_rest = m.sb("v_rest", [P, TB, H, DH])
        o_sum = m.sb("o_sum", [P, TB, H, VW])
        nmax = m.sb("nmax", [P, 2, TB])
        rec = m.sb("rec0", [P, TB, H])
        attn = m.sb("attn0", [P, TB, P])
        attnT = m.sb("attnT0", [P, N])
        g_ps = m.ps("g_ps", [P, 512])
        s_ps = [m.ps(f"s_ps{i}", [P, 512]) for i in range(2)]
        t_ps = [m.ps(f"t_ps{i}", [P, 512]) for i in range(2)]
        o_ps = [m.ps(f"o_ps0{j}", [P, 512]) for j in range(TB)]
        misc = m.ps("misc0", [P, 512])
        o_view = [bank[:, 0:H * VS].rearrange("p (h e) -> p h e", h=H) for bank in o_ps]

        g_ready, g_taken, g_rounded = m.sem("g_ready"), m.sem("g_taken"), m.sem("g_rounded")
        g_copied = m.sem("g_copied")
        s_ready, max_done, exp_done = m.sem("s_ready"), m.sem("max_done"), m.sem("exp_done")
        pT_ready, pv_done, x_rounded = m.sem("pT_ready"), m.sem("pv_done"), m.sem("x_rounded")
        pT_done = [m.sem(f"pT{n}_done") for n in range(PARTS)]
        p_rest_done, vals_done, v_part, v_rest_done = m.sem("p_rest_done"), m.sem("vals_done"), m.sem("v_part"), m.sem("v_rest_done")
        o_summed = m.sem("o_summed")
        xh_done, xh_turned, xTs_done, xT_done = m.sem("xh_done"), m.sem("xh_turned"), m.sem("xTs_done"), m.sem("xT_done")
        v_ready, v_done = m.sem("v_ready"), m.sem("v_done")
        bp_added, rec_done, attn_done = m.sem("bp_added"), m.sem("rec_done"), m.sem("attn_done")
        attn_turned, attnT_done, proj_ready = m.sem("attn_turned"), m.sem("attnT_done"), m.sem("proj_ready")
        res_done = m.sem("res_done")


        def pe_prep_turn(pe, b):
            after(pe, xh_done, (b + 1) * TB)
            after(pe, res_done, (b - 1) * TB)
            after(pe, vals_done, b)
            for j in range(TB):
                last = nc.tensor.transpose(misc[:, j * P:(j + 1) * P], xh[:, j, :], keep.ident)
            last.then_inc(xh_turned, 1)

        def pe_prep_values(pe, b):
            pe.wait_ge(xTs_done, b + 1)
            for j in range(TB):
                last = nc.tensor.matmul(misc[:, N + j * P:N + (j + 1) * P], xTs[:, j * P:(j + 1) * P],
                                        keep.wv0[:, :, :], start=True, stop=True)
            last.then_inc(v_ready, 1)

        def act_prep(act, b):
            act.wait_ge(xh_turned, b + 1)
            after(act, v_ready, b)
            after(act, xT_done, b)
            nc.scalar.copy(xTs[:, :], misc[:, 0:N]).then_inc(xTs_done, 1)

        def dve_prep_norm(dve, b):
            after(dve, xh_turned, b)
            for j in range(TB):
                t = b * TB + j
                nc.vector.tensor_scalar(xh[:, j, :], keep.x[:, t, :], keep.mv[:, t, 0:1], keep.rstd_col(t),
                                        ALU.subtract, ALU.mult).then_inc(xh_done, 1)

        def dve_prep_bias(dve, b):
            dve.wait_ge(xh_done, (b + 1) * TB)
            for j in range(TB):
                t = b * TB + j
                nc.vector.tensor_tensor(keep.x[:, t, :], keep.x[:, t, :], keep.biases[:, R_BP:R_BP + P],
                                        ALU.add).then_inc(bp_added, 1)

        def dve_prep_copy(dve, b, half):
            dve.wait_ge(xTs_done, b + 1)
            after(dve, s_ready, (b - 1) * H)
            nc.vector.tensor_copy(x_hi[:, half, :], xTs[:, :]).then_inc(x_rounded, 1)
            nc.vector.tensor_copy(x_first[:, half, :], xTs[:, 0:P])
            dve.wait_ge(x_rounded, b + 1)
            nc.vector.tensor_tensor(x_lo[:, half, :], xTs[:, :], x_hi[:, half, :], ALU.subtract).then_inc(xT_done, 1)

        def dve_prep_values(dve, b, half):
            dve.wait_ge(v_ready, b + 1)
            after(dve, v_done, b)
            nc.vector.tensor_tensor(
                vals[:, :, :, :].rearrange("p j h e -> p j (h e)"),
                misc[:, N:2 * N].rearrange("p (j c) -> p j c", j=TB),
                keep.biases[:, R_BV:R_BV + P].unsqueeze(1).to_broadcast([P, TB, P]), ALU.add).then_inc(vals_done, 1)

        def dve_split_values(dve, b, half):
            dve.wait_ge(vals_done, b + 1)
            after(dve, pv_done, (b - 1) * H)
            at = lambda j, n: keep.v0[:, half, j, :, n * VW:n * VW + DH]
            for j in range(TB):
                nc.vector.tensor_copy(at(j, 0), vals[:, j, :, :]).then_inc(v_part, 1)
            dve.wait_ge(v_part, (2 * b + 1) * TB)
            for j in range(TB):
                nc.vector.tensor_tensor(v_rest[:, j, :, :], vals[:, j, :, :], at(j, 0), ALU.subtract
                                        ).then_inc(v_rest_done, 1)
            dve.wait_ge(v_rest_done, (b + 1) * TB)
            for j in range(TB):
                nc.vector.tensor_copy(at(j, 1), v_rest[:, j, :, :]).then_inc(v_part, 1)
            dve.wait_ge(v_part, (2 * b + 2) * TB)
            for j in range(TB):
                ins = nc.vector.tensor_tensor(at(j, 2), v_rest[:, j, :, :], at(j, 1), ALU.subtract)
            ins.then_inc(v_done, 1)

        def pe_folded(pe, k, h, half):
            after(pe, g_taken, k)
            pe_split_product(nc, g_ps[:, 0:N], keep.fold_hi[:, h, :], keep.fold_lo[:, h, :], x_hi[:, half, :],
                             x_lo[:, half, :], True).then_inc(g_ready, 1)

        def pe_scores(pe, k, i, g, half):
            pe.wait_ge(g_copied, k + 1)
            after(pe, exp_done, k - 1)
            s = s_ps[i]
            nc.tensor.matmul(s[:, 0:P], g_all[:, g, 0:P], x_first[:, half, :], start=True, stop=False)
            nc.tensor.matmul(s[:, 0:P], keep.ident_bf[:, :], keep.mask_bf[:, :], start=False, stop=True)
            pe_split_product(nc, s[:, P:3 * P], g_hi[:, g, :], g_lo[:, g, :], x_hi[:, half, :], x_lo[:, half, :], False)
            last = nc.tensor.matmul(s[:, 2 * P:3 * P], keep.ident_bf[:, :], keep.mask_bf[:, :], start=False, stop=True)
            last.then_inc(s_ready, 1)

        def pe_turn(pe, k, i):
            pe.wait_ge(exp_done, k + 1)
            after(pe, p_rest_done, k - 1)
            for c in range(3):
                last = nc.tensor.transpose(t_ps[i][:, c * P:(c + 1) * P], prob[:, i, c * P:(c + 1) * P], keep.ident)
            last.then_inc(pT_ready, 1)

        def pe_values(pe, k, h, half):
            for done in pT_done:
                pe.wait_ge(done, k + 1)
            for j, blocks in ((0, ((0, 0),)), (1, ((1, 0), (2, 1)))):
                for n, (c, kj) in enumerate(blocks):
                    for part in range(PARTS):
                        last = nc.tensor.matmul(o_view[j][:, h, :], pT[part][:, h % 4, c * P:(c + 1) * P],
                                                keep.v0[:, half, kj, h, :], start=(n == 0 and part == 0),
                                                stop=(n == len(blocks) - 1 and part == PARTS - 1))
            last.then_inc(pv_done, 1)

        def pe_finish_turn(pe, b, values):
            pe.wait_ge(attn_done, (b + 1) * TB)
            pe.wait_ge(vals_done, values)
            for j in range(TB):
                last = nc.tensor.transpose(misc[:, j * P:(j + 1) * P], attn[:, j, :], keep.ident)
            last.then_inc(attn_turned, 1)

        def pe_finish_project(pe, b):
            pe.wait_ge(attnT_done, b + 1)
            for j in range(TB):
                last = nc.tensor.matmul(misc[:, N + j * P:N + (j + 1) * P], attnT[:, j * P:(j + 1) * P],
                                        keep.wp[:, :], start=True, stop=True)
            last.then_inc(proj_ready, 1)

        def act_finish(act, b):
            act.wait_ge(attn_turned, b + 1)
            after(act, proj_ready, b)
            nc.scalar.copy(attnT[:, :], misc[:, 0:N]).then_inc(attnT_done, 1)

        def dve_finish_normalise(dve, b):
            dve.wait_ge(pv_done, (b + 1) * H)
            after(dve, attn_done, b * TB)
            for j in range(TB):
                parts = o_view[j][:, :, 0:PARTS * VW].rearrange("p h (n e) -> p h e n", n=PARTS)
                nc.vector.tensor_reduce(o_sum[:, j, :, :], parts, AX_X, ALU.add).then_inc(o_summed, 1)
            dve.wait_ge(o_summed, (b + 1) * TB)
            nc.vector.reciprocal(rec[:, :, :], o_sum[:, :, :, DH]).then_inc(rec_done, 1)
            dve.wait_ge(rec_done, b + 1)
            after(dve, attn_turned, b)
            for j in range(TB):
                nc.vector.tensor_tensor(attn[:, j, :].rearrange("p (h e) -> p h e", h=H), o_sum[:, j, :, 0:DH],
                                        rec[:, j, :].unsqueeze(2).to_broadcast([P, H, DH]),
                                        ALU.mult).then_inc(attn_done, 1)

        def dve_finish_residual(dve, b):
            dve.wait_ge(proj_ready, b + 1)
            dve.wait_ge(bp_added, (b + 1) * TB)
            for j in range(TB):
                t = b * TB + j
                nc.vector.tensor_tensor(keep.x[:, t, :], misc[:, N + j * P:N + (j + 1) * P], keep.x[:, t, :],
                                        ALU.add).then_inc(res_done, 1)

        def dve_stats(dve, b):
            for j in range(TB):
                nc.vector.bn_stats(keep.stats[:, b * TB + j, :], keep.x[:, b * TB + j, :])

        def act_head(act, k, i):
            act.wait_ge(max_done, k + 1)
            after(act, pT_ready, k - 1)
            nc.scalar.activation(prob[:, i, 0:P], s_ps[i][:, 0:P], ACT.Exp, bias=nmax[:, i, 0:1])
            nc.scalar.activation(prob[:, i, P:3 * P], s_ps[i][:, P:3 * P], ACT.Exp,
                                 bias=nmax[:, i, 1:2]).then_inc(exp_done, 1)

        def act_folded(act, k, h):
            act.wait_ge(g_ready, k + 1)
            after(act, s_ready, k - 3)
            nc.scalar.activation(g_all[:, h % 4, :], g_ps[:, 0:N], ACT.Identity,
                                 bias=keep.fold_bias[:, h:h + 1]).then_inc(g_taken, 1)

        def dve_folded(dve, k, h):
            dve.wait_ge(g_taken, k + 1)
            after(dve, s_ready, k - 3)
            nc.vector.tensor_copy(g_hi[:, h % 4, :], g_all[:, h % 4, P:N]).then_inc(g_rounded, 1)

        def pool_folded(pool, k, h):
            pool.wait_ge(g_rounded, k + 1)
            after(pool, s_ready, k - 3)
            nc.gpsimd.tensor_tensor(g_lo[:, h % 4, :], g_all[:, h % 4, P:N], g_hi[:, h % 4, :], ALU.subtract
                                    ).then_inc(g_copied, 1)

        def dve_head_max(dve, k, i):
            dve.wait_ge(s_ready, k + 1)
            after(dve, exp_done, k - 1)
            nc.vector.tensor_reduce(nmax[:, i, 0:1], s_ps[i][:, 0:P], AX_X, ALU.max, negate=True)
            nc.vector.tensor_reduce(nmax[:, i, 1:2], s_ps[i][:, P:3 * P], AX_X, ALU.max,
                                    negate=True).then_inc(max_done, 1)

        def dve_head_turned(dve, k, i, q):
            dve.wait_ge(pT_done[0], k + 1)
            after(dve, pT_done[2], k - 1)
            nc.vector.tensor_tensor(p_rest[:, i, :], t_ps[i][:, 0:3 * P], pT[0][:, q, :], ALU.subtract
                                    ).then_inc(p_rest_done, 1)

        def act_head_part(act, k, i, q):
            act.wait_ge(pT_ready, k + 1)
            after(act, pv_done, k - 3)
            nc.scalar.copy(pT[0][:, q, :], t_ps[i][:, 0:3 * P]).then_inc(pT_done[0], 1)

        def dve_head_part(dve, k, i, q):
            dve.wait_ge(p_rest_done, k + 1)
            after(dve, pv_done, k - 3)
            nc.vector.tensor_copy(pT[1][:, q, :], p_rest[:, i, :]).then_inc(pT_done[1], 1)

        def pool_head_part(pool, k, i, q):
            pool.wait_ge(pT_done[1], k + 1)
            after(pool, pv_done, k - 3)
            nc.gpsimd.tensor_tensor(pT[2][:, q, :], p_rest[:, i, :], pT[1][:, q, :], ALU.subtract
                                    ).then_inc(pT_done[2], 1)

        def over_batches(engine, body):
            body(0, True, False)
            body(1, False, False)
            with engine.Fori(2, batches - 1) as b:
                body(b, False, False)
            body(batches - 1, False, True)

        with nc.Block() as block:
            @block.tensor
            def _(pe):
                pe_prep_turn(pe, 0)
                pe_prep_values(pe, 0)
                pe.wait_ge(xT_done, 1)
                for h in range(2):
                    pe_folded(pe, h, h, 0)

                def body(b, first, last):
                    half = b % 2
                    for h in range(H):
                        k, i = b * H + h, h % 2
                        if h == 5:
                            pe.wait_ge(v_done, b + 1)
                            after(pe, o_summed, b * TB)
                            pe_values(pe, k - 5, 0, half)
                        pe_scores(pe, k, i, h % 4, half)
                        if h < H - 2:
                            pe_folded(pe, k + 2, h + 2, half)
                        elif not last:
                            pe.wait_ge(xT_done, b + 2)
                            pe_folded(pe, k + 2, h + 2 - H, (b + 1) % 2)
                        if h >= 2 or not first:
                            pe_turn(pe, k - 2, i)
                        if h >= 5:
                            pe_values(pe, k - 4, h - 4, half)
                        elif h < 4 and not first:
                            pe_values(pe, k - 4, H + h - 4, (b + 1) % 2)
                        if h == 5 and not first:
                            pe_finish_turn(pe, b - 1, b + 1)
                        if h == 6 and not first:
                            pe_finish_project(pe, b - 1)
                        if h == 9 and not last:
                            pe_prep_turn(pe, b + 1)
                        if h == 11 and not last:
                            pe_prep_values(pe, b + 1)

                over_batches(pe, body)
                k = batches * H
                pe_turn(pe, k - 2, 0)
                pe_turn(pe, k - 1, 1)
                for n in range(4, 0, -1):
                    pe_values(pe, k - n, H - n, (batches - 1) % 2)
                pe_finish_turn(pe, batches - 1, batches)
                pe_finish_project(pe, batches - 1)

            @block.scalar
            def _(act):
                act_prep(act, 0)
                for h in range(2):
                    act_folded(act, h, h)

                def body(b, first, last):
                    for h in range(H):
                        k, i = b * H + h, h % 2
                        if h < H - 2 or not last:
                            act_folded(act, k + 2, (h + 2) % H)
                        if h >= 2 or not first:
                            act_head_part(act, k - 2, i, (h - 2) % 4)
                        act_head(act, k, i)
                        if h == 5 and not first:
                            act_finish(act, b - 1)
                        if h == 9 and not last:
                            act_prep(act, b + 1)

                over_batches(act, body)
                for i in range(2):
                    act_head_part(act, batches * H - 2 + i, i, 2 + i)
                act_finish(act, batches - 1)

            @block.gpsimd
            def _(pool):
                for h in range(2):
                    pool_folded(pool, h, h)

                def body(b, first, last):
                    for h in range(H):
                        if h < H - 2 or not last:
                            pool_folded(pool, b * H + h + 2, (h + 2) % H)
                        if h >= 2 or not first:
                            pool_head_part(pool, b * H + h - 2, h % 2, (h - 2) % 4)
                over_batches(pool, body)
                for i in range(2):
                    pool_head_part(pool, batches * H - 2 + i, i, 2 + i)

            @block.vector
            def _(dve):
                dve_prep_norm(dve, 0)
                dve_prep_bias(dve, 0)
                dve_prep_copy(dve, 0, 0)
                for h in range(2):
                    dve_folded(dve, h, h)
                dve_prep_values(dve, 0, 0)
                dve_split_values(dve, 0, 0)

                def body(b, first, last):
                    for h in range(H):
                        k, i = b * H + h, h % 2
                        dve_head_max(dve, k, i)
                        if h < H - 2 or not last:
                            dve_folded(dve, k + 2, (h + 2) % H)
                        if h == 8 and not first:
                            dve.wait_ge(res_done, b * TB)
                        if h >= 2 or not first:
                            dve_head_turned(dve, k - 2, i, (h - 2) % 4)
                            dve_head_part(dve, k - 2, i, (h - 2) % 4)
                        if not first:
                            if h == 3:
                                dve_finish_normalise(dve, b - 1)
                            if h == 7:
                                dve_finish_residual(dve, b - 1)
                            if h == 8:
                                dve_stats(dve, b - 1)
                        if not last:
                            if h == 8:
                                dve_prep_norm(dve, b + 1)
                            if h == 9:
                                dve_prep_bias(dve, b + 1)
                            if h == 10:
                                dve_prep_copy(dve, b + 1, (b + 1) % 2)
                            if h == 12:
                                dve_prep_values(dve, b + 1, (b + 1) % 2)
                            if h == 13:
                                dve_split_values(dve, b + 1, (b + 1) % 2)

                over_batches(dve, body)
                for i in range(2):
                    dve_head_turned(dve, batches * H - 2 + i, i, 2 + i)
                    dve_head_part(dve, batches * H - 2 + i, i, 2 + i)
                dve_finish_normalise(dve, batches - 1)
                dve_finish_residual(dve, batches - 1)
                dve.wait_ge(res_done, batches * TB)
                dve_stats(dve, batches - 1)


def over_pairs(engine, pairs, body):
    body(0, True)
    if pairs > 1:
        body(1, False)
    if pairs > 2:
        with engine.Fori(2, pairs) as p:
            body(p, False)


def route(nc, keep, wide, tiles):
    pairs = tiles // (2 * TC)
    with ExitStack() as stack:
        m = Names(nc, stack)
        xh = m.sb("xh1", [P, 2, TC, P])
        xTs = m.sb("xTs1", [P, 2, CHUNK])
        logits = m.sb("logits", [P, tiles, E])
        score = m.sb("score", [P, tiles, E])
        choice = m.sb("choice", [P, tiles, E])
        rank = m.sb("rank", [P, tiles, E])
        test = m.sb("test", [P, tiles, E])
        hi2 = m.sb("hi2", [P, tiles, NG, 2])
        sum2 = m.sb("sum2", [P, tiles, NG, 2])
        gscore = m.sb("gscore", [P, tiles, NG])
        grank = m.sb("grank", [P, tiles, NG])
        gtest = m.sb("gtest", [P, tiles, NG])
        total = m.sb("total", [P, tiles])
        inv = m.sb("inv", [P, tiles])
        x_ps = [m.ps(f"x_ps{i}", [P, 512]) for i in range(2)]
        l_ps = [m.ps(f"l_ps{i}", [P, 512]) for i in range(2)]

        xh_done, xh_turned = m.sem("xh_done1"), m.sem("xh_turned1")
        xTs_done, xT_done = m.sem("xTs_done1"), m.sem("xT_done1")
        l_ready, l_copied = m.sem("l_ready"), m.sem("l_copied")
        scored, step = m.sem("scored"), m.sem("route_step")

        with nc.Block() as block:
            @block.tensor
            def _(pe):
                def body(p, first):
                    for i in range(2):
                        c = 2 * p + i
                        pe.wait_ge(xh_done, (c + 1) * TC)
                        if not first:
                            pe.wait_ge(xTs_done, c - 1)
                            pe.wait_ge(xT_done, c - 1)
                        for t in range(TC):
                            last = nc.tensor.transpose(x_ps[i][:, t * P:(t + 1) * P], xh[:, i, t, :], keep.ident)
                        last.then_inc(xh_turned, 1)
                        pe.wait_ge(xTs_done, c + 1)
                        if not first:
                            pe.wait_ge(l_copied, c - 1)
                        for t in range(TC):
                            last = nc.tensor.matmul(l_ps[i][:, t * E:(t + 1) * E], xTs[:, i, t * P:(t + 1) * P],
                                                    keep.routerT[:, :], start=True, stop=True)
                        last.then_inc(l_ready, 1)
                over_pairs(pe, pairs, body)

            @block.scalar
            def _(act):
                def body(p, first):
                    for i in range(2):
                        c = 2 * p + i
                        act.wait_ge(xh_turned, c + 1)
                        if not first:
                            act.wait_ge(l_ready, c - 1)
                        nc.scalar.copy(xTs[:, i, :], x_ps[i][:, :]).then_inc(xTs_done, 1)
                        act.wait_ge(xTs_done, c + 1)
                        nc.scalar.copy(wide.xT[:, c, :], xTs[:, i, :]).then_inc(xT_done, 1)
                over_pairs(act, pairs, body)
                act.wait_ge(l_copied, 2 * pairs)
                nc.scalar.activation(score[:, :, :], logits[:, :, :], ACT.Sigmoid).then_inc(scored, 1)

            @block.vector
            def _(dve):
                def norm(c, i):
                    for t in range(TC):
                        n = c * TC + t
                        nc.vector.tensor_scalar(xh[:, i, t, :], keep.x[:, n, :], keep.mv[:, n, 0:1],
                                                keep.rstd_col(n), ALU.subtract, ALU.mult).then_inc(xh_done, 1)

                def body(p, first):
                    for i in range(2):
                        c = 2 * p + i
                        if not first:
                            dve.wait_ge(xh_turned, c - 1)
                        norm(c, i)
                    for i in range(2):
                        c = 2 * p + i
                        dve.wait_ge(l_ready, c + 1)
                        nc.vector.tensor_copy(logits[:, bass.ds(c * TC, TC), :],
                                              l_ps[i][:, 0:TC * E].rearrange("p (t e) -> p t e", t=TC)
                                              ).then_inc(l_copied, 1)
                over_pairs(dve, pairs, body)

                steps = [0]

                def then(ins):
                    steps[0] += 1
                    ins.then_inc(step, 1)
                    dve.wait_ge(step, steps[0])

                v = nc.vector
                dve.wait_ge(scored, 1)
                bias = keep.biases[:, R_EB:R_EB + E].unsqueeze(1).to_broadcast([P, tiles, E])
                then(v.tensor_tensor(choice[:, :, :], score[:, :, :], bias, ALU.add))
                quad = choice[:, :, :].rearrange("p t (g h a) -> p t g h a", g=NG, h=2)
                flat = lambda ap: ap.rearrange("p t g h -> p (t g h)")
                half = choice[:, :, :].rearrange("p t (q a) -> p (t q) a", a=2)
                hi2f, sum2f = flat(hi2[:, :, :, :]), flat(sum2[:, :, :, :])
                v.tensor_tensor(hi2f, half[:, :, 0], half[:, :, 1], ALU.max)
                then(v.tensor_tensor(sum2f, half[:, :, 0], half[:, :, 1], ALU.add))
                hi2p = hi2[:, :, :, :].rearrange("p t g h -> p (t g) h")
                sum2p = sum2[:, :, :, :].rearrange("p t g h -> p (t g) h")
                gs = gscore[:, :, :].rearrange("p t g -> p (t g)")
                gt = gtest[:, :, :].rearrange("p t g -> p (t g)")
                v.tensor_tensor(gs, hi2p[:, :, 0], hi2p[:, :, 1], ALU.add)
                then(v.tensor_tensor(gt, sum2p[:, :, 0], sum2p[:, :, 1], ALU.max))
                then(v.tensor_tensor(gs, gs, gt, ALU.max))

                def ranks(values, rank, test, width):
                    for e in range(width):
                        ins = v.memset(rank[:, :, e:e + 1], float(width - 1 - e))
                    then(ins)
                    for d in range(1, width):
                        lo, hi = slice(0, width - d), slice(d, width)
                        then(v.tensor_tensor(test[:, :, lo], values[:, :, lo], values[:, :, hi], ALU.is_ge))
                        then(v.tensor_tensor(rank[:, :, lo], rank[:, :, lo], test[:, :, lo], ALU.subtract))
                        then(v.tensor_tensor(rank[:, :, hi], rank[:, :, hi], test[:, :, lo], ALU.add))

                ranks(gscore, grank, gtest, NG)
                then(v.tensor_scalar(gtest[:, :, :], grank[:, :, :], float(TOPK_GROUP), None, ALU.is_lt))
                grouped = choice[:, :, :].rearrange("p t (g a) -> p (t g) a", g=NG)
                then(v.tensor_tensor(grouped, grouped,
                                     gtest[:, :, :].rearrange("p t g -> p (t g)").unsqueeze(2)
                                     .to_broadcast([P, tiles * NG, EG]), ALU.mult))
                ranks(choice, rank, test, E)
                then(v.scalar_tensor_tensor(out=test[:, :, :], in0=rank[:, :, :], scalar=float(TOP_K),
                                            in1=score[:, :, :], op0=ALU.is_lt, op1=ALU.mult))
                then(v.tensor_reduce(total[:, :], test[:, :, :], AX_X, ALU.add))
                then(v.tensor_scalar(total[:, :], total[:, :], 1e-20, None, ALU.add))
                then(v.reciprocal(inv[:, :], total[:, :]))
                then(v.scalar_tensor_tensor(out=rank[:, :, :], in0=test[:, :, :], scalar=SCALING,
                                            in1=inv[:, :].unsqueeze(2).to_broadcast([P, tiles, E]),
                                            op0=ALU.mult, op1=ALU.mult))
                v.memset(wide.weight[:, tiles:tiles + TC, :], 0.0)
                v.memset(wide.xT[:, tiles // TC, :], 0.0)
                for part in range(PARTS):
                    w = wide.weight[:, 0:tiles, part * E:(part + 1) * E]
                    then(v.tensor_copy(w, rank[:, :, :]))
                    if part < PARTS - 1:
                        then(v.tensor_tensor(rank[:, :, :], rank[:, :, :], w, ALU.subtract))


def experts(nc, keep, wide, tiles):
    pairs = tiles // (2 * TC)
    chunks = 2 * pairs
    with ExitStack() as stack:
        m = Names(nc, stack)
        wst = m.sb("wst", [P, 2, TC, PARTS * E], BF16)
        wT = m.sb("wT", [PARTS * E, 2, CHUNK], BF16)
        x_hi = m.sb("x_hi2", [P, 2, CHUNK], F32R)
        x_lo = m.sb("x_lo2", [P, 2, CHUNK], F32R)
        act_g = m.sb("act_g", [P, 2, CHUNK])
        gated = m.sb("gated", [P, 2, CHUNK])
        inter = m.sb("inter", [P, 2, CHUNK])
        g_ps = [m.ps(f"eg_ps{i}", [P, 512]) for i in range(2)]
        u_ps = [m.ps(f"eu_ps{i}", [P, 512]) for i in range(2)]
        w_ps = [m.ps(f"ew_ps{i}", [P, 512]) for i in range(2)]
        wT_ps = m.ps("wT_ps", [P, 1024], BF16)
        y_ps = m.ps("y_ps", [P, 512])

        x_rounded, x_split = m.sem("x_rounded2"), m.sem("x_split")
        wst_done, w_turned, wT_done = m.sem("wst_done"), m.sem("w_turned"), m.sem("wT_done")
        g_ready, u_ready, w_ready = m.sem("eg_ready"), m.sem("eu_ready"), m.sem("ew_ready")
        silu_done, gated_done, inter_done = m.sem("silu_done"), m.sem("gated_done"), m.sem("inter_done")
        down_done, res_done = m.sem("down_done"), m.sem("res_done2")


        with nc.Block() as block:
            @block.tensor
            def _(pe):
                def weights_staged(c):
                    pe.wait_ge(wst_done, c + 1)
                    after(pe, wT_done, c)

                def turn_weights(i):
                    for t in range(TC):
                        last = nc.tensor.transpose(wT_ps[0:PARTS * E, t * P:(t + 1) * P], wst[:, i, t, :],
                                                   keep.ident_bf[:, :])
                    last.then_inc(w_turned, 1)

                def down(n, j, q, c, first):
                    pe.wait_ge(inter_done, n + 1)
                    if j == 0 and not first:
                        pe.wait_ge(res_done, c)
                    for t in range(TC):
                        last = nc.tensor.matmul(y_ps[:, t * P:(t + 1) * P], inter[:, q, t * P:(t + 1) * P],
                                                keep.downT[:, j, :], start=(j == 0 and t == 0),
                                                stop=(j == BLOCKS - 1), skip_group_check=True)
                    last.then_inc(down_done, 1)

                def body(p, first):
                    for i in range(2):
                        c = 2 * p + i
                        for j in range(BLOCKS):
                            q = (i * BLOCKS + j) % 2
                            n = c * BLOCKS + j
                            early = first and i == 0
                            if j == 6:
                                weights_staged(c + 1)
                            if not (early and j < 2):
                                pe.wait_ge(silu_done, n - 1)
                            if j == 0:
                                pe.wait_ge(x_split, c + 1)
                            pe_split_product(nc, g_ps[q][:, :], keep.gateT[0][:, j, :], keep.gateT[1][:, j, :],
                                             x_hi[:, i, :], x_lo[:, i, :], True).then_inc(g_ready, 1)
                            if j == 6:
                                turn_weights(1 - i)
                            if not (early and j < 2):
                                pe.wait_ge(inter_done, n - 1)
                            pe_split_product(nc, u_ps[q][:, :], keep.upT[0][:, j, :], keep.upT[1][:, j, :],
                                             x_hi[:, i, :], x_lo[:, i, :], True).then_inc(u_ready, 1)
                            if j < PAIRS:
                                if j == 0:
                                    pe.wait_ge(wT_done, c + 1)
                                nc.tensor.matmul(w_ps[q][:, :], keep.sel_bf[:, j * P:(j + 1) * P], wT[:, i, :],
                                                 start=True, stop=True).then_inc(w_ready, 1)
                            if j > 0:
                                down(n - 1, j - 1, 1 - q, c, early)
                            elif not early:
                                down(n - 1, BLOCKS - 1, 1 - q, c - 1, False)
                weights_staged(0)
                turn_weights(0)
                over_pairs(pe, pairs, body)
                down(chunks * BLOCKS - 1, BLOCKS - 1, 1, chunks - 1, False)

            @block.scalar
            def _(act):
                def copy_weights(c, i):
                    act.wait_ge(w_turned, c + 1)
                    after(act, w_ready, (c - 1) * PAIRS)
                    nc.scalar.copy(wT[:, i, :], wT_ps[0:PARTS * E, 0:CHUNK]).then_inc(wT_done, 1)

                def body(p, first):
                    for i in range(2):
                        c = 2 * p + i
                        for j in range(BLOCKS):
                            if j == 7:
                                copy_weights(c + 1, 1 - i)
                            q = (i * BLOCKS + j) % 2
                            n = c * BLOCKS + j
                            act.wait_ge(g_ready, n + 1)
                            if not (first and i == 0 and j < 2):
                                act.wait_ge(inter_done, n - 1)
                            nc.scalar.activation(act_g[:, q, :], g_ps[q][:, :], ACT.Silu).then_inc(silu_done, 1)
                copy_weights(0, 0)
                over_pairs(act, pairs, body)

            @block.vector
            def _(dve):
                def stage_weights(c, i):
                    after(dve, w_turned, c - 1)
                    nc.vector.tensor_copy(wst[:, i, :, :], wide.weight[:, bass.ds(c * TC, TC), :]).then_inc(wst_done, 1)

                def split_x(c, i):
                    after(dve, u_ready, (c - 1) * BLOCKS)
                    nc.vector.tensor_copy(x_hi[:, i, :], wide.xT[:, c, :]).then_inc(x_rounded, 1)
                    dve.wait_ge(x_rounded, c + 1)
                    nc.vector.tensor_tensor(x_lo[:, i, :], wide.xT[:, c, :], x_hi[:, i, :], ALU.subtract
                                            ).then_inc(x_split, 1)

                def residual(c):
                    dve.wait_ge(down_done, (c + 1) * BLOCKS)
                    nc.vector.tensor_tensor(keep.x[:, bass.ds(c * TC, TC), :],
                                            y_ps[:, :].rearrange("p (t d) -> p t d", t=TC),
                                            keep.x[:, bass.ds(c * TC, TC), :], ALU.add).then_inc(res_done, 1)

                def statistics(c):
                    for t in range(TC):
                        nc.vector.bn_stats(keep.stats[:, c * TC + t, :], keep.x[:, c * TC + t, :])

                def body(p, first):
                    for i in range(2):
                        c = 2 * p + i
                        for j in range(BLOCKS):
                            q = (i * BLOCKS + j) % 2
                            n = c * BLOCKS + j
                            if j == 1 and not (first and i == 0):
                                residual(c - 1)
                            if j == 4:
                                stage_weights(c + 1, 1 - i)
                            if j == 5:
                                split_x(c + 1, 1 - i)
                            dve.wait_ge(silu_done, n + 1)
                            dve.wait_ge(u_ready, n + 1)
                            early = first and i == 0 and j < 2
                            if not early:
                                dve.wait_ge(down_done, n - 1)
                            if j == 2 and not (first and i == 0):
                                dve.wait_ge(res_done, c)
                            if j < PAIRS:
                                nc.vector.tensor_tensor(gated[:, q, :], u_ps[q][:, :], act_g[:, q, :],
                                                        ALU.mult).then_inc(gated_done, 1)
                                dve.wait_ge(gated_done, c * PAIRS + j + 1)
                                dve.wait_ge(w_ready, c * PAIRS + j + 1)
                                nc.vector.tensor_tensor(inter[:, q, :], w_ps[q][:, :], gated[:, q, :],
                                                        ALU.mult).then_inc(inter_done, 1)
                            else:
                                nc.vector.tensor_tensor(inter[:, q, :], u_ps[q][:, :], act_g[:, q, :],
                                                        ALU.mult).then_inc(inter_done, 1)
                            if j == 2 and not (first and i == 0):
                                statistics(c - 1)

                split_x(0, 0)
                stage_weights(0, 0)
                over_pairs(dve, pairs, body)
                residual(chunks - 1)
                dve.wait_ge(res_done, chunks)
                statistics(chunks - 1)


def hyperbolic_attention(nc, keep, batches):
    pairs = batches // 2
    S = len(PAIRINGS)
    GROUP = 4
    GROUPS = H // GROUP
    HP = H // 2
    ROWS = 32
    AHEAD = 2
    IROW = 64
    JH = TB * H
    RW = IROW + 2 * S
    LAG = 5
    MAKE_AT = 1
    FINISH_AT = 8
    FEATURES_AT = 8
    SPLITS_AT = (10, 11, 13)
    SQUARE_AT = 5
    FW = QD + 2
    with ExitStack() as stack:
        m = Names(nc, stack)
        xh = m.sb("xh3", [P, TB, P])
        xTs = m.sb("xTs3", [P, N])
        vst = m.sb("vst", [P, 2, TB, P])
        norm2 = m.sb("norm2", [P, 2, JH])
        gap = m.sb("gap", [P, 2, JH])
        sides = m.sb("sides", [P, 2, 2, JH])
        isides = m.sb("isides", [P, 2, 2, JH])
        signs = m.sb("signs", [P, 2, 2, JH])
        feat = m.sb("feat", [P, 2, JH, FW])
        rest = m.sb("rest", [P, 2, JH, FW])
        square = rest[:, :, :, 0:DH]
        part = [m.sb(f"part{i}", [P, 2, JH, FW], BF16) for i in range(PARTS)]
        rows = m.sb("rows", [P, 2, 2, JH, RW], BF16)
        one = m.sb("one", [P, 1], BF16)
        rowsT = m.sb("rowsT", [RW, 2, GROUPS, GROUP * N], BF16)
        dist = m.sb("dist", [P, AHEAD + 2, 2 * N])
        u = m.sb("u", [P, H, 2 * N])
        w = m.sb("w", [P, 2, H, 2 * N])
        v = m.sb("v3", [P, 2, TB, H, ROWS])
        o = m.sb("o3", [P, GROUPS, N])
        rec = m.sb("rec3", [P, TB, H])
        attn = xh
        attnT = m.sb("attnT3", [P, N])

        d_ps = [m.ps(f"d_ps{i}", [P, 512]) for i in range(2)]
        i_ps = [m.ps(f"i_ps{i}", [P, 512]) for i in range(2)]
        o_ps = [m.ps(f"o_ps3{i}", [P, 512]) for i in range(2)]
        r_ps = m.ps("r_ps", [P, 1024], BF16)
        misc = m.ps("misc3", [P, 512])

        S_ = m.sem
        zeroed, v_cleared = S_("zeroed"), S_("v_cleared")
        xh_done, xh_turned, xT_done = S_("xh_done3"), S_("xh_turned3"), S_("xT_done3")
        qkv_ready, qkv_copied = S_("qkv_ready"), S_("qkv_copied")
        square_done, norm2_done, gap_done = S_("square_done"), S_("norm2_done"), S_("gap_done")
        sides_done, isides_done, masked_done, feat_done = S_("sides_done"), S_("isides_done"), S_("masked_done"), S_("feat_done")
        part_done, rest_done, rows_done = S_("part_done"), S_("rest_done"), S_("rows_done")
        rows_turned, rowsT_done, v_done = S_("rows_turned"), S_("rowsT_done"), S_("v_done3")
        d_ready, i_ready, dist_done = S_("d_ready"), S_("i_ready"), S_("dist_done")
        u_done, prod_done = S_("u_done"), S_("prod_done")
        root_done, sum_done, ln_done, w_done, pv_done = S_("root_done"), S_("sum_done3"), S_("ln_done"), S_("w_done"), S_("pv_done3")
        o_copied, o_turned, rec_done, attn_done = S_("o_copied"), S_("o_turned"), S_("rec_done3"), S_("attn_done3")
        attn_turned, attnT_done, proj_ready = S_("attn_turned3"), S_("attnT_done3"), S_("proj_ready3")
        res_done = S_("res_done3")

        def on_scalar(h):
            return h in (0, 6) or 8 <= h < 14

        def two_heads(buffer, p):
            return buffer[:, 2 * p:2 * p + 2, :].rearrange("p h n -> p (h n)")

        def pe_turn_x(pe, b):
            pe.wait_ge(xh_done, (b + 1) * TB)
            after(pe, res_done, (b - 4) * TB)
            after(pe, qkv_copied, b * TB)
            for j in range(TB):
                last = nc.tensor.transpose(misc[:, j * P:(j + 1) * P], xh[:, j, :], keep.ident)
            last.then_inc(xh_turned, 1)

        def pe_qkv(pe, b, j):
            pe.wait_ge(xT_done, b + 1)
            after(pe, qkv_copied, b * TB + j)
            nc.tensor.matmul(misc[:, 0:3 * P], xTs[:, j * P:(j + 1) * P], keep.qkvoT[:, 0:3, :], start=True,
                             stop=True).then_inc(qkv_ready, 1)

        def pe_turn_rows(pe, b, i, g, side):
            pe.wait_ge(rows_done, b + 1)
            after(pe, rowsT_done, b * 2 * GROUPS + 2 * g + side)
            for q in range(GROUP):
                for j in range(TB):
                    last = nc.tensor.transpose(r_ps[0:RW, (q * TB + j) * P:(q * TB + j + 1) * P],
                                               rows[:, i, side, j * H + g * GROUP + q, :], keep.ident_bf[:, :])
            last.then_inc(rows_turned, 1)

        def pe_pairwise(pe, h, r0, n, ps):
            g, q = h // GROUP, h % GROUP
            for j in range(TB):
                last = nc.tensor.matmul(ps[:, j * N:(j + 1) * N],
                                        rowsT[r0:r0 + n, 1, g, q * N + j * P:q * N + (j + 1) * P],
                                        rowsT[r0:r0 + n, 0, g, q * N:(q + 1) * N], start=True, stop=True)
            return last

        def pe_distances(pe, b, h):
            pe.wait_ge(rowsT_done, b * 2 * GROUPS + 2 * (h // GROUP) + 2)
            after(pe, dist_done, b * H + h - 1)
            pe_pairwise(pe, h, 0, S * QD, d_ps[h % 2]).then_inc(d_ready, 1)

        def pe_inverses(pe, b, h):
            after(pe, u_done, b * H + h - 1)
            pe_pairwise(pe, h, IROW, 2 * S, i_ps[h % 2]).then_inc(i_ready, 1)

        def pe_values(pe, b, h, i):
            pe.wait_ge(w_done, b * HP + h // 2 + 1)
            if h == 0:
                pe.wait_ge(v_done, b + 1)
                after(pe, o_copied, b * 2)
            g, q = h // GROUP, h % GROUP
            out = o_ps[g // 2][q * ROWS:(q + 1) * ROWS, (g % 2) * N:(g % 2 + 1) * N]
            for j in range(TB):
                last = nc.tensor.matmul(out, v[:, i, j, h, :], w[:, i, h, j * N:(j + 1) * N],
                                        start=(j == 0), stop=(j == TB - 1))
            last.then_inc(pv_done, 1)

        def pe_turn_o(pe, b, j, users):
            pe.wait_ge(o_copied, (b + 1) * 2)
            after(pe, qkv_copied, users * TB)
            after(pe, attn_done, b * TB + j)
            for g in range(GROUPS):
                last = nc.tensor.transpose(misc[:, g * P:(g + 1) * P], o[:, g, j * P:(j + 1) * P], keep.ident)
            last.then_inc(o_turned, 1)

        def pe_turn_attn(pe, b):
            pe.wait_ge(attn_done, (b + 1) * TB)
            for j in range(TB):
                last = nc.tensor.transpose(misc[:, j * P:(j + 1) * P], attn[:, j, :], keep.ident)
            last.then_inc(attn_turned, 1)

        def pe_project(pe, b):
            pe.wait_ge(attnT_done, b + 1)
            for j in range(TB):
                last = nc.tensor.matmul(misc[:, N + j * P:N + (j + 1) * P], attnT[:, j * P:(j + 1) * P],
                                        keep.qkvoT[:, 3, :], start=True, stop=True)
            last.then_inc(proj_ready, 1)

        def act_xT(act, b):
            act.wait_ge(xh_turned, b + 1)
            after(act, qkv_ready, b * TB)
            nc.scalar.copy(xTs[:, :], misc[:, 0:N]).then_inc(xT_done, 1)

        def act_qkv(act, b, i, j):
            act.wait_ge(qkv_ready, b * TB + j + 1)
            after(act, part_done, b * PARTS)
            after(act, rest_done, b * (PARTS - 1))
            after(act, square_done, b)
            after(act, v_done, b - 1)
            by_head = lambda n: misc[:, n * P:(n + 1) * P].rearrange("p (h e) -> p h e", h=H)
            nc.scalar.activation(feat[:, 0, j * H:(j + 1) * H, 0:DH], by_head(0), ACT.Copy, scale=-2.0)
            nc.scalar.activation(feat[:, 1, j * H:(j + 1) * H, 0:DH], by_head(1), ACT.Copy, scale=2.0)
            nc.scalar.copy(vst[:, i, j, :], misc[:, 2 * P:3 * P]).then_inc(qkv_copied, 1)

        def rows_turn(b, h, one_after):
            if h % 2:
                return []
            if h < GROUP:
                return [(b, GROUPS - 1, h // 2)]
            return [(b + 1, h // GROUP - 1, h % GROUP // 2)] if one_after else []

        def rows_on_scalar(g, side):
            return g < GROUPS - 1

        def copy_rows(engine, b, g, side):
            engine.wait_ge(rows_turned, b * 2 * GROUPS + 2 * g + side + 1)
            after(engine, i_ready, (b - 1) * H + (g + 1) * GROUP)
            if engine is nc.scalar:
                ins = nc.scalar.copy(rowsT[:, side, g, :], r_ps[0:RW, :])
            else:
                ins = nc.vector.tensor_copy(rowsT[:, side, g, :], r_ps[0:RW, :])
            ins.then_inc(rowsT_done, 1)

        def take_distances(engine, b, h):
            k, i, slot = b * H + h, h % 2, h % (AHEAD + 2)
            engine.wait_ge(d_ready, k + 1)
            after(engine, dist_done, k)
            after(engine, u_done, k - 1 - AHEAD)
            if on_scalar(h):
                ins = nc.scalar.activation(dist[:, slot, :], d_ps[i][:, :], ACT.Relu)
            else:
                ins = nc.vector.tensor_scalar(dist[:, slot, :], d_ps[i][:, :], 0.0, None, ALU.max)
            ins.then_inc(dist_done, 1)

        def act_root(act, b, p, i):
            act.wait_ge(prod_done, b * HP + p + 1)
            nc.scalar.activation(two_heads(w[:, i], p), two_heads(w[:, i], p), ACT.Sqrt).then_inc(root_done, 1)

        def act_ln(act, b, p, i):
            act.wait_ge(sum_done, b * HP + p + 1)
            nc.scalar.activation(two_heads(w[:, i], p), two_heads(w[:, i], p), ACT.Ln, bias=1.0).then_inc(ln_done, 1)

        def act_exp(act, b, p, i):
            act.wait_ge(ln_done, b * HP + p + 1)
            nc.scalar.activation(two_heads(w[:, i], p), two_heads(w[:, i], p), ACT.Exp, scale=-1.0).then_inc(w_done, 1)

        def act_attnT(act, b):
            act.wait_ge(attn_turned, b + 1)
            after(act, proj_ready, b)
            nc.scalar.copy(attnT[:, :], misc[:, 0:N]).then_inc(attnT_done, 1)

        def pool_sum(pool, b, p, i):
            pool.wait_ge(root_done, b * HP + p + 1)
            nc.gpsimd.tensor_tensor(two_heads(w[:, i], p), two_heads(u, p), two_heads(w[:, i], p), ALU.add
                                    ).then_inc(sum_done, 1)

        def pool_square(pool, b):
            pool.wait_ge(qkv_copied, (b + 1) * TB)
            after(pool, part_done, b * PARTS)
            qk = feat[:, :, :, 0:DH].rearrange("p s j e -> p (s j) e")
            nc.gpsimd.tensor_tensor(square.rearrange("p s j e -> p (s j) e"), qk, qk, ALU.mult
                                    ).then_inc(square_done, 1)

        def pool_rests(pool, b):
            for n in range(PARTS - 1):
                left = rest if n else feat
                pool.wait_ge(part_done, b * PARTS + n + 1)
                nc.gpsimd.tensor_tensor(rest[:, :, :, :], left[:, :, :, :], part[n][:, :, :, :], ALU.subtract
                                        ).then_inc(rest_done, 1)

        def pool_rows(pool, b, i):
            pool.wait_ge(part_done, (b + 1) * PARTS)
            after(pool, rows_turned, (b - 1) * 2 * GROUPS)
            first = True
            for side in range(2):
                for n in reversed(range(PARTS)):
                    at = [s for s, pair in enumerate(PAIRINGS) if pair[side] == n]
                    step = at[1] - at[0] if len(at) > 1 else 1
                    for r0, width, f0 in ((IROW, 2, QD), (0, QD, 0)):
                        dst = rows[:, i, side, :, r0:r0 + S * width].rearrange("p j (s f) -> p j s f", s=S)
                        dst = dst[:, :, at[0]:at[-1] + 1:step, :]
                        src = part[n][:, side, :, f0:f0 + width].unsqueeze(2).to_broadcast([P, JH, len(at), width])
                        if first:
                            ones = one[:, :].unsqueeze(2).unsqueeze(3).to_broadcast([P, JH, len(at), width])
                            ins = nc.gpsimd.tensor_tensor(dst, src, ones, ALU.mult)
                        else:
                            ins = nc.gpsimd.tensor_scalar(dst, src, 1.0, 0.0, ALU.mult, ALU.add)
                        first = False
            ins.then_inc(rows_done, 1)

        def dve_norm(dve, b):
            after(dve, xh_turned, b)
            after(dve, attn_turned, b - 4)
            for j in range(TB):
                t = b * TB + j
                nc.vector.tensor_scalar(xh[:, j, :], keep.x[:, t, :], keep.mv[:, t, 0:1], keep.rstd_col(t),
                                        ALU.subtract, ALU.mult).then_inc(xh_done, 1)

        def dve_features(dve, b):
            vec = nc.vector
            dve.wait_ge(square_done, b + 1)
            vec.tensor_reduce(norm2[:, :, :].rearrange("p s j -> p (s j)"),
                              square.rearrange("p s j e -> p (s j) e"), AX_X,
                              ALU.add).then_inc(norm2_done, 1)
            dve.wait_ge(norm2_done, b + 1)
            vec.tensor_scalar(gap[:, :, :], norm2[:, :, :], -0.25, 1.0, ALU.mult, ALU.add).then_inc(gap_done, 1)
            vec.tensor_copy(feat[:, 0, :, DH], norm2[:, 0, :])
            vec.tensor_copy(feat[:, 1, :, DH + 1], norm2[:, 1, :])
            dve.wait_ge(gap_done, b + 1)
            vec.tensor_scalar(sides[:, 0], gap[:, :, :], TINY, None, ALU.max)
            vec.tensor_scalar(sides[:, 1], gap[:, :, :], -1.0, TINY, ALU.mult, ALU.max).then_inc(sides_done, 1)
            vec.tensor_scalar(signs[:, 0], gap[:, :, :], 0.0, None, ALU.is_ge)
            vec.tensor_scalar(signs[:, 1], gap[:, :, :], 0.0, None, ALU.is_lt).then_inc(sides_done, 1)
            dve.wait_ge(sides_done, 2 * (b + 1))
            vec.reciprocal(isides[:, :, :, :], sides[:, :, :, :]).then_inc(isides_done, 1)

        def dve_features_end(dve, b):
            vec = nc.vector
            dve.wait_ge(isides_done, b + 1)
            vec.tensor_tensor(isides[:, :, :, :], isides[:, :, :, :], signs[:, :, :, :],
                              ALU.mult).then_inc(masked_done, 1)
            dve.wait_ge(masked_done, b + 1)
            for a in range(2):
                vec.tensor_copy(feat[:, 0, :, QD + a], isides[:, a, 0, :])
                ins = vec.scalar_tensor_tensor(out=feat[:, 1, :, QD + a], in0=signs[:, 1 - a, 1, :], scalar=BIG,
                                               in1=isides[:, a, 1, :], op0=ALU.mult, op1=ALU.add)
            ins.then_inc(feat_done, 1)

        def dve_split(dve, b, n):
            if n == 0:
                dve.wait_ge(feat_done, b + 1)
                after(dve, rows_done, b)
                left = feat
            else:
                left = rest
                dve.wait_ge(rest_done, b * (PARTS - 1) + n)
            nc.vector.tensor_copy(part[n][:, :, :, :], left[:, :, :, :]).then_inc(part_done, 1)

        def dve_values(dve, b, i):
            dve.wait_ge(qkv_copied, (b + 1) * TB)
            after(dve, pv_done, (b - 1) * H)
            for j in range(TB):
                ins = nc.vector.tensor_copy(v[:, i, j, :, 0:DH], vst[:, i, j, :].rearrange("p (h e) -> p h e", h=H))
            ins.then_inc(v_done, 1)

        def dve_ratio(dve, b, h):
            k, q = b * H + h, h % 2
            dve.wait_ge(dist_done, k + 1)
            dve.wait_ge(i_ready, k + 1)
            after(dve, sum_done, (b - 1) * HP + h // 2 + 1)
            nc.vector.scalar_tensor_tensor(out=u[:, h, :], in0=i_ps[q][:, :], scalar=1.0 / DEN_MIN,
                                           in1=dist[:, h % (AHEAD + 2), :], op0=ALU.min, op1=ALU.mult).then_inc(u_done, 1)

        def dve_product(dve, b, p, i):
            dve.wait_ge(u_done, b * H + 2 * p + 2)
            after(dve, pv_done, (b - 2) * H + 2 * p + 2)
            nc.vector.scalar_tensor_tensor(out=two_heads(w[:, i], p), in0=two_heads(u, p), scalar=2.0,
                                           in1=two_heads(u, p), op0=ALU.add, op1=ALU.mult).then_inc(prod_done, 1)

        def dve_copy_o(dve, b):
            dve.wait_ge(pv_done, (b + 1) * H)
            after(dve, o_turned, b * TB)
            for n in range(2):
                nc.vector.tensor_copy(o[:, 2 * n:2 * n + 2, :], o_ps[n][:, :].rearrange("p (g n) -> p g n", g=2)
                                      ).then_inc(o_copied, 1)

        def dve_reciprocals(dve, b, j):
            dve.wait_ge(o_turned, b * TB + j + 1)
            nc.vector.reciprocal(rec[:, j, :], misc[:, :].rearrange("p (h r) -> p h r", h=H)[:, :, DH]
                                 ).then_inc(rec_done, 1)

        def dve_normalise(dve, b, j, users):
            dve.wait_ge(rec_done, b * TB + j + 1)
            dve.wait_ge(xh_turned, users)
            after(dve, attn_turned, b)
            ov = misc[:, :].rearrange("p (h r) -> p h r", h=H)
            nc.vector.tensor_tensor(attn[:, j, :].rearrange("p (h e) -> p h e", h=H), ov[:, :, 0:DH],
                                    rec[:, j, :].unsqueeze(2).to_broadcast([P, H, DH]), ALU.mult
                                    ).then_inc(attn_done, 1)

        def dve_residual(dve, b):
            dve.wait_ge(proj_ready, b + 1)
            for j in range(TB):
                t = b * TB + j
                nc.vector.tensor_tensor(keep.x[:, t, :], misc[:, N + j * P:N + (j + 1) * P], keep.x[:, t, :],
                                        ALU.add).then_inc(res_done, 1)

        def dve_stats(dve, b):
            for j in range(TB):
                nc.vector.bn_stats(keep.stats[:, b * TB + j, :], keep.x[:, b * TB + j, :])

        def ahead(b, h, one_after):
            if h + AHEAD < H:
                return [(b, h + AHEAD)]
            return [(b + 1, h + AHEAD - H)] if one_after else []

        def over_batches(engine, body):
            def turn(p, first, last):
                for i in range(2):
                    b = 2 * p + i
                    body(b, i, not (first and i == 0), not first, not (last and i == 1), not last)
            turn(0, True, pairs == 1)
            if pairs > 2:
                turn(1, False, False)
            if pairs > 3:
                with engine.Fori(2, pairs - 1) as p:
                    turn(p, False, False)
            if pairs > 1:
                turn(pairs - 1, False, True)

        END = batches - 1

        with nc.Block() as block:
            @block.tensor
            def _(pe):
                pe.wait_ge(zeroed, 5)
                for b in range(2):
                    pe_turn_x(pe, b)
                    for j in range(TB):
                        pe_qkv(pe, b, j)
                for g in range(GROUPS - 1):
                    for side in range(2):
                        pe_turn_rows(pe, 0, 0, g, side)
                for h in range(AHEAD):
                    pe_distances(pe, 0, h)

                def body(b, i, one_before, two_before, one_after, two_after):
                    for h in range(H):
                        pe_inverses(pe, b, h)
                        for a in ahead(b, h, one_after):
                            pe_distances(pe, *a)
                        for r in rows_turn(b, h, one_after):
                            pe_turn_rows(pe, r[0], i if h < GROUP else 1 - i, r[1], r[2])
                        if two_after:
                            if h == MAKE_AT:
                                pe_turn_x(pe, b + 2)
                            if h in (MAKE_AT + 2, MAKE_AT + 4):
                                pe_qkv(pe, b + 2, (h - MAKE_AT) // 2 - 1)
                        if two_before:
                            if h in (FINISH_AT, FINISH_AT + 2):
                                pe_turn_o(pe, b - 2, (h - FINISH_AT) // 2, b + 3 if two_after else batches)
                            if h == FINISH_AT + 4:
                                pe_turn_attn(pe, b - 2)
                            if h == FINISH_AT + 6:
                                pe_project(pe, b - 2)
                        if one_before and h >= LAG:
                            pe_values(pe, b - 1, h - LAG, 1 - i)
                    if one_before:
                        for h in range(H - LAG, H):
                            pe_values(pe, b - 1, h, 1 - i)
                over_batches(pe, body)

                def finish(b):
                    after(pe, res_done, b * TB)
                    for j in range(TB):
                        pe_turn_o(pe, b, j, batches)
                    pe_turn_attn(pe, b)
                    pe_project(pe, b)
                finish(END - 1)
                for h in range(H):
                    pe_values(pe, END, h, 1)
                finish(END)

            @block.scalar
            def _(act):
                nc.scalar.preload_act_table_set("natural_log_exp_and_others")
                for b in range(2):
                    act_xT(act, b)
                    for j in range(TB):
                        act_qkv(act, b, b, j)
                for g in range(GROUPS - 1):
                    for side in range(2):
                        copy_rows(act, 0, g, side)
                for h in range(AHEAD):
                    if on_scalar(h):
                        take_distances(act, 0, h)

                def body(b, i, one_before, two_before, one_after, two_after):
                    nc.scalar.preload_act_table_set("natural_log_exp_and_others")
                    for h in range(H):
                        if h % 2 == 1:
                            for r in rows_turn(b, h - 1, one_after):
                                if rows_on_scalar(r[1], r[2]):
                                    copy_rows(act, *r)
                        for a in ahead(b, h, one_after):
                            if on_scalar(a[1]):
                                take_distances(act, *a)
                        if two_after:
                            if h == MAKE_AT + 1:
                                act_xT(act, b + 2)
                            if h in (MAKE_AT + 3, MAKE_AT + 5):
                                act_qkv(act, b + 2, i, (h - MAKE_AT - 3) // 2)
                        if two_before and h == FINISH_AT + 5:
                            act_attnT(act, b - 2)
                        if one_before:
                            if h % 2 == 1:
                                act_ln(act, b - 1, h // 2, 1 - i)
                            elif h > 0:
                                act_exp(act, b - 1, h // 2 - 1, 1 - i)
                    if one_before:
                        act_exp(act, b - 1, HP - 1, 1 - i)
                    for p in range(HP):
                        act_root(act, b, p, i)
                over_batches(act, body)
                nc.scalar.preload_act_table_set("natural_log_exp_and_others")
                act_attnT(act, END - 1)
                for p in range(HP):
                    act_ln(act, END, p, 1)
                    act_exp(act, END, p, 1)
                act_attnT(act, END)

            @block.gpsimd
            def _(pool):
                nc.gpsimd.memset(rows[:, :, :, :, :], 0.0).then_inc(zeroed, 1)
                nc.gpsimd.memset(one[:, :], 1.0).then_inc(zeroed, 1)
                nc.gpsimd.memset(v[:, :, :, :, DH:ROWS], 0.0).then_inc(v_cleared, 1)
                pool.wait_ge(v_cleared, 1)
                nc.gpsimd.memset(v[:, :, :, :, DH:VW], 1.0).then_inc(zeroed, 1)
                nc.gpsimd.memset(feat[:, 0, :, DH + 1:QD], 0.5).then_inc(zeroed, 1)
                nc.gpsimd.memset(feat[:, 1, :, DH:DH + 1], 0.5).then_inc(zeroed, 1)
                pool.wait_ge(zeroed, 5)
                for b in range(2):
                    pool_square(pool, b)
                    pool_rests(pool, b)
                    pool_rows(pool, b, b)

                def body(b, i, one_before, two_before, one_after, two_after):
                    for p in range(HP):
                        if two_after and p == SQUARE_AT:
                            pool_square(pool, b + 2)
                        if one_before:
                            pool_sum(pool, b - 1, p, 1 - i)
                    if two_after:
                        pool_rests(pool, b + 2)
                        pool_rows(pool, b + 2, i)
                over_batches(pool, body)
                for p in range(HP):
                    pool_sum(pool, END, p, 1)

            @block.vector
            def _(dve):
                dve.wait_ge(zeroed, 5)

                dve_norm(dve, 0)
                for b in range(2):
                    dve_features(dve, b)
                    dve_features_end(dve, b)
                    for n in range(PARTS):
                        dve_split(dve, b, n)
                    if b == 0:
                        dve_norm(dve, 1)
                for h in range(AHEAD):
                    if not on_scalar(h):
                        take_distances(dve, 0, h)

                def body(b, i, one_before, two_before, one_after, two_after):
                    if two_after:
                        dve_norm(dve, b + 2)
                    dve_values(dve, b, i)
                    if two_before:
                        dve_copy_o(dve, b - 2)
                    for h in range(H):
                        for a in ahead(b, h, one_after):
                            if not on_scalar(a[1]):
                                take_distances(dve, *a)
                        dve_ratio(dve, b, h)
                        if h >= 2 and h % 2 == 0:
                            dve_product(dve, b, h // 2 - 1, i)
                        if h % 2 == 1:
                            for r in rows_turn(b, h - 1, one_after):
                                if not rows_on_scalar(r[1], r[2]):
                                    copy_rows(dve, *r)
                        if two_before:
                            if h in (FINISH_AT + 1, FINISH_AT + 3):
                                dve_reciprocals(dve, b - 2, (h - FINISH_AT) // 2)
                                dve_normalise(dve, b - 2, (h - FINISH_AT) // 2, b + 3 if two_after else batches)
                            if h == FINISH_AT + 7:
                                dve_residual(dve, b - 2)
                        if two_after:
                            if h == FEATURES_AT:
                                dve_features(dve, b + 2)
                            if h == FEATURES_AT + 1:
                                dve_features_end(dve, b + 2)
                            if h in SPLITS_AT:
                                dve_split(dve, b + 2, SPLITS_AT.index(h))
                    if two_before:
                        dve.wait_ge(res_done, (b - 1) * TB)
                    dve_product(dve, b, HP - 1, i)
                    if two_before:
                        dve_stats(dve, b - 2)
                over_batches(dve, body)
                for b in (END - 1, END):
                    dve_copy_o(dve, b)
                    for j in range(TB):
                        dve_reciprocals(dve, b, j)
                        dve_normalise(dve, b, j, batches)
                    dve_residual(dve, b)
                dve.wait_ge(res_done, batches * TB)
                dve_stats(dve, END - 1)
                dve_stats(dve, END)


def mlp(nc, io, keep, y_dram, tiles):
    pairs = tiles // (2 * TC)
    chunks = 2 * pairs
    with ExitStack() as stack:
        m = Names(nc, stack)
        xh = m.sb("xh4", [P, 2, TC, P])
        xTs = m.sb("xTs4", [P, 2, CHUNK])
        hidden = m.sb("hidden", [P, 2, WB, CHUNK])
        y = m.sb("y_rows", [P, 2, TC, P])
        w1 = m.sb("w1", [P, WIDTH])
        w2 = m.sb("w2", [P, WB, P])
        x_ps = m.ps("x_ps4", [P, 512])
        h_ps = [m.ps(f"h_ps{i}", [P, 512]) for i in range(4)]
        y_ps = [m.ps(f"y_ps4{i}", [P, 512]) for i in range(2)]

        xh_done, xh_turned, xT_done = m.sem("xh_done4"), m.sem("xh_turned4"), m.sem("xT_done4")
        h_ready, relu_done = m.sem("h_ready"), m.sem("relu_done")
        y_ready, bias_added, y_done = m.sem("y_ready"), m.sem("bias_added"), m.sem("y_done")
        weights_in = m.sem("weights_in4")
        stored = [m.sem(f"y_stored{i}") for i in range(2)]

        with nc.Block() as block:
            @block.tensor
            def _(pe):
                def turn(c, i):
                    pe.wait_ge(xh_done, (c + 1) * TC)
                    after(pe, xT_done, c)
                    for t in range(TC):
                        last = nc.tensor.transpose(x_ps[:, t * P:(t + 1) * P], xh[:, i, t, :], keep.ident)
                    last.then_inc(xh_turned, 1)

                def up(c, i, first):
                    pe.wait_ge(xT_done, c + 1)
                    for w in range(WB):
                        if not (first and i == 0):
                            pe.wait_ge(relu_done, (c - 1) * WB + w + 1)
                        nc.tensor.matmul(h_ps[w][:, :], w1[:, w * P:(w + 1) * P], xTs[:, i, :], start=True,
                                         stop=True).then_inc(h_ready, 1)

                def down(c, i):
                    after(pe, y_done, c - 1)
                    for w in range(WB):
                        pe.wait_ge(relu_done, c * WB + w + 1)
                        for t in range(TC):
                            last = nc.tensor.matmul(y_ps[i][:, t * P:(t + 1) * P], hidden[:, i, w, t * P:(t + 1) * P],
                                                    w2[:, w, :], start=(w == 0 and t == 0),
                                                    stop=(w == WB - 1), skip_group_check=True)
                    last.then_inc(y_ready, 1)

                pe.wait_ge(weights_in, 32)

                def body(p, first):
                    for i in range(2):
                        c = 2 * p + i
                        turn(c, i)
                        if not (first and i == 0):
                            down(c - 1, 1 - i)
                        up(c, i, first)
                over_pairs(pe, pairs, body)
                down(chunks - 1, 1)

            @block.scalar
            def _(act):
                def body(p, first):
                    for i in range(2):
                        c = 2 * p + i
                        act.wait_ge(xh_turned, c + 1)
                        if not first:
                            act.wait_ge(h_ready, (c - 1) * WB)
                        nc.scalar.copy(xTs[:, i, :], x_ps[:, :]).then_inc(xT_done, 1)
                        for w in range(WB):
                            act.wait_ge(h_ready, c * WB + w + 1)
                            if not first:
                                act.wait_ge(y_ready, c - 1)
                            nc.scalar.activation(hidden[:, i, w, :], h_ps[w][:, :], ACT.Relu,
                                                 bias=keep.b1T[:, w:w + 1]).then_inc(relu_done, 1)
                over_pairs(act, pairs, body)

            @block.vector
            def _(dve):
                b2 = keep.biases[:, R_B2:R_B2 + P].unsqueeze(1).to_broadcast([P, TC, P])

                def norm(c, i):
                    after(dve, xh_turned, c - 1)
                    for t in range(TC):
                        n = c * TC + t
                        nc.vector.tensor_scalar(xh[:, i, t, :], keep.x[:, n, :], keep.mv[:, n, 0:1],
                                                keep.rstd_col(n), ALU.subtract, ALU.mult).then_inc(xh_done, 1)

                def finish(p, i, first):
                    c = 2 * p + i
                    if not first and not (isinstance(p, int) and p == 0):
                        dve.wait_ge(stored[i], 16 * p)
                    nc.vector.tensor_tensor(y[:, i, :, :], keep.x[:, bass.ds(c * TC, TC), :], b2,
                                            ALU.add).then_inc(bias_added, 1)
                    dve.wait_ge(bias_added, c + 1)
                    dve.wait_ge(y_ready, c + 1)
                    nc.vector.tensor_tensor(y[:, i, :, :], y_ps[i][:, :].rearrange("p (t d) -> p t d", t=TC),
                                            y[:, i, :, :], ALU.add).then_inc(y_done, 1)

                def body(p, first):
                    norm(2 * p, 0)
                    if not first:
                        finish(p - 1, 1, False)
                    norm(2 * p + 1, 1)
                    finish(p, 0, first)
                over_pairs(dve, pairs, body)
                finish(pairs - 1, 1, pairs == 1)

            @block.sync
            def _(sp):
                sp.dma_start(w1[:, :], io["L1_ffn_w1"]).then_inc(weights_in, 16)
                sp.dma_start(w2[:, :, :], io["L1_ffn_w2"].rearrange("(w p) d -> p w d", p=P)).then_inc(weights_in, 16)
                dram = y_dram.rearrange("b (j p) d -> p (b j) d", p=P)

                def body(p, first):
                    for i in range(2):
                        c = 2 * p + i
                        sp.wait_ge(y_done, c + 1)
                        sp.dma_start(dram[:, bass.ds(c * TC, TC), :], y[:, i, :, :]).then_inc(stored[i], 16)
                over_pairs(sp, pairs, body)
                for i in range(2):
                    sp.wait_ge(stored[i], 16 * pairs)


class Kept:

    def __init__(self, m, tiles):
        self.x = m.sb("x", [P, tiles, P])
        self.mv = m.sb("mv", [P, tiles, 2])
        self.rstd = m.sb("rstd", [P, tiles])
        self.stats = m.sb("stats", [P, tiles, 6])
        self.ident_f = m.sb("ident", [P, P])
        self.ident = self.ident_f[:, :]
        self.ident_bf = m.sb("ident_bf", [P, P], BF16)
        self.biases = m.sb("biases", [P, R_WIDTH])
        self.qkvoT = m.sb("qkvoT", [P, 4, P])
        self.b1T = m.sb("b1T", [P, WB])

    def first_block(self, m):
        self.mask_bf = m.sb("mask_bf", [P, P], BF16)
        self.sel_bf = m.sb("sel_bf", [PARTS * E, PAIRS * P], BF16)
        self.fold_hi = m.sb("fold_hi", [P, H, P], F32R)
        self.fold_lo = m.sb("fold_lo", [P, H, P], F32R)
        self.fold_bias = m.sb("fold_bias", [P, H])
        self.wv0 = m.sb("wv0", [P, H, DH])
        self.wp = m.sb("wp", [P, P])
        self.v0 = m.sb("v0", [P, 2, TB, H, VS], BF16)
        self.gateT = tuple(m.sb(f"gateT_{part}", [P, BLOCKS, P], F32R) for part in ("hi", "lo"))
        self.upT = tuple(m.sb(f"upT_{part}", [P, BLOCKS, P], F32R) for part in ("hi", "lo"))
        self.downT = m.sb("downT", [P, BLOCKS, P])
        self.routerT = m.sb("routerT", [P, E])

    def rstd_col(self, t):
        return self.rstd[:, bass.ds(t, 1)] if not isinstance(t, int) else self.rstd[:, t:t + 1]


class Wide:

    def __init__(self, m, tiles):
        self.xT = m.sb("xT_all", [P, tiles // TC + 1, CHUNK])
        self.weight = m.sb("weight", [P, tiles + TC, PARTS * E], BF16)


def two_blocks(nc, io, out, batches):
    tiles = batches * TB
    with ExitStack() as stack:
        keep = Kept(Names(nc, stack), tiles)
        with ExitStack() as first:
            keep.first_block(Names(nc, first))
            load_and_fold(nc, io, keep, tiles)
            rstd_of_all(nc, keep, tiles, "attn")
            causal_attention(nc, keep, batches)
            wide = Wide(Names(nc, first), tiles)
            rstd_of_all(nc, keep, tiles, "moe")
            route(nc, keep, wide, tiles)
            experts(nc, keep, wide, tiles)
        rstd_of_all(nc, keep, tiles, "hyp")
        hyperbolic_attention(nc, keep, batches)
        rstd_of_all(nc, keep, tiles, "mlp")
        mlp(nc, io, keep, out, tiles)


def constants():
    import numpy as np

    c = np.zeros((P, C_WIDTH), np.float32)
    c[:, C_IDENT:C_IDENT + P] = np.eye(P)
    c[:, C_MASK:C_MASK + P] = np.triu(np.full((P, P), -3e38), 1)
    for part in range(PARTS):
        for e in range(E):
            c[part * E + e, C_SEL + e * INTER:C_SEL + (e + 1) * INTER] = 1
    return c


_INPUTS = (
    "L0_attn_x", "L0_attn_Wkqv", "L0_attn_bkqv", "L0_attn_Wp", "L0_attn_bp", "L0_ffn_gate_w", "L0_ffn_e_bias",
    "L0_ffn_gate_proj", "L0_ffn_up_proj", "L0_ffn_down_proj", "L0_ffn_shared_gate_w", "L0_ffn_shared_up_w",
    "L0_ffn_shared_down_w", "L1_attn_wq", "L1_attn_wk", "L1_attn_wv", "L1_attn_wo", "L1_ffn_w1", "L1_ffn_b1",
    "L1_ffn_w2", "L1_ffn_b2",
)


def kernel(**inputs):
    import numpy as np
    import concourse.bacc as bacc
    from concourse.bass_utils import run_bass_kernel_spmd

    nc = bacc.Bacc("TRN2", target_bir_lowering=False, num_devices=1)
    arrays = {name: np.ascontiguousarray(inputs[name]) for name in _INPUTS}
    arrays["consts"] = constants()
    io = {name: nc.dram_tensor(name, a.shape, mybir.dt.from_np(a.dtype), kind="ExternalInput").ap()
          for name, a in arrays.items()}
    shape = arrays["L0_attn_x"].shape
    y = nc.dram_tensor("y", shape, F32, kind="ExternalOutput").ap()
    two_blocks(nc, io, y, shape[0])
    r = run_bass_kernel_spmd(nc, [arrays], core_ids=[0])
    return r.results[0]["y"]
```
